# Optimizing a Trainium2 kernel written in Bass

```python
import numpy as np
import jax
import jax.numpy as jnp

def _softmax(x, axis=-1):
    return jax.nn.softmax(x, axis=axis)

def _gelu(x):
    return jax.nn.gelu(x, approximate=True)

def _silu(x):
    return jax.nn.silu(x)

def _sigmoid(x):
    return jax.nn.sigmoid(x)

def _layernorm(x, axis=-1, eps=1e-05):
    m = jnp.mean(x, axis=axis, keepdims=True)
    v = jnp.var(x, axis=axis, keepdims=True)
    return (x - m) / jnp.sqrt(v + eps)

def _scatter_add(tgt, idx, src, axis=0):
    return tgt.at[idx].add(src)

def _segment_sum(src, seg, n):
    return jax.ops.segment_sum(src, seg, n)
kernel_name = 'mk_gnn_ffn_d2_gnn_r8_c7532f'

def setup_inputs(seed: int=0):
    np.random.seed(seed)
    _w = jnp.asarray

    def _rec_inputs():
        import jax
        import jax.numpy as jnp
        _gk = jax.random.key(seed)
        x = -7.329e-05 + 0.9999 * jax.random.normal(jax.random.fold_in(_gk, 1), (6250, 512), jnp.float32)
        _s = jax.random.randint(jax.random.fold_in(_gk, 2), (50000,), 0, 6250, jnp.int32)
        _d = jax.random.randint(jax.random.fold_in(_gk, 3), (50000,), 0, 6250, jnp.int32)
        _loop = jnp.arange(6250, dtype=jnp.int32)
        src = jnp.concatenate([_s, _d, _loop])
        dst = jnp.concatenate([_d, _s, _loop])
        _o = jnp.argsort(dst, stable=True)
        src = src[_o]
        dst = dst[_o]
        edge_weight = jax.random.uniform(jax.random.fold_in(_gk, 13), (106250,), jnp.float32, 0.0, 0.999999)
        return (x, src, dst, edge_weight)
    x, src, dst, edge_weight = _rec_inputs()

    def _L0_gnn_setup():
        import jax, jax.numpy as jnp
        import numpy as np
        N = 12500
        E = 100000
        D_IN = 512
        D_OUT = 512
        EPS = 1e-05
        key = jax.random.key(seed)
        k = jax.random.split(key, 7)
        x = jax.random.normal(k[0], (N, D_IN), dtype=jnp.float32)
        edge_index = jax.random.randint(k[1], (2, E), 0, N, dtype=jnp.int64)
        W_l = jax.random.normal(k[2], (D_OUT, D_IN), dtype=jnp.float32) * 0.02
        b_l = jnp.zeros((D_OUT,), dtype=jnp.float32)
        W_r = jax.random.normal(k[3], (D_OUT, D_IN), dtype=jnp.float32) * 0.02
        gamma = jnp.ones((D_OUT,), dtype=jnp.float32)
        beta = jnp.zeros((D_OUT,), dtype=jnp.float32)
        return {'x': x, 'edge_index': edge_index, 'W_l': W_l, 'b_l': b_l, 'W_r': W_r, 'gamma': gamma, 'beta': beta}
    _L0_gnn_all = _L0_gnn_setup()
    _L0_gnn_in = {k: v for k, v in _L0_gnn_all.items() if k in ('W_l', 'b_l', 'W_r', 'gamma', 'beta')}
    del _L0_gnn_all

    def _L0_ffn_setup():
        import jax, jax.numpy as jnp
        import numpy as np
        D_MODEL = 512
        D_FF = 256
        N_EXPERTS = 8
        TOP_K = 2
        key = jax.random.key(seed)
        ks = jax.random.split(key, 7)
        x = jax.random.normal(ks[0], (8, 512, D_MODEL), dtype=jnp.float32)
        router_w = jax.random.normal(ks[1], (D_MODEL, N_EXPERTS), dtype=jnp.float32) * 0.02
        router_b = jnp.zeros((N_EXPERTS,), dtype=jnp.float32)
        s1 = 1.0 / np.sqrt(D_MODEL)
        s2 = 1.0 / np.sqrt(D_FF)
        w1 = jax.random.uniform(ks[2], (N_EXPERTS, D_MODEL, D_FF), jnp.float32, -s1, s1)
        b1 = jax.random.uniform(ks[3], (N_EXPERTS, D_FF), jnp.float32, -s1, s1)
        w2 = jax.random.uniform(ks[4], (N_EXPERTS, D_FF, D_MODEL), jnp.float32, -s2, s2)
        b2 = jax.random.uniform(ks[5], (N_EXPERTS, D_MODEL), jnp.float32, -s2, s2)
        return {'x': x, 'router_w': router_w, 'router_b': router_b, 'w1': w1, 'b1': b1, 'w2': w2, 'b2': b2}
    _L0_ffn_all = _L0_ffn_setup()
    _L0_ffn_in = {k: v for k, v in _L0_ffn_all.items() if k in ('router_w', 'router_b', 'w1', 'b1', 'w2', 'b2')}
    del _L0_ffn_all

    def _L1_gnn_setup():
        import jax, jax.numpy as jnp
        import numpy as np
        N_NODES = 12500
        N_EDGES = 200000
        D_IN = 512
        D_OUT = 512
        key = jax.random.key(seed)
        k1, k2, k3, k4, k5 = jax.random.split(key, 5)
        h = jax.random.normal(k1, (N_NODES, D_IN), dtype=jnp.float32)
        weight = jax.random.normal(k2, (D_IN, D_OUT), dtype=jnp.float32) * (1.0 / np.sqrt(D_IN))
        edge_weight = jax.random.uniform(k3, (N_EDGES,), dtype=jnp.float32)
        src = jax.random.randint(k4, (N_EDGES,), 0, N_NODES, dtype=jnp.int64)
        dst = jax.random.randint(k5, (N_EDGES,), 0, N_NODES, dtype=jnp.int64)
        return {'h': h, 'weight': weight, 'edge_weight': edge_weight, 'src': src, 'dst': dst}
    _L1_gnn_all = _L1_gnn_setup()
    _L1_gnn_in = {k: v for k, v in _L1_gnn_all.items() if k in ('weight',)}
    del _L1_gnn_all

    def _L1_ffn_setup():
        import jax, jax.numpy as jnp
        import numpy as np
        DIM = 512
        FFN_DIM = 1408
        GROUP = 128
        EPS = 1e-05

        def _quantize_weight(w, group_size):
            o, i = w.shape
            wg = w.reshape(o, i // group_size, group_size)
            scale = jnp.mean(jnp.abs(wg), axis=-1, keepdims=True) + EPS
            wq = jnp.clip(jnp.round(wg / scale), -1.0, 1.0) * scale
            return wq.reshape(o, i)

        def _bitlinear(x, w, group_size=GROUP):
            wq = w + jax.lax.stop_gradient(_quantize_weight(w, group_size) - w)
            return jnp.einsum('bsd,fd->bsf', x, wq)
        key = jax.random.key(seed)
        k_x, k_g, k_u, k_d = jax.random.split(key, 4)
        x = jax.random.normal(k_x, (8, 512, DIM), dtype=jnp.float32)
        sd_in = 1.0 / np.sqrt(DIM)
        sd_ffn = 1.0 / np.sqrt(FFN_DIM)
        w_gate = jax.random.normal(k_g, (FFN_DIM, DIM), dtype=jnp.float32) * sd_in
        w_up = jax.random.normal(k_u, (FFN_DIM, DIM), dtype=jnp.float32) * sd_in
        w_down = jax.random.normal(k_d, (DIM, FFN_DIM), dtype=jnp.float32) * sd_ffn
        return {'x': x, 'w_gate': w_gate, 'w_up': w_up, 'w_down': w_down}
    _L1_ffn_all = _L1_ffn_setup()
    _L1_ffn_in = {k: v for k, v in _L1_ffn_all.items() if k in ('w_gate', 'w_up', 'w_down')}
    del _L1_ffn_all
    return {'x': x, 'src': src, 'dst': dst, 'edge_weight': edge_weight, 'L0_gnn_W_l': _L0_gnn_in['W_l'], 'L0_gnn_b_l': _L0_gnn_in['b_l'], 'L0_gnn_W_r': _L0_gnn_in['W_r'], 'L0_gnn_gamma': _L0_gnn_in['gamma'], 'L0_gnn_beta': _L0_gnn_in['beta'], 'L0_ffn_router_w': _L0_ffn_in['router_w'], 'L0_ffn_router_b': _L0_ffn_in['router_b'], 'L0_ffn_w1': _L0_ffn_in['w1'], 'L0_ffn_b1': _L0_ffn_in['b1'], 'L0_ffn_w2': _L0_ffn_in['w2'], 'L0_ffn_b2': _L0_ffn_in['b2'], 'L1_gnn_weight': _L1_gnn_in['weight'], 'L1_ffn_w_gate': _L1_ffn_in['w_gate'], 'L1_ffn_w_up': _L1_ffn_in['w_up'], 'L1_ffn_w_down': _L1_ffn_in['w_down']}

def reference(x, src, dst, edge_weight, L0_gnn_W_l, L0_gnn_b_l, L0_gnn_W_r, L0_gnn_gamma, L0_gnn_beta, L0_ffn_router_w, L0_ffn_router_b, L0_ffn_w1, L0_ffn_b1, L0_ffn_w2, L0_ffn_b2, L1_gnn_weight, L1_ffn_w_gate, L1_ffn_w_up, L1_ffn_w_down):
    import jax
    import jax.numpy as jnp

    def _L0_gnn_ref(x, edge_index, W_l, b_l, W_r, gamma, beta):
        import jax, jax.numpy as jnp
        import numpy as np
        N = 12500
        E = 100000
        D_IN = 512
        D_OUT = 512
        EPS = 1e-05
        n = x.shape[0]
        src, dst = (edge_index[0], edge_index[1])
        summed = jax.ops.segment_sum(x[src], dst, num_segments=n)
        cnt = jax.ops.segment_sum(jnp.ones((src.shape[0],), x.dtype), dst, num_segments=n)
        aggr = summed / jnp.maximum(cnt, 1.0)[:, None]
        h = aggr @ W_l.T + b_l + x @ W_r.T
        mu = jnp.mean(h, axis=0)
        var = jnp.mean(jnp.square(h - mu), axis=0)
        h_norm = (h - mu) * jax.lax.rsqrt(var + EPS) * gamma + beta
        return jax.nn.relu(h_norm)

    def _L0_ffn_ref(x, router_w, router_b, w1, b1, w2, b2):
        import jax, jax.numpy as jnp
        import numpy as np
        D_MODEL = 512
        D_FF = 256
        N_EXPERTS = 8
        TOP_K = 2
        leading = x.shape[:-1]
        d = x.shape[-1]
        x_flat = x.reshape(-1, d)
        T = x_flat.shape[0]
        logits = x_flat @ router_w + router_b
        probs = jax.nn.softmax(logits, axis=-1)
        sel_w, sel_idx = jax.lax.top_k(probs, TOP_K)
        sel_w = sel_w / (jnp.sum(sel_w, axis=-1, keepdims=True) + 1e-09)
        tok = jnp.arange(T)
        comb = jnp.zeros((T, N_EXPERTS), dtype=x_flat.dtype)
        for k in range(TOP_K):
            comb = comb.at[tok, sel_idx[:, k]].add(sel_w[:, k])
        out = jnp.zeros_like(x_flat)
        for e in range(N_EXPERTS):
            h = jax.nn.gelu(x_flat @ w1[e] + b1[e], approximate=False)
            y = h @ w2[e] + b2[e]
            out = out + comb[:, e:e + 1] * y
        return out.reshape(*leading, d)

    def _L1_gnn_ref(h, weight, edge_weight, src, dst):
        import jax, jax.numpy as jnp
        import numpy as np
        N_NODES = 12500
        N_EDGES = 200000
        D_IN = 512
        D_OUT = 512
        hp = h @ weight
        msgs = hp[src] * edge_weight[:, None]
        agg = jax.ops.segment_sum(msgs, dst, num_segments=h.shape[0])
        return jax.nn.relu(agg)

    def _L1_ffn_ref(x, w_gate, w_up, w_down):
        import jax, jax.numpy as jnp
        import numpy as np
        DIM = 512
        FFN_DIM = 1408
        GROUP = 128
        EPS = 1e-05

        def _quantize_weight(w, group_size):
            o, i = w.shape
            wg = w.reshape(o, i // group_size, group_size)
            scale = jnp.mean(jnp.abs(wg), axis=-1, keepdims=True) + EPS
            wq = jnp.clip(jnp.round(wg / scale), -1.0, 1.0) * scale
            return wq.reshape(o, i)

        def _bitlinear(x, w, group_size=GROUP):
            wq = w + jax.lax.stop_gradient(_quantize_weight(w, group_size) - w)
            return jnp.einsum('bsd,fd->bsf', x, wq)
        gate = _bitlinear(x, w_gate)
        up = _bitlinear(x, w_up)
        h = jax.nn.silu(gate) * up
        return _bitlinear(h, w_down)
    edge_index = jnp.stack([src, dst])
    x = x + _L0_gnn_ref(_layernorm(x, axis=-1), edge_index, L0_gnn_W_l, L0_gnn_b_l, L0_gnn_W_r, L0_gnn_gamma, L0_gnn_beta)
    x = x + _L0_ffn_ref(_layernorm(x, axis=-1)[None], L0_ffn_router_w, L0_ffn_router_b, L0_ffn_w1, L0_ffn_b1, L0_ffn_w2, L0_ffn_b2)[0]
    x = x + _L1_gnn_ref(_layernorm(x, axis=-1), L1_gnn_weight, edge_weight, src, dst)
    x = x + _L1_ffn_ref(_layernorm(x, axis=-1)[None], L1_ffn_w_gate, L1_ffn_w_up, L1_ffn_w_down)[0]
    return x

_drawn_inputs = setup_inputs


def setup_inputs(seed=0):
    import zlib

    import numpy as np

    out = dict(_drawn_inputs(seed))
    spreads = {'L0_gnn_b_l': (0.0, 0.8),
     'L0_gnn_gamma': (1.0, 0.2),
     'L0_gnn_beta': (0.0, 0.1),
     'L0_ffn_router_b': (0.0, 0.1)}
    factors = {'L0_ffn_b1': 7.707}
    for name, (base, spread) in spreads.items():
        noise = np.random.default_rng([zlib.crc32(name.encode()), seed]).standard_normal(out[name].shape)
        drawn = base * np.exp(spread * noise) if base else spread * noise
        out[name] = jnp.asarray(drawn.astype(out[name].dtype))
    for name, factor in factors.items():
        out[name] = (out[name] * factor).astype(out[name].dtype)
    return out
```

```python
import concourse.bass as bass
from concourse import mybir
from contextlib import ExitStack


def gnn_kernel(nc, x, src, dst, edge_weight, W_l, b_l, W_r, gamma, beta, router_w, router_b,
               w1, b1, w2, b2, W_g, w_gate, w_up, w_down, out, upto=99):
    f32, f16, i32 = mybir.dt.float32, mybir.dt.float16, mybir.dt.int32
    ALU = mybir.AluOpType
    ACT = mybir.ActivationFunctionType
    AX = mybir.AxisListType
    ds = bass.ds

    N, D = x.shape
    E = src.shape[0]
    P = 128
    KC = D // P
    NB = -(-N // P)
    LAST = N - (NB - 1) * P
    NP = NB * P
    NE, _, FE = w1.shape
    FF = w_gate.shape[0]
    FT = FF // P
    EPS = 1e-5
    WS = 256.0

    G = 16
    NG = -(-E // (P * G)) * P
    HT = 9
    HE = HT * P
    CE = 2 * HE
    GPC = CE // G
    EP = NG * G + CE
    MAXCH = -(-NG // GPC)
    BIG = 8192.0
    SPLIT = 50

    def dram(name, shape, dt):
        return nc.dram_tensor(name, shape, dt, kind="Internal").ap()

    src_p, dst_p = dram("src_p", [EP], i32), dram("dst_p", [EP], i32)
    ew_p = dram("ew_p", [EP], f32)
    group_min, group_max = dram("group_min", [NG], f32), dram("group_max", [NG], f32)
    xn1 = dram("xn1", [NP, 2 * D], f16)
    hpre = dram("hpre", [NP, D], f32)
    NS = 2 * N // P + NE
    FULL = -(-2 * N // P)
    x1_d, x2_d = dram("x1_d", [NP, D], f32), dram("x2_d", [NP, D], f32)
    z_d, xn3 = dram("z_d", [NP, 2 * D], f16), dram("xn3", [NP, 2 * D], f16)
    items_in = dram("items_in", [(NS + 1) * P, 2 * D], f16)
    items_out = dram("items_out", [NS * P, D], f32)

    def each_block(eng, body):
        body(0, 0, P)
        body(1, 1, P)
        with eng.Fori(2, NB - 1, 2) as n:
            b = n.with_bounds(min_val=2, max_val=NB - 3)
            body(b, 0, P)
            body(b + 1, 1, P)
        body(NB - 1, 0, LAST)

    class Item:

        def __init__(self, k, i, count):
            self.k, self.i = k, i
            self.fixed = isinstance(k, int)
            self.valid = not self.fixed or 0 <= k < count
            self.rows = LAST if self.fixed and k == NB - 1 and count == NB else P
            self.loads = 8 * (k - i) + 16

        def after(self, n):
            return not self.fixed or self.k >= n

    def pipeline(eng, count, lag, body):
        lead = lag + 2 + lag % 2
        stop = lead + 2 * ((count - 1 - lead) // 2)

        def step(t, i):
            def item(s):
                found = Item(t - s, (i - s) % 2, count)
                return found if found.valid else None
            body(item)

        for t in range(lead):
            step(t, t % 2)
        with eng.Fori(lead, stop, 2) as n:
            t = n.with_bounds(min_val=lead, max_val=stop - 2)
            step(t, 0)
            step(t + 1, 1)
        for t in range(stop, count + lag):
            step(t, t % 2)

    ctx = ExitStack()
    with ctx:
        def sb(name, shape, dt, at=ctx):
            return at.enter_context(nc.sbuf_tensor(name, shape, dt))

        def pb(name, shape, dt, at=ctx):
            return at.enter_context(nc.psum_tensor(name, shape, dt))

        def sem(name, at):
            if at not in sems_of:
                sems_of[at] = []

                def release():
                    nc.clear_and_free_semaphores(sems_of[at])
                    nc.all_engine_barrier()

                at.callback(release)
            sems_of[at].append(nc.alloc_semaphore(f"{name}_p{len(sems_of)}"))
            return sems_of[at][-1]

        sems_of = {}

        table = sb("table", [1, 3 * 64], i32)
        ident16 = sb("ident16", [P, P], f16)
        ident32 = sb("ident32", [P, P], f32)
        iota_row = sb("iota_row", [P, P], f32)
        zeros16 = sb("zeros16", [P, D], f16)
        ones_col = sb("ones_col", [P, 1], f16)
        eps_col = sb("eps_col", [P, 1], f32)
        bn_scale = sb("bn_scale", [P, D], f32)
        bn_shift = sb("bn_shift", [P, D], f32)
        place = sb("place", [P, NB, 2], i32)
        share = sb("share", [P, NB, 2], f32)
        slots = sb("slots", [1, 128], i32)

        class Norm:

            def __init__(self, at, name, buffers=2, x=None):
                self.x = x or [sb(f"{name}_x{i}", [P, D], f32, at) for i in range(buffers)]
                self.z = [sb(f"{name}_z{i}", [P, D], f32, at) for i in range(buffers)]
                self.hl = [sb(f"{name}_hl{i}", [P, 2 * D], f16, at) for i in range(buffers)]
                self.st6 = sb(f"{name}_st6", [P, 6], f32, at)
                self.mv = [sb(f"{name}_mv{i}", [P, 4], f32, at) for i in range(buffers)]
                self.var_done, self.std_done, self.z_done, self.hi_done, self.lo_done = (
                    sem(f"{name}_{n}", at) for n in ("var_done", "std_done", "z_done", "hi_done", "lo_done"))

            def var(self, dve, m):
                r = slice(0, m.rows)
                nc.vector.bn_stats(self.st6[r, :], self.x[m.i][r, :])
                dve.drain()
                nc.vector.bn_aggr(self.mv[m.i][r, 0:2], self.st6[r, :]).then_inc(self.var_done, 1)

            def std(self, act, m):
                r = slice(0, m.rows)
                act.wait_ge(self.var_done, m.k + 1)
                nc.scalar.activation(self.mv[m.i][r, 2:3], self.mv[m.i][r, 1:2], ACT.Sqrt, bias=eps_col[r, :])\
                  .then_inc(self.std_done, 1)

            def scale(self, dve, m):
                r = slice(0, m.rows)
                dve.wait_ge(self.std_done, m.k + 1)
                nc.vector.reciprocal(self.mv[m.i][r, 3:4], self.mv[m.i][r, 2:3])
                dve.drain()
                nc.vector.tensor_scalar(self.z[m.i][r, :], self.x[m.i][r, :], self.mv[m.i][r, 0:1],
                                        self.mv[m.i][r, 3:4], ALU.subtract, ALU.mult).then_inc(self.z_done, 1)

            def hi(self, act, m):
                r = slice(0, m.rows)
                act.wait_ge(self.z_done, m.k + 1)
                nc.scalar.activation(self.hl[m.i][r, 0:D], self.z[m.i][r, :], ACT.Copy).then_inc(self.hi_done, 1)

            def lo(self, dve, m):
                r = slice(0, m.rows)
                dve.wait_ge(self.hi_done, m.k + 1)
                nc.vector.tensor_tensor(self.hl[m.i][r, D:2 * D], self.z[m.i][r, :], self.hl[m.i][r, 0:D],
                                        ALU.subtract).then_inc(self.lo_done, 1)

        def layer0():
            ph = ExitStack()
            with ph:
                wlr = sb("wlr", [P, 2 * KC, 2, D], f16, ph)
                prepare(wlr)
                if upto >= 2:
                    sage(wlr)

        def prepare(wlr):
            p1 = ExitStack()
            with p1:
                pad_0 = sb("pad_0", [SPLIT, (EP - E) // SPLIT], i32, p1)
                pad_d = sb("pad_d", [SPLIT, (EP - E) // SPLIT], i32, p1)
                dst_all = sb("dst_all", [P, NG * G // P], i32, p1)
                gmin = sb("gmin", [P, NG // P], f32, p1)
                gmax = sb("gmax", [P, NG // P], f32, p1)
                gmin_all = sb("gmin_all", [64, NG], f32, p1)
                gmax_all = sb("gmax_all", [64, NG], f32, p1)
                g_iota = sb("g_iota", [64, NG], f32, p1)
                win = sb("win", [64, 8], f32, p1)
                cols = sb("cols", [64, 3], f32, p1)
                k_iota = sb("k_iota", [64, MAXCH + 1], f32, p1)
                k_hit = sb("k_hit", [64, MAXCH + 1], f32, p1)
                tri = sb("tri", [64, 64], f32, p1)
                wnat = sb("wnat", [P, 2, KC, D], f32, p1)
                xt = sb("xt", [P, 2, D], f32, p1)
                zt = sb("zt", [P, D], f32, p1)
                zhl = sb("zhl", [P, 2, 2 * D], f16, p1)
                st6 = sb("st6", [P, 6], f32, p1)
                mv = sb("mv", [P, 4], f32, p1)
                zpad = sb("zpad", [32, 2 * D], f16, p1)
                tab_ps = pb("tab_ps", [1, 512], f32, p1)
                w_ps = [pb(f"w_ps{i}", [P, D], f32, p1) for i in range(2)]

                pads_set = sem("pads_set", p1)
                edges_copied = sem("edges_copied", p1)
                dst_loaded = sem("dst_loaded", p1)
                groups_reduced = sem("groups_reduced", p1)
                groups_stored = sem("groups_stored", p1)
                groups_loaded = sem("groups_loaded", p1)
                pool_zeroed = sem("pool_zeroed", p1)
                consts_set = sem("consts_set", p1)
                windows_found = sem("windows_found", p1)
                table_summed = sem("table_summed", p1)
                w_loaded = sem("w_loaded", p1)
                w_turned = sem("w_turned", p1)
                w_hi_done = sem("w_hi_done", p1)
                w_lo_done = sem("w_lo_done", p1)
                x_loaded = [sem(f"x_loaded{i}", p1) for i in range(2)]
                pad_stored = sem("pad_stored", p1)
                var_done = sem("var_done", p1)
                std_done = sem("std_done", p1)
                z_done = sem("z_done", p1)
                z_hi_done = sem("z_hi_done", p1)
                z_lo_done = sem("z_lo_done", p1)
                z_stored = [sem(f"z_stored{i}", p1) for i in range(2)]

                block = p1.enter_context(nc.Block())

                @block.gpsimd
                def _(pool):
                    nc.gpsimd.memset(pad_0[:], 0).then_inc(pads_set, 1)
                    nc.gpsimd.memset(pad_d[:], NP).then_inc(pads_set, 1)
                    nc.gpsimd.memset(zpad[:], 0.0).then_inc(pool_zeroed, 1)
                    nc.gpsimd.memset(eps_col[:], EPS).then_inc(pool_zeroed, 1)
                    nc.gpsimd.memset(ident16[:], 0.0).then_inc(pool_zeroed, 1)
                    nc.gpsimd.memset(ident32[:], 0.0).then_inc(pool_zeroed, 1)
                    nc.gpsimd.memset(tri[:], 1.0).then_inc(pool_zeroed, 1)
                    nc.gpsimd.memset(zeros16[:], 0.0)
                    nc.gpsimd.memset(ones_col[:], 1.0)
                    pool.wait_ge(pool_zeroed, 5)
                    nc.gpsimd.affine_select(out=ident32[:], in_=ident32[:], compare_op=ALU.not_equal, fill=1.0,
                                            base=0, pattern=[[-1, P]], channel_multiplier=1).then_inc(consts_set, 1)
                    nc.gpsimd.affine_select(out=ident16[:], in_=ident16[:], compare_op=ALU.not_equal, fill=1.0,
                                            base=0, pattern=[[-1, P]], channel_multiplier=1)
                    nc.gpsimd.affine_select(out=tri[:], in_=tri[:], compare_op=ALU.is_gt, fill=0.0,
                                            base=0, pattern=[[1, 64]], channel_multiplier=-1)
                    nc.gpsimd.iota(iota_row[:], [[1, P]], base=0, channel_multiplier=0,
                                   allow_small_or_imprecise_dtypes=True)
                    nc.gpsimd.iota(k_iota[:], [[GPC, MAXCH + 1]], base=0, channel_multiplier=0,
                                   allow_small_or_imprecise_dtypes=True)
                    nc.gpsimd.iota(win[:, 0:1], [[0, 1]], base=0, channel_multiplier=P,
                                   allow_small_or_imprecise_dtypes=True)
                    nc.gpsimd.iota(g_iota[:], [[1, NG]], base=0, channel_multiplier=0,
                                   allow_small_or_imprecise_dtypes=True).then_inc(consts_set, 1)

                    def store(b, i, nr):
                        pool.wait_ge(z_hi_done, b + 1)
                        pool.wait_ge(z_lo_done, b + 1)
                        pool.dma_start(xn1[ds(b * P, nr), :], zhl[0:nr, i, :]).then_inc(z_stored[i], 16)

                    each_block(pool, store)
                    for i in range(2):
                        pool.wait_ge(z_stored[i], 16 * ((NB + 1 - i) // 2))

                @block.sync
                def _(sp):
                    def load(b, i, nr):
                        if not isinstance(b, int) or b >= 2:
                            sp.wait_ge(z_done, b - 1)
                        sp.dma_start(xt[0:nr, i, :], x[ds(b * P, nr), :]).then_inc(x_loaded[i], 16)

                    for a, padded in ((src, src_p), (dst, dst_p), (edge_weight, ew_p)):
                        sp.dma_start(padded[0:E].rearrange("(a b) -> a b", a=SPLIT),
                                     a.rearrange("(a b) -> a b", a=SPLIT)).then_inc(edges_copied, 16)
                    sp.wait_ge(pads_set, 2)
                    for padded, pad in ((src_p, pad_0), (dst_p, pad_d), (ew_p, pad_0)):
                        view = pad[:].bitcast(f32) if padded is ew_p else pad[:]
                        sp.dma_start(padded[E:EP].rearrange("(a b) -> a b", a=SPLIT), view)\
                          .then_inc(edges_copied, 16)
                    for n, w in enumerate((W_l, W_r)):
                        sp.dma_start(wnat[:, n], w.rearrange("(c p) k -> p c k", p=P)).then_inc(w_loaded, 16)
                    sp.wait_ge(edges_copied, 96)
                    sp.dma_start(dst_all[:], dst_p[0:NG * G].rearrange("(p c) -> p c", p=P)).then_inc(dst_loaded, 16)
                    sp.wait_ge(pool_zeroed, 1)
                    sp.dma_start(xn1[N:NP, :], zpad[0:NP - N, :]).then_inc(pad_stored, 16)
                    sp.wait_ge(groups_reduced, 2)
                    sp.dma_start(group_min.rearrange("(p c) -> p c", p=P), gmin[:]).then_inc(groups_stored, 16)
                    sp.dma_start(group_max.rearrange("(p c) -> p c", p=P), gmax[:]).then_inc(groups_stored, 16)
                    sp.wait_ge(groups_stored, 32)
                    sp.dma_start(gmin_all[:], group_min.partition_broadcast(64)).then_inc(groups_loaded, 16)
                    sp.dma_start(gmax_all[:], group_max.partition_broadcast(64)).then_inc(groups_loaded, 16)
                    each_block(sp, load)
                    sp.wait_ge(pad_stored, 16)

                @block.tensor
                def _(pe):
                    pe.wait_ge(w_loaded, 32)
                    pe.wait_ge(consts_set, 1)
                    for k in range(2 * KC):
                        if k >= 2:
                            pe.wait_ge(w_hi_done, k - 1)
                            pe.wait_ge(w_lo_done, k - 1)
                        for o in range(KC):
                            last = nc.tensor.transpose(w_ps[k % 2][:, o * P:(o + 1) * P],
                                                       wnat[:, k // KC, o, (k % KC) * P:(k % KC + 1) * P],
                                                       ident32[:])
                        last.then_inc(w_turned, 1)
                    pe.wait_ge(windows_found, 1)
                    pe.wait_ge(consts_set, 2)
                    nc.tensor.matmul(tab_ps[0:1, 0:64], cols[:, 0:1], ident32[0:64, 0:64], start=True, stop=True)
                    nc.tensor.matmul(tab_ps[0:1, 64:128], cols[:, 0:1], tri[:], start=True, stop=True)
                    nc.tensor.matmul(tab_ps[0:1, 128:192], cols[:, 1:2], ident32[0:64, 0:64],
                                     start=True, stop=True).then_inc(table_summed, 1)

                @block.scalar
                def _(act):
                    for k in range(2 * KC):
                        act.wait_ge(w_turned, k + 1)
                        nc.scalar.activation(wlr[:, k, 0, :], w_ps[k % 2][:], ACT.Copy, scale=WS)\
                          .then_inc(w_hi_done, 1)

                    def normalise(b, i, nr):
                        act.wait_ge(var_done, b + 1)
                        nc.scalar.activation(mv[0:nr, 2:3], mv[0:nr, 1:2], ACT.Sqrt, bias=eps_col[0:nr, :])\
                          .then_inc(std_done, 1)
                        if not isinstance(b, int) or b >= 2:
                            act.wait_ge(z_stored[i], (b - i) * 8)
                        act.wait_ge(z_done, b + 1)
                        nc.scalar.activation(zhl[0:nr, i, 0:D], zt[0:nr, :], ACT.Copy).then_inc(z_hi_done, 1)

                    each_block(act, normalise)

                @block.vector
                def _(dve):
                    dve.wait_ge(dst_loaded, 16)
                    groups = dst_all[:].rearrange("p (c g) -> p c g", g=G)
                    nc.vector.tensor_reduce(gmin[:], groups, AX.X, ALU.min).then_inc(groups_reduced, 1)
                    nc.vector.tensor_reduce(gmax[:], groups, AX.X, ALU.max).then_inc(groups_reduced, 1)
                    for k in range(2 * KC):
                        dve.wait_ge(w_hi_done, k + 1)
                        nc.vector.scalar_tensor_tensor(wlr[:, k, 1, :], w_ps[k % 2][:], WS, wlr[:, k, 0, :],
                                                       ALU.mult, ALU.subtract).then_inc(w_lo_done, 1)
                    dve.wait_ge(groups_loaded, 32)
                    dve.wait_ge(consts_set, 2)
                    nc.vector.tensor_scalar(win[:, 1:2], win[:, 0:1], float(P - 1), None, ALU.add)
                    dve.drain()
                    nc.vector.tensor_scalar(gmin_all[:], gmin_all[:], win[:, 1:2], None, ALU.is_le)
                    dve.drain()
                    nc.vector.scalar_tensor_tensor(gmax_all[:], gmax_all[:], win[:, 0:1], gmin_all[:],
                                                   ALU.is_ge, ALU.mult)
                    dve.drain()
                    nc.vector.scalar_tensor_tensor(gmin_all[:], g_iota[:], 1.0, gmax_all[:], ALU.add, ALU.mult)
                    nc.vector.tensor_scalar(g_iota[:], g_iota[:], -1.0, BIG, ALU.mult, ALU.add)
                    dve.drain()
                    nc.vector.tensor_reduce(win[:, 2:3], gmin_all[:], AX.X, ALU.max)
                    nc.vector.tensor_tensor(gmax_all[:], gmax_all[:], g_iota[:], ALU.mult)
                    dve.drain()
                    nc.vector.tensor_reduce(win[:, 3:4], gmax_all[:], AX.X, ALU.max)
                    dve.drain()
                    nc.vector.tensor_scalar(win[:, 4:5], win[:, 3:4], -1.0, BIG, ALU.mult, ALU.add)
                    dve.drain()
                    nc.vector.tensor_tensor(win[:, 5:6], win[:, 2:3], win[:, 4:5], ALU.subtract)
                    nc.vector.tensor_scalar(cols[:, 1:2], win[:, 4:5], float(NG - 1), float(G), ALU.min, ALU.mult)
                    dve.drain()
                    nc.vector.tensor_scalar(k_hit[:], k_iota[:], win[:, 5:6], None, ALU.is_lt)
                    dve.drain()
                    nc.vector.tensor_reduce(win[:, 6:7], k_hit[:], AX.X, ALU.add)
                    dve.drain()
                    nc.vector.tensor_scalar(cols[:, 0:1], win[:, 6:7], 1.0, None, ALU.max).then_inc(windows_found, 1)
                    dve.wait_ge(table_summed, 1)
                    nc.vector.tensor_copy(table[:], tab_ps[:, 0:192])

                    def normalise(b, i, nr):
                        dve.wait_ge(x_loaded[i], (b - i) * 8 + 16)
                        nc.vector.bn_stats(st6[0:nr, :], xt[0:nr, i, :])
                        dve.drain()
                        nc.vector.bn_aggr(mv[0:nr, 0:2], st6[0:nr, :]).then_inc(var_done, 1)
                        dve.wait_ge(std_done, b + 1)
                        nc.vector.reciprocal(mv[0:nr, 3:4], mv[0:nr, 2:3])
                        dve.drain()
                        nc.vector.tensor_scalar(zt[0:nr, :], xt[0:nr, i, :], mv[0:nr, 0:1], mv[0:nr, 3:4],
                                                ALU.subtract, ALU.mult).then_inc(z_done, 1)
                        dve.wait_ge(z_hi_done, b + 1)
                        nc.vector.tensor_tensor(zhl[0:nr, i, D:2 * D], zt[0:nr, :], zhl[0:nr, i, 0:D],
                                                ALU.subtract).then_inc(z_lo_done, 1)
                        dve.drain()

                    each_block(dve, normalise)

        class Edges:

            def __init__(self, at, weighted):
                tag = "w_" if weighted else "u_"
                self.weighted = weighted
                self.idx = [sb(f"{tag}idx{h}", [P, HT], i32, at) for h in range(2)]
                self.tgt = [sb(f"{tag}tgt{h}", [P, HT], i32, at) for h in range(2)]
                self.rows = sb(f"{tag}rows", [P, 2 * HT, 2 * D], f16, at)
                self.local = [sb(f"{tag}local{h}", [P, HT], f32, at) for h in range(2)]
                self.mask = [sb(f"{tag}mask{h}", [P, HT, P], f16, at) for h in range(2)]
                self.first_node = sb(f"{tag}first_node", [P, 1], f32, at)
                if weighted:
                    self.ew = [sb(f"{tag}ew{h}", [P, HT], f32, at) for h in range(2)]
                    self.ew_hi16 = [sb(f"{tag}ew_hi16_{h}", [P, HT], f16, at) for h in range(2)]
                    self.ew_hi = [sb(f"{tag}ew_hi{h}", [P, HT], f32, at) for h in range(2)]
                    self.ew_lo = [sb(f"{tag}ew_lo{h}", [P, HT], f32, at) for h in range(2)]
                    self.mask_lo = [sb(f"{tag}mask_lo{h}", [P, HT, P], f16, at) for h in range(2)]
                self.idx_loaded = [sem(f"{tag}idx_loaded{h}", at) for h in range(2)]
                self.tgt_loaded = [sem(f"{tag}tgt_loaded{h}", at) for h in range(2)]
                self.gathered = [sem(f"{tag}gathered{j}", at) for j in range(2 * HT)]
                self.idx_seen = sem(f"{tag}idx_seen", at)
                self.masked = sem(f"{tag}masked", at)
                self.summed = sem(f"{tag}summed", at)

            def chunks(self, eng, b, body):
                n = eng.value_load(table[0:1, ds(b, 1)], min_val=1, max_val=MAXCH)
                q0 = eng.value_load(table[0:1, ds(b + 64, 1)], min_val=0, max_val=NB * MAXCH)
                with eng.Fori(0, n) as i:
                    body(eng.snap(q0 + i).with_bounds(min_val=0, max_val=NB * MAXCH), i)

            def load(self, eng, b):
                e0 = eng.value_load(table[0:1, ds(b + 128, 1)], min_val=0, max_val=(NG - 1) * G)

                def chunk(q, i):
                    for h in range(2):
                        eng.wait_ge(self.summed, q * 2 + (h + 1))
                        at = eng.snap(e0 + i * CE + h * HE).with_bounds(min_val=0, max_val=EP - HE)
                        part = lambda t: t[ds(at, HE)].rearrange("(p j) -> p j", j=HT)
                        eng.dma_start(self.idx[h][:], part(src_p)).then_inc(self.idx_loaded[h], 16)
                        eng.dma_start(self.tgt[h][:], part(dst_p)).then_inc(self.tgt_loaded[h], 16)
                        if self.weighted:
                            eng.dma_start(self.ew[h][:], part(ew_p)).then_inc(self.tgt_loaded[h], 16)

                self.chunks(eng, b, chunk)

            def gather(self, eng, b, rows_of):
                def chunk(q, i):
                    for h in range(2):
                        eng.wait_ge(self.idx_loaded[h], q * 16 + 16)
                        eng.sem_inc(self.idx_seen, 1)
                        for j in range(HT):
                            eng.indirect_dma_start(
                                out=self.rows[:, h * HT + j, :], out_offset=None, in_=rows_of,
                                in_offset=bass.IndirectOffsetOnAxis(ap=self.idx[h][:, j:j + 1], axis=0),
                            ).then_inc(self.gathered[h * HT + j], 16)

                self.chunks(eng, b, chunk)

            def chunk_masks(self, dve, q):
                loads = 2 if self.weighted else 1
                for h in range(2):
                    dve.wait_ge(self.tgt_loaded[h], q * (16 * loads) + 16 * loads)
                    nc.vector.tensor_scalar(self.local[h][:], self.tgt[h][:], self.first_node[:], None,
                                            ALU.subtract)
                    if self.weighted:
                        nc.vector.tensor_copy(self.ew_hi16[h][:], self.ew[h][:])
                        dve.drain()
                        nc.vector.tensor_copy(self.ew_hi[h][:], self.ew_hi16[h][:])
                        nc.vector.tensor_tensor(self.ew_lo[h][:], self.ew[h][:], self.ew_hi16[h][:],
                                                ALU.subtract)
                    dve.drain()
                    for j in range(HT):
                        to = self.local[h][:, j:j + 1]
                        if self.weighted:
                            nc.vector.tensor_scalar(self.mask[h][:, j, :], iota_row[:], to,
                                                    self.ew_hi[h][:, j:j + 1], ALU.is_equal, ALU.mult)
                            last = nc.vector.tensor_scalar(self.mask_lo[h][:, j, :], iota_row[:], to,
                                                           self.ew_lo[h][:, j:j + 1], ALU.is_equal, ALU.mult)
                        else:
                            last = nc.vector.tensor_scalar(self.mask[h][:, j, :], iota_row[:], to, None,
                                                           ALU.is_equal)
                    last.then_inc(self.masked, 1)

            def masks(self, dve, b):
                self.chunks(dve, b, lambda q, i: self.chunk_masks(dve, q))
                self.next_block(dve)

            def masks_first(self, dve, b):
                q0 = dve.value_load(table[0:1, ds(b + 64, 1)], min_val=0, max_val=NB * MAXCH)
                self.chunk_masks(dve, q0)

            def masks_rest(self, dve, b):
                n = dve.value_load(table[0:1, ds(b, 1)], min_val=1, max_val=MAXCH)
                q0 = dve.value_load(table[0:1, ds(b + 64, 1)], min_val=0, max_val=NB * MAXCH)
                with dve.If(n > 1):
                    with dve.Fori(1, n) as i:
                        self.chunk_masks(dve, dve.snap(q0 + i).with_bounds(min_val=0, max_val=NB * MAXCH))
                self.next_block(dve)

            def next_block(self, dve):
                dve.drain()
                nc.vector.tensor_scalar(self.first_node[:], self.first_node[:], float(P), None, ALU.add)
                dve.drain()

            def sum(self, pe, b, acc, count):
                nc.tensor.matmul(acc[:], zeros16[:, 0:P], zeros16[:], start=True, stop=False, skip_group_check=True)
                if count is not None:
                    nc.tensor.matmul(count, zeros16[:, 0:P], zeros16[:, 0:1], start=True, stop=False,
                                     skip_group_check=True)

                def add(to, mask, rows):
                    return nc.tensor.matmul(to, mask, rows, start=False, stop=False, skip_group_check=True)

                def chunk(q, i):
                    for h in range(2):
                        pe.wait_ge(self.masked, q * 2 + (h + 1))
                        for j in range(HT):
                            t = h * HT + j
                            pe.wait_ge(self.gathered[t], q * 16 + 16)
                            mask = self.mask[h][:, j, :]
                            last = add(acc[:], mask, self.rows[:, t, 0:D])
                            last = add(acc[:], mask, self.rows[:, t, D:2 * D])
                            if self.weighted:
                                last = add(acc[:], self.mask_lo[h][:, j, :], self.rows[:, t, 0:D])
                            if count is not None:
                                last = add(count, mask, ones_col[:])
                        last.then_inc(self.summed, 1)

                self.chunks(pe, b, chunk)

        def split_product(out, left, right, chunks, last_sem=None):
            for c in range(chunks):
                for n, (l, r) in enumerate(((0, 0), (0, 1), (1, 0))):
                    last = nc.tensor.matmul(out, left(c, l), right(c, r), start=(c == 0 and n == 0),
                                            stop=(c == chunks - 1 and n == 2))
            return last

        def sage(wlr):
            p2 = ExitStack()
            with p2:
                edges = Edges(p2, False)
                own = sb("own", [P, 2 * D], f16, p2)
                mean_hl = sb("mean_hl", [P, 2, D], f16, p2)
                mean_t = sb("mean_t", [P, 2, KC, P], f16, p2)
                own_t = sb("own_t", [P, 2, KC, P], f16, p2)
                inv = sb("inv", [P, 2], f32, p2)
                h_sb = sb("h_sb", [P, D], f32, p2)
                h_sq = sb("h_sq", [P, D], f32, p2)
                bias = sb("bias", [P, D], f32, p2)
                gam = sb("gam", [P, D], f32, p2)
                bet = sb("bet", [P, D], f32, p2)
                ones32 = sb("ones32", [P, 2, P], f32, p2)
                stat = sb("stat", [P, 3, D], f32, p2)
                acc = pb("acc", [P, D], f32, p2)
                cnt = pb("cnt", [P, D], f32, p2)
                mean_ps = pb("mean_ps", [P, 2, KC, P], f16, p2)
                own_ps = pb("own_ps", [P, 2, KC, P], f16, p2)
                h_ps = pb("h_ps", [P, D], f32, p2)
                sum_ps = pb("sum_ps", [P, D], f32, p2)
                sq_ps = pb("sq_ps", [P, D], f32, p2)

                ones_set = sem("ones_set", p2)
                rows_loaded = sem("rows_loaded", p2)
                own_loaded = sem("own_loaded", p2)
                acc_ready = sem("acc_ready", p2)
                inv_done = sem("inv_done", p2)
                mean_hi_done = sem("mean_hi_done", p2)
                mean_lo_done = sem("mean_lo_done", p2)
                turned = sem("turned", p2)
                mean_t_done = sem("mean_t_done", p2)
                own_t_done = sem("own_t_done", p2)
                h_summed = sem("h_summed", p2)
                h_done = sem("h_done", p2)
                h_sq_done = sem("h_sq_done", p2)
                h_stored = sem("h_stored", p2)
                stats_added = sem("stats_added", p2)
                bn_var = sem("bn_var", p2)
                bn_std = sem("bn_std", p2)

                block = p2.enter_context(nc.Block())

                def after_first(eng, body):
                    body(0)
                    with eng.Fori(1, NB - 1) as b:
                        body(b)
                    body(NB - 1)

                first = lambda b: isinstance(b, int) and b == 0
                final = lambda b: isinstance(b, int) and b == NB - 1

                @block.gpsimd
                def _(pool):
                    nc.gpsimd.memset(ones32[:], 1.0).then_inc(ones_set, 1)
                    pool.wait_ge(ones_set, 1)
                    nc.gpsimd.affine_select(out=ones32[:, 1, :], in_=ones32[:, 1, :], compare_op=ALU.is_gt,
                                            fill=0.0, base=LAST, pattern=[[0, P]], channel_multiplier=-1)\
                        .then_inc(ones_set, 1)
                    after_first(pool, lambda b: edges.gather(pool, b, xn1))

                @block.sync
                def _(sp):
                    for t, a in ((bias, b_l), (gam, gamma), (bet, beta)):
                        sp.dma_start(t[:], a.partition_broadcast(P)).then_inc(rows_loaded, 16)

                    def step(b):
                        edges.load(sp, b)
                        if not first(b):
                            sp.wait_ge(turned, b)
                        sp.dma_start(own[:], xn1[ds(b * P, P), :]).then_inc(own_loaded, 16)

                    after_first(sp, step)

                @block.tensor
                def _(pe):
                    pe.sem_inc(edges.summed, 2)
                    pe.wait_ge(ones_set, 2)
                    for t in (sum_ps, sq_ps):
                        nc.tensor.matmul(t[:], zeros16[:, 0:P], zeros16[:], start=True, stop=False,
                                         skip_group_check=True)

                    def project(b):
                        pe.wait_ge(mean_t_done, b + 1)
                        pe.wait_ge(own_t_done, b + 1)
                        split_product(h_ps[:], lambda c, part: (mean_t if c < KC else own_t)[:, part, c % KC, :],
                                      lambda c, part: wlr[:, c, part, :], 2 * KC).then_inc(h_summed, 1)

                    def turn(b):
                        pe.wait_ge(mean_hi_done, b + 1)
                        pe.wait_ge(mean_lo_done, b + 1)
                        pe.wait_ge(own_loaded, b * 16 + 16)
                        for part in range(2):
                            for c in range(KC):
                                nc.tensor.transpose(mean_ps[:, part, c, :], mean_hl[:, part, c * P:(c + 1) * P],
                                                    ident16[:])
                                last = nc.tensor.transpose(own_ps[:, part, c, :],
                                                           own[:, part * D + c * P:part * D + (c + 1) * P],
                                                           ident16[:])
                        last.then_inc(turned, 1)

                    def add_stats(b, valid):
                        pe.wait_ge(h_done, b + 1)
                        pe.wait_ge(h_sq_done, b + 1)
                        nc.tensor.matmul(sum_ps[:], ones32[:, valid, :], h_sb[:], start=False, stop=False,
                                         skip_group_check=True)
                        nc.tensor.matmul(sq_ps[:], ones32[:, valid, :], h_sq[:], start=False, stop=False,
                                         skip_group_check=True).then_inc(stats_added, 1)

                    def step(b):
                        edges.sum(pe, b, acc, cnt[:, 0:1])
                        nc.tensor.matmul(cnt[:, 0:1], zeros16[:, 0:P], zeros16[:, 0:1], start=False, stop=True,
                                         skip_group_check=True).then_inc(acc_ready, 1)
                        if not first(b):
                            project(b - 1)
                        turn(b)
                        if not first(b):
                            add_stats(b - 1, 0)

                    after_first(pe, step)
                    project(NB - 1)
                    add_stats(NB - 1, 1)

                @block.scalar
                def _(act):
                    def square(b):
                        act.wait_ge(h_done, b + 1)
                        if not first(b):
                            act.wait_ge(stats_added, b)
                        nc.scalar.activation(h_sq[:], h_sb[:], ACT.Square).then_inc(h_sq_done, 1)
                        act.dma_start(hpre[ds(b * P, P), :], h_sb[:]).then_inc(h_stored, 16)

                    def step(b):
                        act.wait_ge(inv_done, b + 1)
                        nc.scalar.activation(mean_hl[:, 0, :], acc[:], ACT.Copy, scale=inv[:, 1:2])\
                          .then_inc(mean_hi_done, 1)
                        if not first(b):
                            square(b - 1)
                        act.wait_ge(turned, b + 1)
                        nc.scalar.activation(mean_t[:], mean_ps[:], ACT.Copy).then_inc(mean_t_done, 1)

                    after_first(act, step)
                    square(NB - 1)
                    act.wait_ge(h_stored, NB * 16)
                    act.wait_ge(bn_var, 1)
                    nc.scalar.activation(bn_scale[:], stat[:, 1, :], ACT.Sqrt, bias=eps_col[:]).then_inc(bn_std, 1)

                @block.vector
                def _(dve):
                    nc.vector.memset(edges.first_node[:], 0.0)
                    dve.drain()
                    dve.wait_ge(rows_loaded, 48)

                    def add_bias(b):
                        dve.wait_ge(h_summed, b + 1)
                        if not first(b):
                            dve.wait_ge(stats_added, b)
                            dve.wait_ge(h_stored, b * 16)
                        nc.vector.scalar_tensor_tensor(h_sb[:], h_ps[:], 1.0 / WS, bias[:], ALU.mult, ALU.add)\
                          .then_inc(h_done, 1)

                    def step(b):
                        edges.masks(dve, b)
                        dve.wait_ge(acc_ready, b + 1)
                        nc.vector.tensor_scalar(inv[:, 0:1], cnt[:, 0:1], 1.0, None, ALU.max)
                        dve.drain()
                        nc.vector.reciprocal(inv[:, 1:2], inv[:, 0:1]).then_inc(inv_done, 1)
                        dve.drain()
                        dve.wait_ge(mean_hi_done, b + 1)
                        nc.vector.scalar_tensor_tensor(mean_hl[:, 1, :], acc[:], inv[:, 1:2], mean_hl[:, 0, :],
                                                       ALU.mult, ALU.subtract).then_inc(mean_lo_done, 1)
                        if not first(b):
                            add_bias(b - 1)
                        dve.wait_ge(turned, b + 1)
                        nc.vector.tensor_copy(own_t[:], own_ps[:]).then_inc(own_t_done, 1)

                    after_first(dve, step)
                    add_bias(NB - 1)
                    dve.wait_ge(stats_added, NB)
                    nc.vector.tensor_scalar(stat[:, 0, :], sum_ps[:], 1.0 / N, None, ALU.mult)
                    dve.drain()
                    nc.vector.tensor_tensor(stat[:, 2, :], stat[:, 0, :], stat[:, 0, :], ALU.mult)
                    dve.drain()
                    nc.vector.scalar_tensor_tensor(stat[:, 1, :], sq_ps[:], 1.0 / N, stat[:, 2, :], ALU.mult,
                                                   ALU.subtract).then_inc(bn_var, 1)
                    dve.wait_ge(bn_std, 1)
                    nc.vector.reciprocal(stat[:, 1, :], bn_scale[:])
                    dve.drain()
                    nc.vector.tensor_tensor(bn_scale[:], stat[:, 1, :], gam[:], ALU.mult)
                    dve.drain()
                    nc.vector.tensor_tensor(stat[:, 2, :], stat[:, 0, :], bn_scale[:], ALU.mult)
                    dve.drain()
                    nc.vector.tensor_tensor(bn_shift[:], bet[:], stat[:, 2, :], ALU.subtract)

        def route():
            at = ExitStack()
            with at:
                norm = Norm(at, "n1")
                x_in = [sb(f"x_in{i}", [P, D], f32, at) for i in range(2)]
                h_in = [sb(f"h_in{i}", [P, D], f32, at) for i in range(2)]
                act_in = [sb(f"act_in{i}", [P, D], f32, at) for i in range(2)]
                z_t = sb("z_t", [P, 2, KC, P], f16, at)
                rw32 = sb("rw32", [P, KC, NE], f32, at)
                rw = sb("rw", [P, 2, KC, NE], f16, at)
                rb = sb("rb", [P, NE], f32, at)
                logits = sb("logits", [P, NB, NE], f32, at)
                less = sb("less", [P, NE], f32, at)
                t1, t2, hot1, hot2, base = (sb(n, [P, NB, NE], f32, at) for n in ("t1", "t2", "hot1", "hot2", "base"))
                hot = sb("hot", [P, NB, NE], f16, at)
                top1, top2, mx, den = (sb(n, [P, NB], f32, at) for n in ("top1", "top2", "mx", "den"))
                before = sb("before", [P, P], f16, at)
                ones = sb("ones", [P, P], f16, at)
                run1, run2 = sb("run1", [P, NB, NE], f32, at), sb("run2", [P, NB, NE], f32, at)
                tiles_i = sb("tiles_i", [P, NE], i32, at)
                tiles, end1, end2 = (sb(n, [P, NE], f32, at) for n in ("tiles", "end1", "end2"))
                slot_iota, slot_of = sb("slot_iota", [1, P], f32, at), sb("slot_of", [1, P], f32, at)
                pad_row = sb("pad_row", [1, NE], f32, at)
                z_ps = pb("z_ps", [P, 2, KC, P], f16, at)
                l_ps = pb("l_ps", [P, 512], f32, at)
                in_ps = pb("in_ps", [P, 512], f32, at)
                all_ps = pb("all_ps", [P, 512], f32, at)

                loaded = [sem(f"loaded{i}", at) for i in range(2)]
                stored = [sem(f"stored{i}", at) for i in range(2)]
                small_loaded = sem("small_loaded", at)
                consts = sem("consts", at)
                rw_split = sem("rw_split", at)
                bn_done = sem("bn_done", at)
                x1_done = sem("x1_done", at)
                turned = sem("turned", at)
                z_t_done = sem("z_t_done", at)
                routed = sem("routed", at)
                logits_done = sem("logits_done", at)
                shifted = sem("shifted", at)
                exp_done = sem("exp_done", at)
                hots_done = sem("hots_done", at)
                hot_masked = sem("hot_masked", at)
                hot_sent = sem("hot_sent", at)
                ranked = sem("ranked", at)
                zeroed = sem("zeroed", at)
                pool_mult = sem("pool_mult", at)

                block = at.enter_context(nc.Block())

                @block.sync
                def _(sp):
                    sp.dma_start(rw32[:], router_w.rearrange("(c p) e -> p c e", p=P)).then_inc(small_loaded, 16)
                    sp.dma_start(rb[:], router_b.partition_broadcast(P)).then_inc(small_loaded, 16)

                    def step(item):
                        if m := item(0):
                            if m.after(2):
                                sp.wait_ge(x1_done, m.k - 1)
                            r, rows = slice(0, m.rows), ds(m.k * P, m.rows)
                            sp.dma_start(h_in[m.i][r, :], hpre[rows, :]).then_inc(loaded[m.i], 16)
                            sp.dma_start(x_in[m.i][r, :], x[rows, :]).then_inc(loaded[m.i], 16)
                        if m := item(2):
                            sp.wait_ge(norm.lo_done, m.k + 1)
                            r, rows = slice(0, m.rows), ds(m.k * P, m.rows)
                            sp.dma_start(x1_d[rows, :], norm.x[m.i][r, :]).then_inc(stored[m.i], 16)
                            sp.dma_start(z_d[rows, :], norm.hl[m.i][r, :]).then_inc(stored[m.i], 16)

                    pipeline(sp, NB, 2, step)
                    for i in range(2):
                        sp.wait_ge(stored[i], 32 * ((NB + 1 - i) // 2))

                @block.gpsimd
                def _(pool):
                    nc.gpsimd.memset(logits[:], 0.0).then_inc(consts, 1)
                    nc.gpsimd.memset(before[:], 1.0).then_inc(zeroed, 1)
                    nc.gpsimd.memset(ones[:], 1.0)
                    pool.wait_ge(zeroed, 1)
                    nc.gpsimd.affine_select(out=before[:], in_=before[:], compare_op=ALU.is_gt, fill=0.0,
                                            base=0, pattern=[[1, P]], channel_multiplier=-1)
                    nc.gpsimd.iota(less[:], [[-1, NE]], base=NE, channel_multiplier=0,
                                   allow_small_or_imprecise_dtypes=True)
                    nc.gpsimd.iota(slot_iota[:], [[1, P]], base=0, channel_multiplier=0,
                                   allow_small_or_imprecise_dtypes=True).then_inc(consts, 1)

                    def step(item):
                        if m := item(0):
                            r = slice(0, m.rows)
                            pool.wait_ge(loaded[m.i], m.loads * 2)
                            if m.after(2):
                                pool.wait_ge(x1_done, m.k - 1)
                            nc.gpsimd.tensor_tensor(act_in[m.i][r, :], h_in[m.i][r, :], bn_scale[r, :], ALU.mult)\
                              .then_inc(pool_mult, 1)
                            pool.wait_ge(pool_mult, m.k + 1)
                            nc.gpsimd.tensor_tensor(act_in[m.i][r, :], act_in[m.i][r, :], bn_shift[r, :], ALU.add)\
                              .then_inc(bn_done, 1)

                    pipeline(pool, NB, 0, step)
                    pool.wait_ge(hots_done, 1)
                    for hot_ in (hot1, hot2):
                        nc.gpsimd.affine_select(out=hot_[:, NB - 1, :], in_=hot_[:, NB - 1, :], compare_op=ALU.is_gt,
                                                fill=0.0, base=LAST, pattern=[[0, NE]], channel_multiplier=-1)\
                          .then_inc(hot_masked, 1)

                @block.tensor
                def _(pe):
                    pe.wait_ge(consts, 2)
                    pe.wait_ge(rw_split, 1)

                    def step(item):
                        if m := item(0):
                            pe.wait_ge(norm.lo_done, m.k + 1)
                            pe.wait_ge(norm.hi_done, m.k + 1)
                            if m.after(1):
                                pe.wait_ge(z_t_done, m.k)
                            for part in range(2):
                                for c in range(KC):
                                    last = nc.tensor.transpose(
                                        z_ps[:, part, c, 0:m.rows],
                                        norm.hl[m.i][0:m.rows, part * D + c * P:part * D + (c + 1) * P],
                                        ident16[0:m.rows, 0:m.rows])
                            last.then_inc(turned, 1)
                            pe.wait_ge(z_t_done, m.k + 1)
                            if m.after(1):
                                pe.wait_ge(logits_done, m.k)
                            split_product(l_ps[0:m.rows, 0:NE], lambda c, part: z_t[:, part, c, 0:m.rows],
                                          lambda c, part: rw[:, part, c, :], KC).then_inc(routed, 1)

                    pipeline(pe, NB, 0, step)
                    pe.wait_ge(hot_sent, 1)
                    flat = hot[:].rearrange("p b e -> p (b e)")
                    nc.tensor.matmul(in_ps[:, 0:NB * NE], before[:], flat, start=True, stop=True)
                    nc.tensor.matmul(all_ps[:, 0:NB * NE], ones[:], flat, start=True, stop=True).then_inc(ranked, 1)

                @block.scalar
                def _(act):
                    act.wait_ge(consts, 2)

                    def step(item):
                        if m := item(0):
                            norm.std(act, m)
                            if m.after(2):
                                act.wait_ge(stored[m.i], m.loads * 2 - 32)
                                act.wait_ge(turned, m.k - 1)
                            norm.hi(act, m)
                        if m := item(1):
                            act.wait_ge(turned, m.k + 1)
                            if m.after(1):
                                act.wait_ge(routed, m.k)
                            nc.scalar.activation(z_t[:, :, :, 0:m.rows], z_ps[:, :, :, 0:m.rows], ACT.Copy)\
                              .then_inc(z_t_done, 1)
                        if m := item(2):
                            act.wait_ge(routed, m.k + 1)
                            nc.scalar.activation(logits[0:m.rows, m.k, :], l_ps[0:m.rows, 0:NE], ACT.Copy)\
                              .then_inc(logits_done, 1)

                    pipeline(act, NB, 2, step)
                    act.wait_ge(shifted, 1)
                    nc.scalar.activation(t1[:], t1[:], ACT.Exp)
                    nc.scalar.activation(top2[:], top2[:], ACT.Exp).then_inc(exp_done, 1)

                @block.vector
                def _(dve):
                    V = nc.vector
                    dve.wait_ge(small_loaded, 32)
                    V.tensor_scalar(rw[:, 0], rw32[:], WS, None, ALU.mult)
                    dve.drain()
                    V.scalar_tensor_tensor(rw[:, 1], rw32[:], WS, rw[:, 0], ALU.mult, ALU.subtract)\
                     .then_inc(rw_split, 1)

                    def step(item):
                        if m := item(0):
                            r = slice(0, m.rows)
                            dve.wait_ge(bn_done, m.k + 1)
                            if m.after(2):
                                dve.wait_ge(stored[m.i], m.loads * 2 - 32)
                            V.scalar_tensor_tensor(norm.x[m.i][r, :], act_in[m.i][r, :], 0.0, x_in[m.i][r, :],
                                                   ALU.max, ALU.add).then_inc(x1_done, 1)
                            dve.drain()
                            norm.var(dve, m)
                        if m := item(1):
                            norm.lo(dve, m)
                        if m := item(0):
                            norm.scale(dve, m)

                    pipeline(dve, NB, 1, step)

                    dve.wait_ge(logits_done, NB)
                    wide = lambda t: t[:].unsqueeze(2).to_broadcast([P, NB, NE])
                    per_expert = lambda t: t[:].unsqueeze(1).to_broadcast([P, NB, NE])
                    V.scalar_tensor_tensor(logits[:], logits[:], 1.0 / WS, per_expert(rb), ALU.mult, ALU.add)
                    dve.drain()
                    V.tensor_reduce(top1[:], logits[:], AX.X, ALU.max)
                    dve.drain()
                    V.tensor_tensor(t1[:], logits[:], wide(top1), ALU.subtract)
                    V.tensor_tensor(hot1[:], logits[:], wide(top1), ALU.is_equal)
                    dve.drain()
                    V.tensor_tensor(t2[:], hot1[:], per_expert(less), ALU.mult)
                    dve.drain()
                    V.tensor_reduce(mx[:], t2[:], AX.X, ALU.max)
                    dve.drain()
                    V.tensor_tensor(hot1[:], t2[:], wide(mx), ALU.is_equal)
                    dve.drain()
                    V.scalar_tensor_tensor(logits[:], hot1[:], -1e30, logits[:], ALU.mult, ALU.add)
                    dve.drain()
                    V.tensor_reduce(top2[:], logits[:], AX.X, ALU.max)
                    dve.drain()
                    V.tensor_tensor(hot2[:], logits[:], wide(top2), ALU.is_equal)
                    dve.drain()
                    V.tensor_tensor(t2[:], hot2[:], per_expert(less), ALU.mult)
                    V.tensor_tensor(top2[:], top2[:], top1[:], ALU.subtract).then_inc(shifted, 1)
                    dve.drain()
                    V.tensor_reduce(mx[:], t2[:], AX.X, ALU.max)
                    dve.drain()
                    V.tensor_tensor(hot2[:], t2[:], wide(mx), ALU.is_equal).then_inc(hots_done, 1)
                    dve.wait_ge(exp_done, 1)
                    V.tensor_reduce(den[:], t1[:], AX.X, ALU.add)
                    dve.drain()
                    V.reciprocal(top1[:], den[:])
                    dve.drain()
                    V.tensor_tensor(top2[:], top2[:], top1[:], ALU.mult)
                    dve.drain()
                    V.scalar_tensor_tensor(den[:], top1[:], 1e-9, top2[:], ALU.add, ALU.add)
                    dve.drain()
                    V.reciprocal(mx[:], den[:])
                    dve.drain()
                    V.tensor_tensor(share[:, :, 0], top1[:], mx[:], ALU.mult)
                    V.tensor_tensor(share[:, :, 1], top2[:], mx[:], ALU.mult)
                    dve.wait_ge(hot_masked, 2)
                    V.tensor_tensor(hot[:], hot1[:], hot2[:], ALU.add).then_inc(hot_sent, 1)
                    dve.wait_ge(ranked, 1)
                    blocks = lambda t: t[:, 0:NB * NE].rearrange("p (b e) -> p b e", e=NE)
                    V.tensor_copy(run1[:], blocks(all_ps))
                    dve.drain()
                    a, b, s = run1, run2, 1
                    while s < NB:
                        V.tensor_copy(b[:, 0:s, :], a[:, 0:s, :])
                        V.tensor_tensor(b[:, s:NB, :], a[:, s:NB, :], a[:, 0:NB - s, :], ALU.add)
                        dve.drain()
                        a, b, s = b, a, 2 * s
                    V.tensor_scalar(tiles_i[:], a[:, NB - 1, :], float(P - 1), None, ALU.add)
                    dve.drain()
                    V.tensor_scalar(tiles_i[:], tiles_i[:], P.bit_length() - 1, None, ALU.logical_shift_right)
                    dve.drain()
                    V.tensor_copy(tiles[:], tiles_i[:])
                    V.tensor_copy(end1[:], tiles_i[:])
                    dve.drain()
                    u, v, s = end1, end2, 1
                    while s < NE:
                        V.tensor_copy(v[:, 0:s], u[:, 0:s])
                        V.tensor_tensor(v[:, s:NE], u[:, s:NE], u[:, 0:NE - s], ALU.add)
                        dve.drain()
                        u, v, s = v, u, 2 * s
                    V.tensor_tensor(v[:], u[:], tiles[:], ALU.subtract)
                    dve.drain()
                    V.tensor_scalar(tiles[:], v[:], float(P), None, ALU.mult)
                    dve.drain()
                    V.tensor_tensor(base[:], a[:], blocks(all_ps), ALU.subtract)
                    dve.drain()
                    V.tensor_tensor(base[:], base[:], blocks(in_ps), ALU.add)
                    dve.drain()
                    V.tensor_tensor(base[:], base[:], per_expert(tiles), ALU.add)
                    dve.drain()
                    V.tensor_tensor(t1[:], base[:], hot1[:], ALU.mult)
                    V.tensor_tensor(t2[:], base[:], hot2[:], ALU.mult)
                    dve.drain()
                    V.tensor_reduce(top1[:], t1[:], AX.X, ALU.add)
                    V.tensor_reduce(top2[:], t2[:], AX.X, ALU.add)
                    dve.drain()
                    V.tensor_copy(place[:, :, 0], top1[:])
                    V.tensor_copy(place[:, :, 1], top2[:])
                    V.memset(slot_of[:], 0.0)
                    dve.drain()
                    for e in range(NE - 1):
                        V.scalar_tensor_tensor(slot_of[:], slot_iota[:], u[0:1, e:e + 1], slot_of[:],
                                               ALU.is_ge, ALU.add)
                        dve.drain()
                    V.tensor_tensor(pad_row[:], tiles[0:1, :], a[0:1, NB - 1, :], ALU.add)
                    dve.drain()
                    V.tensor_copy(slots[:, 0:NS], slot_of[:, 0:NS])
                    V.tensor_copy(slots[:, NS:NS + NE], pad_row[:])

        def dispatch():
            at = ExitStack()
            with at:
                z_in = [sb(f"z_in{i}", [P, 2 * D], f16, at) for i in range(2)]
                to = [sb(f"to{i}", [P, 2], i32, at) for i in range(2)]
                zero_rows = sb("zero_rows", [P, 2 * D], f16, at)
                z_loaded = [sem(f"z_loaded{i}", at) for i in range(2)]
                to_set = sem("to_set", at)
                to_seen = sem("to_seen", at)
                scattered = [sem(f"scattered{i}", at) for i in range(2)]
                zeros_set = sem("zeros_set", at)
                pads_stored = sem("pads_stored", at)
                block = at.enter_context(nc.Block())

                @block.sync
                def _(sp):
                    sp.wait_ge(zeros_set, 1)
                    for t in range(FULL, NS + 1):
                        sp.dma_start(items_in[t * P:(t + 1) * P, :], zero_rows[:]).then_inc(pads_stored, 16)
                    sp.wait_ge(pads_stored, 16 * (NS + 1 - FULL))
                    for e in range(NE):
                        row = sp.value_load(slots[0:1, NS + e:NS + e + 1], min_val=0, max_val=NS * P)
                        sp.dma_start(items_in[ds(row, P), :], zero_rows[:]).then_inc(pads_stored, 16)
                        sp.wait_ge(pads_stored, 16 * (NS + 2 - FULL + e))

                    def step(item):
                        if m := item(0):
                            if m.after(2):
                                sp.wait_ge(scattered[m.i], m.loads * 2 - 32)
                            sp.dma_start(z_in[m.i][0:m.rows, :], z_d[ds(m.k * P, m.rows), :])\
                              .then_inc(z_loaded[m.i], 16)

                    pipeline(sp, NB, 0, step)

                @block.vector
                def _(dve):
                    nc.vector.memset(zero_rows[:], 0.0).then_inc(zeros_set, 1)

                    def step(item):
                        if m := item(0):
                            if m.after(2):
                                dve.wait_ge(scattered[m.i], m.loads * 2 - 32)
                            nc.vector.tensor_copy(to[m.i][:], place[:, m.k, :]).then_inc(to_set, 1)

                    pipeline(dve, NB, 0, step)

                @block.gpsimd
                def _(pool):
                    pool.wait_ge(pads_stored, 16 * (NS + 1 - FULL + NE))

                    def step(item):
                        if m := item(0):
                            pool.wait_ge(z_loaded[m.i], m.loads)
                            pool.wait_ge(to_set, m.k + 1)
                            pool.sem_inc(to_seen, 1)
                            for n in range(2):
                                pool.indirect_dma_start(
                                    out=items_in, in_=z_in[m.i][0:m.rows, :], in_offset=None,
                                    out_offset=bass.IndirectOffsetOnAxis(ap=to[m.i][0:m.rows, n:n + 1], axis=0),
                                ).then_inc(scattered[m.i], 16)

                    pipeline(pool, NB, 0, step)
                    for i in range(2):
                        pool.wait_ge(scattered[i], 32 * ((NB + 1 - i) // 2))

        def experts():
            at = ExitStack()
            FC = FE // P
            with at:
                w1_sb = sb("w1_sb", [P, 2, KC, NE, FE], f16, at)
                w2_sb = sb("w2_sb", [P, 2, FC, NE, D], f16, at)
                b1_sb, b2_sb = sb("b1_sb", [P, NE, FE], f32, at), sb("b2_sb", [P, NE, D], f32, at)
                w_in = [sb(f"w_in{i}", [P, KC * FE], f32, at) for i in range(2)]
                item_in = [sb(f"item_in{i}", [P, 2 * D], f16, at) for i in range(2)]
                it_t = [sb(f"it_t{i}", [P, 2, KC, P], f16, at) for i in range(2)]
                u_sb = [sb(f"u_sb{i}", [P, FE], f32, at) for i in range(2)]
                g_sb = [sb(f"g_sb{i}", [P, FE], f32, at) for i in range(2)]
                g_hl = [sb(f"g_hl{i}", [P, 2, FE], f16, at) for i in range(2)]
                g_t = [sb(f"g_t{i}", [P, 2, FC, P], f16, at) for i in range(2)]
                y_sb = [sb(f"y_sb{i}", [P, D], f32, at) for i in range(2)]
                it_ps = pb("it_ps", [P, 2, KC, P], f16, at)
                u_ps = [pb(f"u_ps{i}", [P, 512], f32, at) for i in range(2)]
                g_ps = pb("g_ps", [P, 2, FC, 2 * P], f16, at)
                y_ps = [pb(f"y_ps{i}", [P, D], f32, at) for i in range(2)]

                w_loaded = [sem(f"ew_loaded{i}", at) for i in range(2)]
                b_loaded = sem("eb_loaded", at)
                w_hi = sem("ew_hi", at)
                w_lo = sem("ew_lo", at)
                it_loaded = [sem(f"it_loaded{i}", at) for i in range(2)]
                it_turned = sem("it_turned", at)
                it_t_done = sem("it_t_done", at)
                up_done = sem("up_done", at)
                u_done = sem("u_done", at)
                g_done = sem("g_done", at)
                g_split = sem("g_split", at)
                g_turned = sem("g_turned", at)
                g_t_done = sem("g_t_done", at)
                down_done = sem("down_done", at)
                y_done = sem("y_done", at)
                y_stored = [sem(f"y_stored{i}", at) for i in range(2)]
                block = at.enter_context(nc.Block())
                parts = [(w, e) for e in range(NE) for w in range(2)]

                def w_view(w, e, part):
                    t, chunks = (w1_sb, KC) if w == 0 else (w2_sb, FC)
                    return t[:, part, :, e, :]

                def w_raw(n, w):
                    return w_in[n % 2][:].rearrange("p (c f) -> p c f", c=KC if w == 0 else FC)

                @block.sync
                def _(sp):
                    sp.dma_start(b1_sb[:], b1.partition_broadcast(P)).then_inc(b_loaded, 16)
                    sp.dma_start(b2_sb[:], b2.partition_broadcast(P)).then_inc(b_loaded, 16)
                    for n, (w, e) in enumerate(parts):
                        if n >= 2:
                            sp.wait_ge(w_hi, n - 1)
                            sp.wait_ge(w_lo, n - 1)
                        sp.dma_start(w_raw(n, w), (w1 if w == 0 else w2)[e].rearrange("(c p) f -> p c f", p=P))\
                          .then_inc(w_loaded[n % 2], 16)

                    def step(item):
                        if m := item(0):
                            if m.after(2):
                                sp.wait_ge(it_turned, m.k - 1)
                            sp.dma_start(item_in[m.i][:], items_in[ds(m.k * P, P), :]).then_inc(it_loaded[m.i], 16)
                        if m := item(4):
                            sp.wait_ge(y_done, m.k + 1)
                            sp.dma_start(items_out[ds(m.k * P, P), :], y_sb[m.i][:]).then_inc(y_stored[m.i], 16)

                    pipeline(sp, NS, 4, step)
                    for i in range(2):
                        sp.wait_ge(y_stored[i], 16 * ((NS + 1 - i) // 2))

                @block.tensor
                def _(pe):
                    def expert(k):
                        return pe.value_load(slots[0:1, ds(k, 1)], min_val=0, max_val=NE - 1)

                    def step(item):
                        if m := item(0):
                            pe.wait_ge(it_loaded[m.i], m.loads)
                            if m.after(1):
                                pe.wait_ge(it_t_done, m.k)
                            for part in range(2):
                                for c in range(KC):
                                    last = nc.tensor.transpose(
                                        it_ps[:, part, c, :],
                                        item_in[m.i][:, part * D + c * P:part * D + (c + 1) * P], ident16[:])
                            last.then_inc(it_turned, 1)
                        if m := item(1):
                            if m.fixed and m.k == 0:
                                pe.wait_ge(w_hi, 2 * NE)
                                pe.wait_ge(w_lo, 2 * NE)
                            e = expert(m.k)
                            pe.wait_ge(it_t_done, m.k + 1)
                            if m.after(2):
                                pe.wait_ge(u_done, m.k - 1)
                            split_product(u_ps[m.i][:, 0:FE], lambda c, part: it_t[m.i][:, part, c, :],
                                          lambda c, part: w1_sb[:, part, c, ds(e, 1), :], KC).then_inc(up_done, 1)
                        if m := item(2):
                            pe.wait_ge(g_split, m.k + 1)
                            if m.after(1):
                                pe.wait_ge(g_t_done, m.k)
                            for part in range(2):
                                for c in range(FC):
                                    last = nc.tensor.transpose(g_ps[:, part, c, 0:P],
                                                               g_hl[m.i][:, part, c * P:(c + 1) * P], ident16[:])
                            last.then_inc(g_turned, 1)
                        if m := item(3):
                            e = expert(m.k)
                            pe.wait_ge(g_t_done, m.k + 1)
                            if m.after(2):
                                pe.wait_ge(y_done, m.k - 1)
                            split_product(y_ps[m.i][:], lambda c, part: g_t[m.i][:, part, c, :],
                                          lambda c, part: w2_sb[:, part, c, ds(e, 1), :], FC).then_inc(down_done, 1)

                    pipeline(pe, NS, 4, step)

                @block.scalar
                def _(act):
                    for n, (w, e) in enumerate(parts):
                        act.wait_ge(w_loaded[n % 2], 16 * (n // 2 + 1))
                        nc.scalar.activation(w_view(w, e, 0), w_raw(n, w), ACT.Copy, scale=WS).then_inc(w_hi, 1)

                    def step(item):
                        if m := item(0):
                            act.wait_ge(it_turned, m.k + 1)
                            if m.after(2):
                                act.wait_ge(up_done, m.k - 1)
                            nc.scalar.activation(it_t[m.i][:], it_ps[:], ACT.Copy).then_inc(it_t_done, 1)
                        if m := item(1):
                            act.wait_ge(u_done, m.k + 1)
                            if m.after(2):
                                act.wait_ge(g_split, m.k - 1)
                            nc.scalar.activation(g_sb[m.i][:], u_sb[m.i][:], ACT.Gelu).then_inc(g_done, 1)

                    pipeline(act, NS, 4, step)

                @block.vector
                def _(dve):
                    for n, (w, e) in enumerate(parts):
                        dve.wait_ge(w_hi, n + 1)
                        nc.vector.scalar_tensor_tensor(w_view(w, e, 1), w_raw(n, w), WS, w_view(w, e, 0),
                                                       ALU.mult, ALU.subtract).then_inc(w_lo, 1)
                    dve.wait_ge(b_loaded, 32)

                    def expert(k):
                        return dve.value_load(slots[0:1, ds(k, 1)], min_val=0, max_val=NE - 1)

                    def step(item):
                        if m := item(1):
                            e = expert(m.k)
                            dve.wait_ge(up_done, m.k + 1)
                            if m.after(2):
                                dve.wait_ge(g_done, m.k - 1)
                            nc.vector.scalar_tensor_tensor(u_sb[m.i][:], u_ps[m.i][:, 0:FE], 1.0 / WS,
                                                           b1_sb[:, ds(e, 1), :].rearrange("p a f -> p (a f)"),
                                                           ALU.mult, ALU.add).then_inc(u_done, 1)
                        if m := item(3):
                            dve.wait_ge(g_turned, m.k + 1)
                            nc.vector.tensor_copy(g_t[m.i][:], g_ps[:, :, :, 0:P]).then_inc(g_t_done, 1)
                        if m := item(4):
                            e = expert(m.k)
                            dve.wait_ge(down_done, m.k + 1)
                            if m.after(2):
                                dve.wait_ge(y_stored[m.i], m.loads - 16)
                            nc.vector.scalar_tensor_tensor(y_sb[m.i][:], y_ps[m.i][:], 1.0 / WS,
                                                           b2_sb[:, ds(e, 1), :].rearrange("p a f -> p (a f)"),
                                                           ALU.mult, ALU.add).then_inc(y_done, 1)
                        if m := item(1):
                            dve.wait_ge(g_done, m.k + 1)
                            if m.after(2):
                                dve.wait_ge(g_turned, m.k - 1)
                            nc.vector.tensor_copy(g_hl[m.i][:, 0, :], g_sb[m.i][:])
                            dve.drain()
                            nc.vector.tensor_tensor(g_hl[m.i][:, 1, :], g_sb[m.i][:], g_hl[m.i][:, 0, :],
                                                    ALU.subtract).then_inc(g_split, 1)

                    pipeline(dve, NS, 4, step)

        def combine():
            at = ExitStack()
            with at:
                norm = Norm(at, "n2")
                x1_in = [sb(f"x1_in{i}", [P, D], f32, at) for i in range(2)]
                y_in = [[sb(f"y_in{i}_{n}", [P, D], f32, at) for n in range(2)] for i in range(2)]
                of = [sb(f"of{i}", [P, 2], i32, at) for i in range(2)]
                x1_loaded = [sem(f"x1_loaded{i}", at) for i in range(2)]
                of_set = sem("of_set", at)
                of_seen = sem("of_seen", at)
                y_gathered = [sem(f"y_gathered{i}", at) for i in range(2)]
                x2_done = sem("x2_done", at)
                stored = [sem(f"x2_stored{i}", at) for i in range(2)]
                block = at.enter_context(nc.Block())

                @block.sync
                def _(sp):
                    def step(item):
                        if m := item(0):
                            if m.after(2):
                                sp.wait_ge(x2_done, m.k - 1)
                            sp.dma_start(x1_in[m.i][0:m.rows, :], x1_d[ds(m.k * P, m.rows), :])\
                              .then_inc(x1_loaded[m.i], 16)
                        if m := item(2):
                            sp.wait_ge(norm.lo_done, m.k + 1)
                            r, rows = slice(0, m.rows), ds(m.k * P, m.rows)
                            sp.dma_start(x2_d[rows, :], norm.x[m.i][r, :]).then_inc(stored[m.i], 16)
                            sp.dma_start(xn3[rows, :], norm.hl[m.i][r, :]).then_inc(stored[m.i], 16)

                    pipeline(sp, NB, 2, step)
                    for i in range(2):
                        sp.wait_ge(stored[i], 32 * ((NB + 1 - i) // 2))

                @block.gpsimd
                def _(pool):
                    def step(item):
                        if m := item(0):
                            if m.after(2):
                                pool.wait_ge(x2_done, m.k - 1)
                            pool.wait_ge(of_set, m.k + 1)
                            pool.sem_inc(of_seen, 1)
                            for n in range(2):
                                pool.indirect_dma_start(
                                    out=y_in[m.i][n][0:m.rows, :], out_offset=None, in_=items_out,
                                    in_offset=bass.IndirectOffsetOnAxis(ap=of[m.i][0:m.rows, n:n + 1], axis=0),
                                ).then_inc(y_gathered[m.i], 16)

                    pipeline(pool, NB, 0, step)

                @block.scalar
                def _(act):
                    def step(item):
                        if m := item(0):
                            norm.std(act, m)
                            if m.after(2):
                                act.wait_ge(stored[m.i], m.loads * 2 - 32)
                            norm.hi(act, m)

                    pipeline(act, NB, 0, step)

                @block.vector
                def _(dve):
                    def point(m):
                        nc.vector.tensor_copy(of[m.i][:], place[:, m.k, :]).then_inc(of_set, 1)

                    def step(item):
                        if m := item(0):
                            point(m)
                        if m := item(1):
                            r = slice(0, m.rows)
                            dve.wait_ge(y_gathered[m.i], m.loads * 2)
                            dve.wait_ge(x1_loaded[m.i], m.loads)
                            if m.after(2):
                                dve.wait_ge(stored[m.i], m.loads * 2 - 32)
                            nc.vector.scalar_tensor_tensor(x1_in[m.i][r, :], y_in[m.i][0][r, :],
                                                           share[r, m.k, 0:1], x1_in[m.i][r, :],
                                                           ALU.mult, ALU.add)
                            dve.drain()
                            nc.vector.scalar_tensor_tensor(norm.x[m.i][r, :], y_in[m.i][1][r, :],
                                                           share[r, m.k, 1:2], x1_in[m.i][r, :],
                                                           ALU.mult, ALU.add).then_inc(x2_done, 1)
                            dve.drain()
                            norm.var(dve, m)
                        if m := item(2):
                            norm.lo(dve, m)
                        if m := item(1):
                            norm.scale(dve, m)

                    pipeline(dve, NB, 2, step)

        def layer1():
            at = ExitStack()
            with at:
                w_gu = [sb(f"w_gu{n}", [P, 2, KC, FF], f16, at) for n in range(2)]
                w_dn = sb("w_dn", [P, 2, FT, D], f16, at)
                w_cv = sb("w_cv", [P, 2, KC, D], f16, at)
                ternary(w_gu, w_dn, w_cv)
                if upto >= 5:
                    graph_and_gated(w_gu, w_dn, w_cv)

        def ternary(w_gu, w_dn, w_cv):
            at = ExitStack()
            with at:
                QC = KC * FT
                raw = [sb(f"raw{n}", [P, QC, P], f32, at) for n in range(3)]
                raw_cv = sb("raw_cv", [P, KC, D], f32, at)
                size = sb("size", [P, QC], f32, at)
                inv_size = sb("inv_size", [P, QC], f32, at)
                t_ps = [pb(f"t_ps{i}", [P, KC, P], f32, at) for i in range(2)]
                raw_loaded = [sem(f"raw_loaded{n}", at) for n in range(3)]
                cv_loaded = sem("cv_loaded", at)
                rounded = sem("rounded", at)
                cv_hi = sem("cv_hi", at)
                t_turned = sem("t_turned", at)
                t_hi = sem("t_hi", at)
                t_lo = sem("t_lo", at)
                block = at.enter_context(nc.Block())
                units = [(n, f) for n in range(3) for f in range(FT)]

                def to(n, f, part):
                    if n < 2:
                        return w_gu[n][:, part, :, f * P:(f + 1) * P]
                    return w_dn[:, part, f, :].rearrange("p (c o) -> p c o", c=KC)

                @block.sync
                def _(sp):
                    for n, w in enumerate((w_gate, w_up)):
                        sp.dma_start(raw[n][:].rearrange("p (f c) k -> p f (c k)", f=FT),
                                     w.rearrange("(f p) k -> p f k", p=P)).then_inc(raw_loaded[n], 16)
                    sp.dma_start(raw[2][:].rearrange("p (c f) k -> p c (f k)", c=KC),
                                 w_down.rearrange("(c p) k -> p c k", p=P)).then_inc(raw_loaded[2], 16)
                    sp.dma_start(raw_cv[:], W_g.rearrange("(c p) o -> p c o", p=P)).then_inc(cv_loaded, 16)

                @block.vector
                def _(dve):
                    V = nc.vector
                    MAGIC = 1.5 * 2.0 ** 23
                    for n in range(3):
                        dve.wait_ge(raw_loaded[n], 16)
                        V.tensor_reduce(size[:], raw[n][:], AX.X, ALU.add, apply_absolute_value=True)
                        dve.drain()
                        V.tensor_scalar(size[:], size[:], 1.0 / P, EPS, ALU.mult, ALU.add)
                        dve.drain()
                        V.reciprocal(inv_size[:], size[:])
                        dve.drain()
                        wide = lambda t: t[:].unsqueeze(2).to_broadcast([P, QC, P])
                        V.tensor_tensor(raw[n][:], raw[n][:], wide(inv_size), ALU.mult)
                        dve.drain()
                        V.tensor_scalar(raw[n][:], raw[n][:], -1.0, 1.0, ALU.max, ALU.min)
                        dve.drain()
                        V.tensor_scalar(raw[n][:], raw[n][:], MAGIC, MAGIC, ALU.add, ALU.subtract)
                        dve.drain()
                        V.tensor_tensor(raw[n][:], raw[n][:], wide(size), ALU.mult).then_inc(rounded, 1)
                        dve.drain()
                    dve.wait_ge(cv_hi, 1)
                    V.scalar_tensor_tensor(w_cv[:, 1], raw_cv[:], WS, w_cv[:, 0], ALU.mult, ALU.subtract)
                    for u, (n, f) in enumerate(units):
                        dve.wait_ge(t_hi, u + 1)
                        V.scalar_tensor_tensor(to(n, f, 1), t_ps[u % 2][:], WS, to(n, f, 0), ALU.mult, ALU.subtract)\
                         .then_inc(t_lo, 1)

                @block.tensor
                def _(pe):
                    for u, (n, f) in enumerate(units):
                        pe.wait_ge(rounded, n + 1)
                        if u >= 2:
                            pe.wait_ge(t_hi, u - 1)
                            pe.wait_ge(t_lo, u - 1)
                        for c in range(KC):
                            group = f * KC + c if n < 2 else c * FT + f
                            last = nc.tensor.transpose(t_ps[u % 2][:, c, :], raw[n][:, group, :], ident32[:])
                        last.then_inc(t_turned, 1)

                @block.scalar
                def _(act):
                    act.wait_ge(cv_loaded, 16)
                    nc.scalar.activation(w_cv[:, 0], raw_cv[:], ACT.Copy, scale=WS).then_inc(cv_hi, 1)
                    for u, (n, f) in enumerate(units):
                        act.wait_ge(t_turned, u + 1)
                        nc.scalar.activation(to(n, f, 0), t_ps[u % 2][:], ACT.Copy, scale=WS).then_inc(t_hi, 1)

        def graph_and_gated(w_gu, w_dn, w_cv):
            at = ExitStack()
            with at:
                R = 4
                W = R * P
                NGR = (NB - 1) // R
                edges = Edges(at, True)
                acc_hl = sb("acc_hl", [P, 2, D], f16, at)
                acc_t = sb("acc_t", [P, 2, KC, P], f16, at)
                x2_in = sb("x2_in", [P, D], f32, at)
                conv = sb("conv", [P, D], f32, at)
                x3 = [[sb(f"x3_{p}_{r}", [P, D], f32, at) for r in range(R)] for p in range(2)]
                norm = Norm(at, "n3", 1, [None])
                z_t = [sb(f"z_t3_{p}", [P, 2, KC, W], f16, at) for p in range(2)]
                silu = [sb(f"silu{i}", [P, W], f32, at) for i in range(2)]
                prod = [sb(f"prod{i}", [P, W], f32, at) for i in range(2)]
                h_t = sb("h_t", [P, FT, 2, W], f16, at)
                acc = pb("acc3", [P, D], f32, at)
                turn_ps = pb("turn_ps", [P, 2, KC, P], f16, at)
                conv_ps = pb("conv_ps", [P, D], f32, at)
                gate_ps = [pb(f"gate_ps{i}", [P, W], f32, at) for i in range(2)]
                up_ps = [pb(f"up_ps{i}", [P, W], f32, at) for i in range(2)]
                down_ps = pb("down_ps", [P, D], f32, at)

                acc_ready = sem("acc_ready3", at)
                acc_hi_done = sem("acc_hi_done", at)
                acc_lo_done = sem("acc_lo_done", at)
                acc_turned = sem("acc_turned", at)
                acc_t_done = sem("acc_t_done", at)
                projected = sem("projected", at)
                conv_done = sem("conv_done", at)
                x2_loaded = sem("x2_loaded", at)
                x3_done = sem("x3_done", at)
                z_turned = sem("z_turned", at)
                z_t_done = sem("z_t_done3", at)
                up_ready = sem("up_ready", at)
                silu_done = sem("silu_done", at)
                prod_done = sem("prod_done", at)
                h_hi_done = sem("h_hi_done", at)
                h_lo_done = sem("h_lo_done", at)
                down_ready = sem("down_ready", at)
                out_done = sem("out_done", at)
                out_stored = [[sem(f"out_stored{p}_{r}", at) for r in range(R)] for p in range(2)]
                block = at.enter_context(nc.Block())

                class Step:

                    def __init__(self, g, p, r):
                        self.g, self.p, self.r = g, p, r
                        self.b = g * R + r
                        self.first = isinstance(g, int) and g == 0 and r == 0
                        self.last = isinstance(g, int) and g == NGR
                        self.rows = LAST if self.last else P

                class Gated:

                    def __init__(self, g, p):
                        self.g, self.p = g, p
                        self.last = isinstance(g, int) and g == NGR
                        self.n = 1 if self.last else R
                        self.width = self.n * P
                        self.first = isinstance(g, int) and g == 0
                        self.units = [("up", f) for f in range(FT)] + [("down", r) for r in range(self.n)]

                def program(step, rest):
                    cuts = [(0, 2, 3, 4), (4, 6, 7, 8), (8, 10, 11, 12), (12, 13, 14, 15)]

                    def group(g, p, before):
                        for r in range(R):
                            gated = Gated(g - 1, 1 - p) if before else None
                            c = cuts[r]
                            step(Step(g, p, r), gated,
                                 [gated.units[c[n]:c[n + 1]] if gated else [] for n in range(3)])

                    group(0, 0, False)
                    group(1, 1, True)
                    group(2, 0, True)
                    with nc_engine[0].Fori(3, NGR - 1, 2) as n:
                        g = n.with_bounds(min_val=3, max_val=NGR - 3)
                        group(g, 1, True)
                        group(g + 1, 0, True)
                    group(NGR - 1, 1, True)
                    gated = Gated(NGR - 1, 1)
                    step(Step(NGR, 0, 0), gated, [gated.units[0:6], gated.units[6:11], gated.units[11:]])
                    rest(Gated(NGR, 0))

                nc_engine = [None]
                assert NGR % 2 == 0 and NB - 1 == NGR * R

                def waits_unit(t, f):
                    return f - 2 if f >= 2 else -1 - f

                @block.gpsimd
                def _(pool):
                    edges.gather(pool, 0, xn3[0:N, :])
                    with pool.Fori(1, NB) as b:
                        edges.gather(pool, b, xn3[0:N, :])

                @block.sync
                def _(sp):
                    edges.load(sp, 0)
                    with sp.Fori(1, NB) as b:
                        edges.load(sp, b)

                @block.tensor
                def _(pe):
                    pe.sem_inc(edges.summed, 2)
                    nc_engine[0] = pe

                    def unit(t, kind, n):
                        if kind == "up":
                            if n == 0:
                                pe.wait_ge(z_t_done, t.g * R + t.n)
                            if not t.first or n >= 2:
                                pe.wait_ge(prod_done, t.g * FT + (waits_unit(t, n) + 1))
                            for ps, w in ((gate_ps, w_gu[0]), (up_ps, w_gu[1])):
                                last = split_product(ps[n % 2][:, 0:t.width],
                                                     lambda c, part: w[:, part, c, n * P:(n + 1) * P],
                                                     lambda c, part: z_t[t.p][:, part, c, 0:t.width], KC)
                            last.then_inc(up_ready, 1)
                        else:
                            pe.wait_ge(h_lo_done, t.g * FT + FT)
                            if not t.first or n >= 1:
                                pe.wait_ge(out_done, t.g * R + n)
                            split_product(down_ps[:], lambda c, part: h_t[:, c, part, n * P:(n + 1) * P],
                                          lambda c, part: w_dn[:, part, c, :], FT).then_inc(down_ready, 1)

                    def step(s, gated, parts):
                        edges.sum(pe, s.b, acc, None)
                        nc.tensor.matmul(acc[:, 0:1], zeros16[:, 0:P], zeros16[:, 0:1], start=False, stop=True,
                                         skip_group_check=True).then_inc(acc_ready, 1)
                        for u in parts[0]:
                            unit(gated, *u)
                        pe.wait_ge(acc_hi_done, s.b + 1)
                        pe.wait_ge(acc_lo_done, s.b + 1)
                        if not s.first:
                            pe.wait_ge(z_t_done, s.b)
                        for part in range(2):
                            for c in range(KC):
                                last = nc.tensor.transpose(turn_ps[:, part, c, :],
                                                           acc_hl[:, part, c * P:(c + 1) * P], ident16[:])
                        last.then_inc(acc_turned, 1)
                        for u in parts[1]:
                            unit(gated, *u)
                        pe.wait_ge(acc_t_done, s.b + 1)
                        if not s.first:
                            pe.wait_ge(conv_done, s.b)
                        split_product(conv_ps[:], lambda c, part: acc_t[:, part, c, :],
                                      lambda c, part: w_cv[:, part, c, :], KC).then_inc(projected, 1)
                        for u in parts[2]:
                            unit(gated, *u)
                        pe.wait_ge(norm.hi_done, s.b + 1)
                        pe.wait_ge(norm.lo_done, s.b + 1)
                        for part in range(2):
                            for c in range(KC):
                                last = nc.tensor.transpose(turn_ps[:, part, c, :],
                                                           norm.hl[0][:, part * D + c * P:part * D + (c + 1) * P],
                                                           ident16[:])
                        last.then_inc(z_turned, 1)

                    def rest(gated):
                        for u in gated.units:
                            unit(gated, *u)

                    program(step, rest)

                class Whole:

                    def __init__(self, b):
                        self.k, self.i, self.rows = b, 0, P

                @block.scalar
                def _(act):
                    nc_engine[0] = act

                    def unit(t, kind, n):
                        if kind == "up":
                            act.wait_ge(up_ready, t.g * FT + (n + 1))
                            nc.scalar.activation(silu[n % 2][:, 0:t.width], gate_ps[n % 2][:, 0:t.width], ACT.Silu,
                                                 scale=1.0 / WS).then_inc(silu_done, 1)
                            act.wait_ge(prod_done, t.g * FT + (n + 1))
                            nc.scalar.activation(h_t[:, n, 0, 0:t.width], prod[n % 2][:, 0:t.width], ACT.Copy)\
                              .then_inc(h_hi_done, 1)
                        else:
                            act.wait_ge(out_done, t.g * R + (n + 1))
                            rows = LAST if t.last else P
                            act.dma_start(out[ds(t.g * W + n * P, rows), :], x3[t.p][n][0:rows, :])\
                               .then_inc(out_stored[t.p][n], 16)

                    def step(s, gated, parts):
                        if not s.first:
                            act.wait_ge(x3_done, s.b)
                        act.dma_start(x2_in[0:s.rows, :], x2_d[ds(s.b * P, s.rows), :]).then_inc(x2_loaded, 16)
                        act.wait_ge(acc_ready, s.b + 1)
                        nc.scalar.activation(acc_hl[:, 0, :], acc[:], ACT.Copy).then_inc(acc_hi_done, 1)
                        for u in parts[0]:
                            unit(gated, *u)
                        act.wait_ge(acc_turned, s.b + 1)
                        nc.scalar.activation(acc_t[:], turn_ps[:], ACT.Copy).then_inc(acc_t_done, 1)
                        for u in parts[1]:
                            unit(gated, *u)
                        act.wait_ge(projected, s.b + 1)
                        nc.scalar.activation(conv[:], conv_ps[:], ACT.Relu, scale=1.0 / WS).then_inc(conv_done, 1)
                        m = Whole(s.b)
                        norm.std(act, m)
                        norm.hi(act, m)
                        for u in parts[2]:
                            unit(gated, *u)
                        act.wait_ge(z_turned, s.b + 1)
                        nc.scalar.activation(z_t[s.p][:, :, :, s.r * P:(s.r + 1) * P], turn_ps[:], ACT.Copy)\
                          .then_inc(z_t_done, 1)

                    def rest(gated):
                        for u in gated.units:
                            unit(gated, *u)
                        for p in range(2):
                            for r in range(R):
                                stores = NGR // 2 + (p == 0 and r == 0)
                                act.wait_ge(out_stored[p][r], 16 * stores)

                    program(step, rest)

                @block.vector
                def _(dve):
                    nc_engine[0] = dve

                    def unit(t, kind, n):
                        if kind == "up":
                            dve.wait_ge(silu_done, t.g * FT + (n + 1))
                            if not t.first or n >= 2:
                                dve.wait_ge(h_hi_done, t.g * FT + (waits_unit(t, n) + 1))
                            nc.vector.scalar_tensor_tensor(prod[n % 2][:, 0:t.width], up_ps[n % 2][:, 0:t.width],
                                                           1.0 / WS, silu[n % 2][:, 0:t.width], ALU.mult, ALU.mult)\
                              .then_inc(prod_done, 1)
                            dve.wait_ge(h_hi_done, t.g * FT + (n + 1))
                            nc.vector.tensor_tensor(h_t[:, n, 1, 0:t.width], prod[n % 2][:, 0:t.width],
                                                    h_t[:, n, 0, 0:t.width], ALU.subtract).then_inc(h_lo_done, 1)
                        else:
                            dve.wait_ge(down_ready, t.g * R + (n + 1))
                            nc.vector.scalar_tensor_tensor(x3[t.p][n][:], down_ps[:], 1.0 / WS, x3[t.p][n][:],
                                                           ALU.mult, ALU.add).then_inc(out_done, 1)

                    nc.vector.memset(edges.first_node[:], 0.0)
                    dve.drain()
                    edges.masks_first(dve, 0)

                    def step(s, gated, parts):
                        edges.masks_rest(dve, s.b)
                        dve.wait_ge(acc_hi_done, s.b + 1)
                        nc.vector.tensor_tensor(acc_hl[:, 1, :], acc[:], acc_hl[:, 0, :], ALU.subtract)\
                          .then_inc(acc_lo_done, 1)
                        if not s.last:
                            edges.masks_first(dve, s.b + 1)
                        for u in parts[0] + parts[1]:
                            unit(gated, *u)
                        dve.wait_ge(conv_done, s.b + 1)
                        dve.wait_ge(x2_loaded, s.b * 16 + 16)
                        if not isinstance(s.g, int) or s.g >= 2:
                            dve.wait_ge(out_stored[s.p][s.r], (s.g - s.p) * 8)
                        norm.x[0] = x3[s.p][s.r]
                        nc.vector.tensor_tensor(x3[s.p][s.r][:], conv[:], x2_in[:], ALU.add).then_inc(x3_done, 1)
                        dve.drain()
                        m = Whole(s.b)
                        norm.var(dve, m)
                        norm.scale(dve, m)
                        norm.lo(dve, m)
                        for u in parts[2]:
                            unit(gated, *u)

                    def rest(gated):
                        for u in gated.units:
                            unit(gated, *u)

                    program(step, rest)

        layer0()
        if upto >= 3:
            route()
            dispatch()
            experts()
            combine()
        if upto >= 4:
            layer1()


_INS = ['x', 'src', 'dst', 'edge_weight', 'L0_gnn_W_l', 'L0_gnn_b_l', 'L0_gnn_W_r', 'L0_gnn_gamma', 'L0_gnn_beta',
        'L0_ffn_router_w', 'L0_ffn_router_b', 'L0_ffn_w1', 'L0_ffn_b1', 'L0_ffn_w2', 'L0_ffn_b2',
        'L1_gnn_weight', 'L1_ffn_w_gate', 'L1_ffn_w_up', 'L1_ffn_w_down']


def kernel(**inputs):
    import numpy as _np
    import concourse.bacc as _bacc
    from concourse import mybir as _mybir
    from concourse.bass_utils import run_bass_kernel_spmd as _run

    nc = _bacc.Bacc("TRN2", target_bir_lowering=False, num_devices=1)
    arrays, args = {}, []
    for name in _INS:
        a = _np.ascontiguousarray(inputs[name])
        arrays[f"in_{name}"] = a
        args.append(nc.dram_tensor(f"in_{name}", a.shape, _mybir.dt.from_np(a.dtype), kind="ExternalInput").ap())
    shape = inputs['x'].shape
    args.append(nc.dram_tensor("out_0", shape, _mybir.dt.float32, kind="ExternalOutput").ap())
    gnn_kernel(nc, *args)
    r = _run(nc, [arrays], core_ids=[0])
    return r.results[0]["out_0"]
```

```python
import concourse.bass as bass
from concourse import mybir
from contextlib import ExitStack


def gnn_kernel(nc, x, src, dst, edge_weight, W_l, b_l, W_r, gamma, beta, router_w, router_b,
               w1, b1, w2, b2, W_g, w_gate, w_up, w_down, out, upto=99):
    f32, f16, i32 = mybir.dt.float32, mybir.dt.float16, mybir.dt.int32
    ALU = mybir.AluOpType
    ACT = mybir.ActivationFunctionType
    AX = mybir.AxisListType
    ds = bass.ds

    N, D = x.shape
    E = src.shape[0]
    P = 128
    KC = D // P
    NB = -(-N // P)
    LAST = N - (NB - 1) * P
    NP = NB * P
    NE, _, FE = w1.shape
    FC = FE // P
    FF = w_gate.shape[0]
    FT = FF // P
    EPS = 1e-5
    WS = 256.0

    G = 16
    NG = -(-E // (P * G)) * P
    HT = 9
    HE = HT * P
    CE = 2 * HE
    GPC = CE // G
    EP = NG * G + CE
    MAXCH = -(-NG // GPC)
    BIG = 8192.0
    SPLIT = 50

    def dram(name, shape, dt):
        return nc.dram_tensor(name, shape, dt, kind="Internal").ap()

    src_p, dst_p = dram("src_p", [EP], i32), dram("dst_p", [EP], i32)
    ew_p = dram("ew_p", [EP], f32)
    group_min, group_max = dram("group_min", [NG], f32), dram("group_max", [NG], f32)
    xn1 = dram("xn1", [NP, 2 * D], f16)
    hpre = dram("hpre", [NP, D], f32)
    NS = 2 * N // P + NE
    x1_d, x2_d = dram("x1_d", [NP, D], f32), dram("x2_d", [NP, D], f32)
    z_d, xn3 = dram("z_d", [NP, 2 * D], f16), dram("xn3", [NP, 2 * D], f16)
    slot_token_d = dram("slot_token_d", [NS * P, 1], i32)
    items_out = dram("items_out", [NS * P, D], f32)

    RING = 4

    class Item:

        def __init__(self, k, i, count):
            self.k, self.i, self.i2 = k, i, i % 2
            self.fixed = isinstance(k, int)
            self.valid = not self.fixed or 0 <= k < count
            self.rows = LAST if self.fixed and k == NB - 1 and count == NB else P
            self.loads = (k - i) * (16 // RING) + 16

        def after(self, n):
            return not self.fixed or self.k >= n

    def ring_uses(i, count):
        return (count + RING - 1 - i) // RING

    def pipeline(eng, count, lag, body):
        lead = RING * (-(-(lag + RING) // RING))
        stop = lead + RING * ((count - 1 - lead) // RING)

        def step(t, i):
            def item(s):
                found = Item(t - s, (i - s) % RING, count)
                return found if found.valid else None
            body(item)

        for t in range(lead):
            step(t, t % RING)
        with eng.Fori(lead, stop, RING) as n:
            t = n.with_bounds(min_val=lead, max_val=stop - RING)
            for i in range(RING):
                step(t + i, i)
        for t in range(stop, count + lag):
            step(t, t % RING)

    ctx = ExitStack()
    with ctx:
        def sb(name, shape, dt, at=ctx):
            return at.enter_context(nc.sbuf_tensor(name, shape, dt))

        def pb(name, shape, dt, at=ctx):
            return at.enter_context(nc.psum_tensor(name, shape, dt))

        def sem(name, at):
            if at not in sems_of:
                sems_of[at] = []

                def release():
                    nc.clear_and_free_semaphores(sems_of[at])
                    nc.all_engine_barrier()

                at.callback(release)
            sems_of[at].append(nc.alloc_semaphore(f"{name}_p{len(sems_of)}"))
            return sems_of[at][-1]

        sems_of = {}

        table = sb("table", [1, 3 * 64], i32)
        ident16 = sb("ident16", [P, P], f16)
        ident32 = sb("ident32", [P, P], f32)
        iota_row = sb("iota_row", [P, P], f32)
        zeros16 = sb("zeros16", [P, D], f16)
        ones_col = sb("ones_col", [P, 1], f16)
        eps_col = sb("eps_col", [P, 1], f32)
        place = sb("place", [P, NB, 3], i32)
        share = sb("share", [P, NB, 2], f32)
        tile_expert = sb("tile_expert", [1, NS], i32)

        class Norm:

            def __init__(self, at, name, buffers=RING, x=None):
                self.x = x or [sb(f"{name}_x{i}", [P, D], f32, at) for i in range(buffers)]
                self.z = [sb(f"{name}_z{i}", [P, D], f32, at) for i in range(buffers)]
                self.hl = [sb(f"{name}_hl{i}", [P, 2 * D], f16, at) for i in range(buffers)]
                self.st6 = [sb(f"{name}_st6_{i}", [P, 6], f32, at) for i in range(buffers)]
                self.mv = [sb(f"{name}_mv{i}", [P, 4], f32, at) for i in range(buffers)]
                self.var_done, self.std_done, self.z_done, self.hi_done, self.lo_done = (
                    sem(f"{name}_{n}", at) for n in ("var_done", "std_done", "z_done", "hi_done", "lo_done"))

            def var(self, dve, m):
                r = slice(0, m.rows)
                nc.vector.bn_stats(self.st6[m.i][r, :], self.x[m.i][r, :])
                dve.drain()
                nc.vector.bn_aggr(self.mv[m.i][r, 0:2], self.st6[m.i][r, :]).then_inc(self.var_done, 1)

            def std(self, act, m):
                r = slice(0, m.rows)
                act.wait_ge(self.var_done, m.k + 1)
                nc.scalar.activation(self.mv[m.i][r, 2:3], self.mv[m.i][r, 1:2], ACT.Sqrt, bias=eps_col[r, :])\
                  .then_inc(self.std_done, 1)

            def scale(self, dve, m):
                r = slice(0, m.rows)
                dve.wait_ge(self.std_done, m.k + 1)
                nc.vector.reciprocal(self.mv[m.i][r, 3:4], self.mv[m.i][r, 2:3])
                dve.drain()
                nc.vector.tensor_scalar(self.z[m.i][r, :], self.x[m.i][r, :], self.mv[m.i][r, 0:1],
                                        self.mv[m.i][r, 3:4], ALU.subtract, ALU.mult).then_inc(self.z_done, 1)

            def hi(self, act, m):
                r = slice(0, m.rows)
                act.wait_ge(self.z_done, m.k + 1)
                nc.scalar.activation(self.hl[m.i][r, 0:D], self.z[m.i][r, :], ACT.Copy).then_inc(self.hi_done, 1)

            def lo(self, dve, m):
                r = slice(0, m.rows)
                dve.wait_ge(self.hi_done, m.k + 1)
                nc.vector.tensor_tensor(self.hl[m.i][r, D:2 * D], self.z[m.i][r, :], self.hl[m.i][r, 0:D],
                                        ALU.subtract).then_inc(self.lo_done, 1)

        def layer0():
            ph = ExitStack()
            with ph:
                bn_scale, bn_shift = sb("bn_scale", [P, D], f32, ph), sb("bn_shift", [P, D], f32, ph)
                graph0(bn_scale, bn_shift)
                if upto >= 3:
                    route(bn_scale, bn_shift)

        def graph0(bn_scale, bn_shift):
            ph = ExitStack()
            with ph:
                wlr = sb("wlr", [P, 2 * KC, 2, D], f16, ph)
                prepare(wlr)
                if upto >= 2:
                    sage(wlr, bn_scale, bn_shift)

        def prepare(wlr):
            p1 = ExitStack()
            with p1:
                pad_0 = sb("pad_0", [SPLIT, (EP - E) // SPLIT], i32, p1)
                pad_d = sb("pad_d", [SPLIT, (EP - E) // SPLIT], i32, p1)
                dst_all = sb("dst_all", [P, NG * G // P], i32, p1)
                gmin = sb("gmin", [P, NG // P], f32, p1)
                gmax = sb("gmax", [P, NG // P], f32, p1)
                gmin_all = sb("gmin_all", [64, NG], f32, p1)
                gmax_all = sb("gmax_all", [64, NG], f32, p1)
                g_iota = sb("g_iota", [64, NG], f32, p1)
                win = sb("win", [64, 8], f32, p1)
                cols = sb("cols", [64, 3], f32, p1)
                k_iota = sb("k_iota", [64, MAXCH + 1], f32, p1)
                k_hit = sb("k_hit", [64, MAXCH + 1], f32, p1)
                tri = sb("tri", [64, 64], f32, p1)
                wnat = sb("wnat", [P, 2, KC, D], f32, p1)
                zpad = sb("zpad", [32, 2 * D], f16, p1)
                tab_ps = pb("tab_ps", [1, 512], f32, p1)
                w_ps = [pb(f"w_ps{i}", [P, D], f32, p1) for i in range(2)]

                pads_set = sem("pads_set", p1)
                edges_copied = sem("edges_copied", p1)
                dst_loaded = sem("dst_loaded", p1)
                groups_reduced = sem("groups_reduced", p1)
                groups_stored = sem("groups_stored", p1)
                groups_loaded = sem("groups_loaded", p1)
                pool_zeroed = sem("pool_zeroed", p1)
                consts_set = sem("consts_set", p1)
                windows_found = sem("windows_found", p1)
                table_summed = sem("table_summed", p1)
                w_loaded = sem("w_loaded", p1)
                w_turned = sem("w_turned", p1)
                w_hi_done = sem("w_hi_done", p1)
                w_lo_done = sem("w_lo_done", p1)
                pad_stored = sem("pad_stored", p1)
                norm = Norm(p1, "n0")
                x_loaded = [sem(f"x_loaded{i}", p1) for i in range(RING)]
                z_stored = [sem(f"z0_stored{i}", p1) for i in range(RING)]

                block = p1.enter_context(nc.Block())

                @block.gpsimd
                def _(pool):
                    nc.gpsimd.memset(pad_0[:], 0).then_inc(pads_set, 1)
                    nc.gpsimd.memset(pad_d[:], NP).then_inc(pads_set, 1)
                    nc.gpsimd.memset(zpad[:], 0.0).then_inc(pool_zeroed, 1)
                    nc.gpsimd.memset(eps_col[:], EPS).then_inc(pool_zeroed, 1)
                    nc.gpsimd.memset(ident16[:], 0.0).then_inc(pool_zeroed, 1)
                    nc.gpsimd.memset(ident32[:], 0.0).then_inc(pool_zeroed, 1)
                    nc.gpsimd.memset(tri[:], 1.0).then_inc(pool_zeroed, 1)
                    nc.gpsimd.memset(zeros16[:], 0.0)
                    nc.gpsimd.memset(ones_col[:], 1.0)
                    pool.wait_ge(pool_zeroed, 5)
                    nc.gpsimd.affine_select(out=ident32[:], in_=ident32[:], compare_op=ALU.not_equal, fill=1.0,
                                            base=0, pattern=[[-1, P]], channel_multiplier=1).then_inc(consts_set, 1)
                    nc.gpsimd.affine_select(out=ident16[:], in_=ident16[:], compare_op=ALU.not_equal, fill=1.0,
                                            base=0, pattern=[[-1, P]], channel_multiplier=1)
                    nc.gpsimd.affine_select(out=tri[:], in_=tri[:], compare_op=ALU.is_gt, fill=0.0,
                                            base=0, pattern=[[1, 64]], channel_multiplier=-1)
                    nc.gpsimd.iota(iota_row[:], [[1, P]], base=0, channel_multiplier=0,
                                   allow_small_or_imprecise_dtypes=True)
                    nc.gpsimd.iota(k_iota[:], [[GPC, MAXCH + 1]], base=0, channel_multiplier=0,
                                   allow_small_or_imprecise_dtypes=True)
                    nc.gpsimd.iota(win[:, 0:1], [[0, 1]], base=0, channel_multiplier=P,
                                   allow_small_or_imprecise_dtypes=True)
                    nc.gpsimd.iota(g_iota[:], [[1, NG]], base=0, channel_multiplier=0,
                                   allow_small_or_imprecise_dtypes=True).then_inc(consts_set, 1)

                @block.sync
                def _(sp):
                    def step(item):
                        if m := item(0):
                            if m.after(RING):
                                sp.wait_ge(norm.z_done, m.k - (RING - 1))
                            sp.dma_start(norm.x[m.i][0:m.rows, :], x[ds(m.k * P, m.rows), :])\
                              .then_inc(x_loaded[m.i], 16)

                    for a, padded in ((src, src_p), (dst, dst_p), (edge_weight, ew_p)):
                        sp.dma_start(padded[0:E].rearrange("(a b) -> a b", a=SPLIT),
                                     a.rearrange("(a b) -> a b", a=SPLIT)).then_inc(edges_copied, 16)
                    sp.wait_ge(pads_set, 2)
                    for padded, pad in ((src_p, pad_0), (dst_p, pad_d), (ew_p, pad_0)):
                        view = pad[:].bitcast(f32) if padded is ew_p else pad[:]
                        sp.dma_start(padded[E:EP].rearrange("(a b) -> a b", a=SPLIT), view)\
                          .then_inc(edges_copied, 16)
                    for n, w in enumerate((W_l, W_r)):
                        sp.dma_start(wnat[:, n], w.rearrange("(c p) k -> p c k", p=P)).then_inc(w_loaded, 16)
                    sp.wait_ge(edges_copied, 96)
                    sp.dma_start(dst_all[:], dst_p[0:NG * G].rearrange("(p c) -> p c", p=P)).then_inc(dst_loaded, 16)
                    sp.wait_ge(pool_zeroed, 1)
                    sp.dma_start(xn1[N:NP, :], zpad[0:NP - N, :]).then_inc(pad_stored, 16)
                    sp.wait_ge(groups_reduced, 2)
                    sp.dma_start(group_min.rearrange("(p c) -> p c", p=P), gmin[:]).then_inc(groups_stored, 16)
                    sp.dma_start(group_max.rearrange("(p c) -> p c", p=P), gmax[:]).then_inc(groups_stored, 16)
                    sp.wait_ge(groups_stored, 32)
                    sp.dma_start(gmin_all[:], group_min.partition_broadcast(64)).then_inc(groups_loaded, 16)
                    sp.dma_start(gmax_all[:], group_max.partition_broadcast(64)).then_inc(groups_loaded, 16)
                    pipeline(sp, NB, 0, step)
                    sp.wait_ge(pad_stored, 16)

                @block.tensor
                def _(pe):
                    pe.wait_ge(w_loaded, 32)
                    pe.wait_ge(consts_set, 1)
                    for k in range(2 * KC):
                        if k >= 2:
                            pe.wait_ge(w_hi_done, k - 1)
                            pe.wait_ge(w_lo_done, k - 1)
                        for o in range(KC):
                            last = nc.tensor.transpose(w_ps[k % 2][:, o * P:(o + 1) * P],
                                                       wnat[:, k // KC, o, (k % KC) * P:(k % KC + 1) * P],
                                                       ident32[:])
                        last.then_inc(w_turned, 1)
                    pe.wait_ge(windows_found, 1)
                    pe.wait_ge(consts_set, 2)
                    nc.tensor.matmul(tab_ps[0:1, 0:64], cols[:, 0:1], ident32[0:64, 0:64], start=True, stop=True)
                    nc.tensor.matmul(tab_ps[0:1, 64:128], cols[:, 0:1], tri[:], start=True, stop=True)
                    nc.tensor.matmul(tab_ps[0:1, 128:192], cols[:, 1:2], ident32[0:64, 0:64],
                                     start=True, stop=True).then_inc(table_summed, 1)

                @block.scalar
                def _(act):
                    for k in range(2 * KC):
                        act.wait_ge(w_turned, k + 1)
                        nc.scalar.activation(wlr[:, k, 0, :], w_ps[k % 2][:], ACT.Copy, scale=WS)\
                          .then_inc(w_hi_done, 1)

                    def step(item):
                        if m := item(3):
                            act.wait_ge(norm.lo_done, m.k + 1)
                            act.dma_start(xn1[ds(m.k * P, m.rows), :], norm.hl[m.i][0:m.rows, :])\
                               .then_inc(z_stored[m.i], 16)
                        if m := item(0):
                            norm.std(act, m)
                        if m := item(1):
                            if m.after(RING):
                                act.wait_ge(z_stored[m.i], m.loads - 16)
                            norm.hi(act, m)

                    pipeline(act, NB, 3, step)
                    for i in range(RING):
                        act.wait_ge(z_stored[i], 16 * ring_uses(i, NB))

                @block.vector
                def _(dve):
                    dve.wait_ge(dst_loaded, 16)
                    groups = dst_all[:].rearrange("p (c g) -> p c g", g=G)
                    nc.vector.tensor_reduce(gmin[:], groups, AX.X, ALU.min).then_inc(groups_reduced, 1)
                    nc.vector.tensor_reduce(gmax[:], groups, AX.X, ALU.max).then_inc(groups_reduced, 1)
                    for k in range(2 * KC):
                        dve.wait_ge(w_hi_done, k + 1)
                        nc.vector.scalar_tensor_tensor(wlr[:, k, 1, :], w_ps[k % 2][:], WS, wlr[:, k, 0, :],
                                                       ALU.mult, ALU.subtract).then_inc(w_lo_done, 1)
                    dve.wait_ge(groups_loaded, 32)
                    dve.wait_ge(consts_set, 2)
                    nc.vector.tensor_scalar(win[:, 1:2], win[:, 0:1], float(P - 1), None, ALU.add)
                    dve.drain()
                    nc.vector.tensor_scalar(gmin_all[:], gmin_all[:], win[:, 1:2], None, ALU.is_le)
                    dve.drain()
                    nc.vector.scalar_tensor_tensor(gmax_all[:], gmax_all[:], win[:, 0:1], gmin_all[:],
                                                   ALU.is_ge, ALU.mult)
                    dve.drain()
                    nc.vector.scalar_tensor_tensor(gmin_all[:], g_iota[:], 1.0, gmax_all[:], ALU.add, ALU.mult)
                    nc.vector.tensor_scalar(g_iota[:], g_iota[:], -1.0, BIG, ALU.mult, ALU.add)
                    dve.drain()
                    nc.vector.tensor_reduce(win[:, 2:3], gmin_all[:], AX.X, ALU.max)
                    nc.vector.tensor_tensor(gmax_all[:], gmax_all[:], g_iota[:], ALU.mult)
                    dve.drain()
                    nc.vector.tensor_reduce(win[:, 3:4], gmax_all[:], AX.X, ALU.max)
                    dve.drain()
                    nc.vector.tensor_scalar(win[:, 4:5], win[:, 3:4], -1.0, BIG, ALU.mult, ALU.add)
                    dve.drain()
                    nc.vector.tensor_tensor(win[:, 5:6], win[:, 2:3], win[:, 4:5], ALU.subtract)
                    nc.vector.tensor_scalar(cols[:, 1:2], win[:, 4:5], float(NG - 1), float(G), ALU.min, ALU.mult)
                    dve.drain()
                    nc.vector.tensor_scalar(k_hit[:], k_iota[:], win[:, 5:6], None, ALU.is_lt)
                    dve.drain()
                    nc.vector.tensor_reduce(win[:, 6:7], k_hit[:], AX.X, ALU.add)
                    dve.drain()
                    nc.vector.tensor_scalar(cols[:, 0:1], win[:, 6:7], 1.0, None, ALU.max).then_inc(windows_found, 1)
                    dve.wait_ge(table_summed, 1)
                    nc.vector.tensor_copy(table[:], tab_ps[:, 0:192])

                    def step(item):
                        if m := item(0):
                            dve.wait_ge(x_loaded[m.i], m.loads)
                            norm.var(dve, m)
                        if m := item(1):
                            norm.scale(dve, m)
                        if m := item(2):
                            norm.lo(dve, m)

                    pipeline(dve, NB, 2, step)

        class Edges:

            def __init__(self, at, weighted):
                tag = "w_" if weighted else "u_"
                self.weighted = weighted
                self.idx = [sb(f"{tag}idx{h}", [P, HT], i32, at) for h in range(2)]
                self.tgt = [sb(f"{tag}tgt{h}", [P, HT], i32, at) for h in range(2)]
                self.rows = sb(f"{tag}rows", [P, 2 * HT, 2 * D], f16, at)
                self.local = [sb(f"{tag}local{h}", [P, HT], f32, at) for h in range(2)]
                self.mask = [sb(f"{tag}mask{h}", [P, HT, P], f16, at) for h in range(2)]
                self.first_node = sb(f"{tag}first_node", [P, 1], f32, at)
                if weighted:
                    self.ew = [sb(f"{tag}ew{h}", [P, HT], f32, at) for h in range(2)]
                    self.ew_hi16 = [sb(f"{tag}ew_hi16_{h}", [P, HT], f16, at) for h in range(2)]
                    self.ew_hi = [sb(f"{tag}ew_hi{h}", [P, HT], f32, at) for h in range(2)]
                    self.ew_lo = [sb(f"{tag}ew_lo{h}", [P, HT], f32, at) for h in range(2)]
                    self.mask_lo = [sb(f"{tag}mask_lo{h}", [P, HT, P], f16, at) for h in range(2)]
                self.idx_loaded = [sem(f"{tag}idx_loaded{h}", at) for h in range(2)]
                self.tgt_loaded = [sem(f"{tag}tgt_loaded{h}", at) for h in range(2)]
                self.gathered = [sem(f"{tag}gathered{j}", at) for j in range(2 * HT)]
                self.idx_seen = sem(f"{tag}idx_seen", at)
                self.masked = sem(f"{tag}masked", at)
                self.summed = sem(f"{tag}summed", at)

            def chunks(self, eng, b, body):
                n = eng.value_load(table[0:1, ds(b, 1)], min_val=1, max_val=MAXCH)
                q0 = eng.value_load(table[0:1, ds(b + 64, 1)], min_val=0, max_val=NB * MAXCH)
                with eng.Fori(0, n) as i:
                    body(eng.snap(q0 + i).with_bounds(min_val=0, max_val=NB * MAXCH), i)

            def load(self, eng, b):
                e0 = eng.value_load(table[0:1, ds(b + 128, 1)], min_val=0, max_val=(NG - 1) * G)

                def chunk(q, i):
                    for h in range(2):
                        eng.wait_ge(self.summed, q * 2 + (h + 1))
                        at = eng.snap(e0 + i * CE + h * HE).with_bounds(min_val=0, max_val=EP - HE)
                        part = lambda t: t[ds(at, HE)].rearrange("(p j) -> p j", j=HT)
                        eng.dma_start(self.idx[h][:], part(src_p)).then_inc(self.idx_loaded[h], 16)
                        eng.dma_start(self.tgt[h][:], part(dst_p)).then_inc(self.tgt_loaded[h], 16)
                        if self.weighted:
                            eng.dma_start(self.ew[h][:], part(ew_p)).then_inc(self.tgt_loaded[h], 16)

                self.chunks(eng, b, chunk)

            def gather(self, eng, b, rows_of):
                def chunk(q, i):
                    for h in range(2):
                        eng.wait_ge(self.idx_loaded[h], q * 16 + 16)
                        eng.sem_inc(self.idx_seen, 1)
                        for j in range(HT):
                            eng.indirect_dma_start(
                                out=self.rows[:, h * HT + j, :], out_offset=None, in_=rows_of,
                                in_offset=bass.IndirectOffsetOnAxis(ap=self.idx[h][:, j:j + 1], axis=0),
                            ).then_inc(self.gathered[h * HT + j], 16)

                self.chunks(eng, b, chunk)

            def chunk_masks(self, dve, q):
                loads = 2 if self.weighted else 1
                for h in range(2):
                    dve.wait_ge(self.tgt_loaded[h], q * (16 * loads) + 16 * loads)
                    nc.vector.tensor_scalar(self.local[h][:], self.tgt[h][:], self.first_node[:], None,
                                            ALU.subtract)
                    if self.weighted:
                        nc.vector.tensor_copy(self.ew_hi16[h][:], self.ew[h][:])
                        dve.drain()
                        nc.vector.tensor_copy(self.ew_hi[h][:], self.ew_hi16[h][:])
                        nc.vector.tensor_tensor(self.ew_lo[h][:], self.ew[h][:], self.ew_hi16[h][:],
                                                ALU.subtract)
                    dve.drain()
                    for j in range(HT):
                        to = self.local[h][:, j:j + 1]
                        if self.weighted:
                            nc.vector.tensor_scalar(self.mask[h][:, j, :], iota_row[:], to,
                                                    self.ew_hi[h][:, j:j + 1], ALU.is_equal, ALU.mult)
                            last = nc.vector.tensor_scalar(self.mask_lo[h][:, j, :], iota_row[:], to,
                                                           self.ew_lo[h][:, j:j + 1], ALU.is_equal, ALU.mult)
                        else:
                            last = nc.vector.tensor_scalar(self.mask[h][:, j, :], iota_row[:], to, None,
                                                           ALU.is_equal)
                    last.then_inc(self.masked, 1)

            def masks(self, dve, b):
                self.chunks(dve, b, lambda q, i: self.chunk_masks(dve, q))
                self.next_block(dve)

            def masks_first(self, dve, b):
                q0 = dve.value_load(table[0:1, ds(b + 64, 1)], min_val=0, max_val=NB * MAXCH)
                self.chunk_masks(dve, q0)

            def masks_rest(self, dve, b):
                n = dve.value_load(table[0:1, ds(b, 1)], min_val=1, max_val=MAXCH)
                q0 = dve.value_load(table[0:1, ds(b + 64, 1)], min_val=0, max_val=NB * MAXCH)
                with dve.If(n > 1):
                    with dve.Fori(1, n) as i:
                        self.chunk_masks(dve, dve.snap(q0 + i).with_bounds(min_val=0, max_val=NB * MAXCH))
                self.next_block(dve)

            def next_block(self, dve):
                dve.drain()
                nc.vector.tensor_scalar(self.first_node[:], self.first_node[:], float(P), None, ALU.add)
                dve.drain()

            def sum(self, pe, b, acc, count):
                nc.tensor.matmul(acc[:], zeros16[:, 0:P], zeros16[:], start=True, stop=False, skip_group_check=True)
                if count is not None:
                    nc.tensor.matmul(count, zeros16[:, 0:P], zeros16[:, 0:1], start=True, stop=False,
                                     skip_group_check=True)

                def add(to, mask, rows):
                    return nc.tensor.matmul(to, mask, rows, start=False, stop=False, skip_group_check=True)

                def chunk(q, i):
                    for h in range(2):
                        pe.wait_ge(self.masked, q * 2 + (h + 1))
                        for j in range(HT):
                            t = h * HT + j
                            pe.wait_ge(self.gathered[t], q * 16 + 16)
                            mask = self.mask[h][:, j, :]
                            last = add(acc[:], mask, self.rows[:, t, 0:D])
                            last = add(acc[:], mask, self.rows[:, t, D:2 * D])
                            if self.weighted:
                                last = add(acc[:], self.mask_lo[h][:, j, :], self.rows[:, t, 0:D])
                            if count is not None:
                                last = add(count, mask, ones_col[:])
                        last.then_inc(self.summed, 1)

                self.chunks(pe, b, chunk)

        def split_product(out, left, right, chunks, last_sem=None):
            for c in range(chunks):
                for n, (l, r) in enumerate(((0, 0), (0, 1), (1, 0))):
                    last = nc.tensor.matmul(out, left(c, l), right(c, r), start=(c == 0 and n == 0),
                                            stop=(c == chunks - 1 and n == 2))
            return last

        def sage(wlr, bn_scale, bn_shift):
            p2 = ExitStack()
            with p2:
                edges = Edges(p2, False)
                own = sb("own", [P, 2 * D], f16, p2)
                mean_hl = sb("mean_hl", [P, 2, D], f16, p2)
                mean_t = sb("mean_t", [P, 2, KC, P], f16, p2)
                own_t = sb("own_t", [P, 2, KC, P], f16, p2)
                inv = sb("inv", [P, 2], f32, p2)
                h_sb = sb("h_sb", [P, D], f32, p2)
                h_sq = sb("h_sq", [P, D], f32, p2)
                bias = sb("bias", [P, D], f32, p2)
                gam = sb("gam", [P, D], f32, p2)
                bet = sb("bet", [P, D], f32, p2)
                ones32 = sb("ones32", [P, 2, P], f32, p2)
                stat = sb("stat", [P, 3, D], f32, p2)
                acc = pb("acc", [P, D], f32, p2)
                cnt = pb("cnt", [P, D], f32, p2)
                mean_ps = pb("mean_ps", [P, 2, KC, P], f16, p2)
                own_ps = pb("own_ps", [P, 2, KC, P], f16, p2)
                h_ps = pb("h_ps", [P, D], f32, p2)
                sum_ps = pb("sum_ps", [P, D], f32, p2)
                sq_ps = pb("sq_ps", [P, D], f32, p2)

                ones_set = sem("ones_set", p2)
                rows_loaded = sem("rows_loaded", p2)
                own_loaded = sem("own_loaded", p2)
                acc_ready = sem("acc_ready", p2)
                inv_done = sem("inv_done", p2)
                mean_hi_done = sem("mean_hi_done", p2)
                mean_lo_done = sem("mean_lo_done", p2)
                turned = sem("turned", p2)
                mean_t_done = sem("mean_t_done", p2)
                own_t_done = sem("own_t_done", p2)
                h_summed = sem("h_summed", p2)
                h_done = sem("h_done", p2)
                h_sq_done = sem("h_sq_done", p2)
                h_stored = sem("h_stored", p2)
                stats_added = sem("stats_added", p2)
                bn_var = sem("bn_var", p2)
                bn_std = sem("bn_std", p2)

                block = p2.enter_context(nc.Block())

                def after_first(eng, body):
                    body(0)
                    with eng.Fori(1, NB - 1) as b:
                        body(b)
                    body(NB - 1)

                first = lambda b: isinstance(b, int) and b == 0
                final = lambda b: isinstance(b, int) and b == NB - 1

                @block.gpsimd
                def _(pool):
                    nc.gpsimd.memset(ones32[:], 1.0).then_inc(ones_set, 1)
                    pool.wait_ge(ones_set, 1)
                    nc.gpsimd.affine_select(out=ones32[:, 1, :], in_=ones32[:, 1, :], compare_op=ALU.is_gt,
                                            fill=0.0, base=LAST, pattern=[[0, P]], channel_multiplier=-1)\
                        .then_inc(ones_set, 1)
                    after_first(pool, lambda b: edges.gather(pool, b, xn1))

                @block.sync
                def _(sp):
                    for t, a in ((bias, b_l), (gam, gamma), (bet, beta)):
                        sp.dma_start(t[:], a.partition_broadcast(P)).then_inc(rows_loaded, 16)

                    def step(b):
                        edges.load(sp, b)
                        if not first(b):
                            sp.wait_ge(turned, b)
                        sp.dma_start(own[:], xn1[ds(b * P, P), :]).then_inc(own_loaded, 16)

                    after_first(sp, step)

                @block.tensor
                def _(pe):
                    pe.sem_inc(edges.summed, 2)
                    pe.wait_ge(ones_set, 2)
                    for t in (sum_ps, sq_ps):
                        nc.tensor.matmul(t[:], zeros16[:, 0:P], zeros16[:], start=True, stop=False,
                                         skip_group_check=True)

                    def project(b):
                        pe.wait_ge(mean_t_done, b + 1)
                        pe.wait_ge(own_t_done, b + 1)
                        split_product(h_ps[:], lambda c, part: (mean_t if c < KC else own_t)[:, part, c % KC, :],
                                      lambda c, part: wlr[:, c, part, :], 2 * KC).then_inc(h_summed, 1)

                    def turn(b):
                        pe.wait_ge(mean_hi_done, b + 1)
                        pe.wait_ge(mean_lo_done, b + 1)
                        pe.wait_ge(own_loaded, b * 16 + 16)
                        for part in range(2):
                            for c in range(KC):
                                nc.tensor.transpose(mean_ps[:, part, c, :], mean_hl[:, part, c * P:(c + 1) * P],
                                                    ident16[:])
                                last = nc.tensor.transpose(own_ps[:, part, c, :],
                                                           own[:, part * D + c * P:part * D + (c + 1) * P],
                                                           ident16[:])
                        last.then_inc(turned, 1)

                    def add_stats(b, valid):
                        pe.wait_ge(h_done, b + 1)
                        pe.wait_ge(h_sq_done, b + 1)
                        nc.tensor.matmul(sum_ps[:], ones32[:, valid, :], h_sb[:], start=False, stop=False,
                                         skip_group_check=True)
                        nc.tensor.matmul(sq_ps[:], ones32[:, valid, :], h_sq[:], start=False, stop=False,
                                         skip_group_check=True).then_inc(stats_added, 1)

                    def step(b):
                        edges.sum(pe, b, acc, cnt[:, 0:1])
                        nc.tensor.matmul(cnt[:, 0:1], zeros16[:, 0:P], zeros16[:, 0:1], start=False, stop=True,
                                         skip_group_check=True).then_inc(acc_ready, 1)
                        if not first(b):
                            project(b - 1)
                        turn(b)
                        if not first(b):
                            add_stats(b - 1, 0)

                    after_first(pe, step)
                    project(NB - 1)
                    add_stats(NB - 1, 1)

                @block.scalar
                def _(act):
                    def square(b):
                        act.wait_ge(h_done, b + 1)
                        if not first(b):
                            act.wait_ge(stats_added, b)
                        nc.scalar.activation(h_sq[:], h_sb[:], ACT.Square).then_inc(h_sq_done, 1)
                        act.dma_start(hpre[ds(b * P, P), :], h_sb[:]).then_inc(h_stored, 16)

                    def step(b):
                        act.wait_ge(inv_done, b + 1)
                        nc.scalar.activation(mean_hl[:, 0, :], acc[:], ACT.Copy, scale=inv[:, 1:2])\
                          .then_inc(mean_hi_done, 1)
                        if not first(b):
                            square(b - 1)
                        act.wait_ge(turned, b + 1)
                        nc.scalar.activation(mean_t[:], mean_ps[:], ACT.Copy).then_inc(mean_t_done, 1)

                    after_first(act, step)
                    square(NB - 1)
                    act.wait_ge(h_stored, NB * 16)
                    act.wait_ge(bn_var, 1)
                    nc.scalar.activation(bn_scale[:], stat[:, 1, :], ACT.Sqrt, bias=eps_col[:]).then_inc(bn_std, 1)

                @block.vector
                def _(dve):
                    nc.vector.memset(edges.first_node[:], 0.0)
                    dve.drain()
                    dve.wait_ge(rows_loaded, 48)

                    def add_bias(b):
                        dve.wait_ge(h_summed, b + 1)
                        if not first(b):
                            dve.wait_ge(stats_added, b)
                            dve.wait_ge(h_stored, b * 16)
                        nc.vector.scalar_tensor_tensor(h_sb[:], h_ps[:], 1.0 / WS, bias[:], ALU.mult, ALU.add)\
                          .then_inc(h_done, 1)

                    def step(b):
                        edges.masks(dve, b)
                        dve.wait_ge(acc_ready, b + 1)
                        nc.vector.tensor_scalar(inv[:, 0:1], cnt[:, 0:1], 1.0, None, ALU.max)
                        dve.drain()
                        nc.vector.reciprocal(inv[:, 1:2], inv[:, 0:1]).then_inc(inv_done, 1)
                        dve.drain()
                        dve.wait_ge(mean_hi_done, b + 1)
                        nc.vector.scalar_tensor_tensor(mean_hl[:, 1, :], acc[:], inv[:, 1:2], mean_hl[:, 0, :],
                                                       ALU.mult, ALU.subtract).then_inc(mean_lo_done, 1)
                        if not first(b):
                            add_bias(b - 1)
                        dve.wait_ge(turned, b + 1)
                        nc.vector.tensor_copy(own_t[:], own_ps[:]).then_inc(own_t_done, 1)

                    after_first(dve, step)
                    add_bias(NB - 1)
                    dve.wait_ge(stats_added, NB)
                    nc.vector.tensor_scalar(stat[:, 0, :], sum_ps[:], 1.0 / N, None, ALU.mult)
                    dve.drain()
                    nc.vector.tensor_tensor(stat[:, 2, :], stat[:, 0, :], stat[:, 0, :], ALU.mult)
                    dve.drain()
                    nc.vector.scalar_tensor_tensor(stat[:, 1, :], sq_ps[:], 1.0 / N, stat[:, 2, :], ALU.mult,
                                                   ALU.subtract).then_inc(bn_var, 1)
                    dve.wait_ge(bn_std, 1)
                    nc.vector.reciprocal(stat[:, 1, :], bn_scale[:])
                    dve.drain()
                    nc.vector.tensor_tensor(bn_scale[:], stat[:, 1, :], gam[:], ALU.mult)
                    dve.drain()
                    nc.vector.tensor_tensor(stat[:, 2, :], stat[:, 0, :], bn_scale[:], ALU.mult)
                    dve.drain()
                    nc.vector.tensor_tensor(bn_shift[:], bet[:], stat[:, 2, :], ALU.subtract)

        def route(bn_scale, bn_shift):
            at = ExitStack()
            with at:
                norm = Norm(at, "n1")
                x_in = [sb(f"x_in{i}", [P, D], f32, at) for i in range(RING)]
                h_in = [sb(f"h_in{i}", [P, D], f32, at) for i in range(RING)]
                act_in = [sb(f"act_in{i}", [P, D], f32, at) for i in range(2)]
                z_t = [sb(f"z_t{i}", [P, 2, KC, P], f16, at) for i in range(2)]
                rw32 = sb("rw32", [P, KC, NE], f32, at)
                rw = sb("rw", [P, 2, KC, NE], f16, at)
                rb = sb("rb", [P, NE], f32, at)
                logits = sb("logits", [P, NB, NE], f32, at)
                less = sb("less", [P, NE], f32, at)
                t1, t2, hot1, hot2, base = (sb(n, [P, NB, NE], f32, at) for n in ("t1", "t2", "hot1", "hot2", "base"))
                hot = sb("hot", [P, NB, NE], f16, at)
                top1, top2, mx, den = (sb(n, [P, NB], f32, at) for n in ("top1", "top2", "mx", "den"))
                before = sb("before", [P, P], f16, at)
                ones = sb("ones", [P, P], f16, at)
                run1, run2 = sb("run1", [P, NB, NE], f32, at), sb("run2", [P, NB, NE], f32, at)
                tiles_i = sb("tiles_i", [P, NE], i32, at)
                tiles, end1, end2 = (sb(n, [P, NE], f32, at) for n in ("tiles", "end1", "end2"))
                slot_iota, slot_of = sb("slot_iota", [1, P], f32, at), sb("slot_of", [1, P], f32, at)
                z_ps = [pb(f"z_ps{i}", [P, 2, KC, P], f16, at) for i in range(2)]
                l_ps = [pb(f"l_ps{i}", [P, 512], f32, at) for i in range(2)]
                in_ps = pb("in_ps", [P, 512], f32, at)
                all_ps = pb("all_ps", [P, 512], f32, at)

                loaded = [sem(f"loaded{i}", at) for i in range(RING)]
                x1_stored = [sem(f"x1_stored{i}", at) for i in range(RING)]
                z_stored = [sem(f"z_stored{i}", at) for i in range(RING)]
                small_loaded = sem("small_loaded", at)
                consts = sem("consts", at)
                rw_split = sem("rw_split", at)
                bn_done = sem("bn_done", at)
                x1_done = sem("x1_done", at)
                turned = sem("turned", at)
                z_t_done = sem("z_t_done", at)
                routed = sem("routed", at)
                logits_done = sem("logits_done", at)
                shifted = sem("shifted", at)
                exp_done = sem("exp_done", at)
                hots_done = sem("hots_done", at)
                hot_masked = sem("hot_masked", at)
                hot_sent = sem("hot_sent", at)
                ranked = sem("ranked", at)
                zeroed = sem("zeroed", at)
                pool_mult = sem("pool_mult", at)

                block = at.enter_context(nc.Block())

                @block.sync
                def _(sp):
                    sp.dma_start(rw32[:], router_w.rearrange("(c p) e -> p c e", p=P)).then_inc(small_loaded, 16)
                    sp.dma_start(rb[:], router_b.partition_broadcast(P)).then_inc(small_loaded, 16)

                    def step(item):
                        if m := item(0):
                            if m.after(RING):
                                sp.wait_ge(x1_done, m.k - (RING - 1))
                            r, rows = slice(0, m.rows), ds(m.k * P, m.rows)
                            sp.dma_start(h_in[m.i][r, :], hpre[rows, :]).then_inc(loaded[m.i], 16)
                            sp.dma_start(x_in[m.i][r, :], x[rows, :]).then_inc(loaded[m.i], 16)

                    pipeline(sp, NB, 0, step)

                @block.gpsimd
                def _(pool):
                    nc.gpsimd.memset(logits[:], 0.0).then_inc(consts, 1)
                    nc.gpsimd.memset(before[:], 1.0).then_inc(zeroed, 1)
                    nc.gpsimd.memset(ones[:], 1.0)
                    pool.wait_ge(zeroed, 1)
                    nc.gpsimd.affine_select(out=before[:], in_=before[:], compare_op=ALU.is_gt, fill=0.0,
                                            base=0, pattern=[[1, P]], channel_multiplier=-1)
                    nc.gpsimd.iota(place[:, :, 2], [[P, NB]], base=0, channel_multiplier=1)
                    nc.gpsimd.iota(less[:], [[-1, NE]], base=NE, channel_multiplier=0,
                                   allow_small_or_imprecise_dtypes=True)
                    nc.gpsimd.iota(slot_iota[:], [[1, P]], base=0, channel_multiplier=0,
                                   allow_small_or_imprecise_dtypes=True).then_inc(consts, 1)

                    def step(item):
                        if m := item(0):
                            r = slice(0, m.rows)
                            pool.wait_ge(loaded[m.i], m.loads * 2)
                            if m.after(2):
                                pool.wait_ge(x1_done, m.k - 1)
                            nc.gpsimd.tensor_tensor(act_in[m.i2][r, :], h_in[m.i][r, :], bn_scale[r, :], ALU.mult)\
                              .then_inc(pool_mult, 1)
                            pool.wait_ge(pool_mult, m.k + 1)
                            nc.gpsimd.tensor_tensor(act_in[m.i2][r, :], act_in[m.i2][r, :], bn_shift[r, :], ALU.add)\
                              .then_inc(bn_done, 1)

                    pipeline(pool, NB, 0, step)
                    pool.wait_ge(hots_done, 1)
                    for hot_ in (hot1, hot2):
                        nc.gpsimd.affine_select(out=hot_[:, NB - 1, :], in_=hot_[:, NB - 1, :], compare_op=ALU.is_gt,
                                                fill=0.0, base=LAST, pattern=[[0, NE]], channel_multiplier=-1)\
                          .then_inc(hot_masked, 1)

                @block.tensor
                def _(pe):
                    pe.wait_ge(consts, 2)
                    pe.wait_ge(rw_split, 1)

                    def step(item):
                        if m := item(0):
                            pe.wait_ge(norm.lo_done, m.k + 1)
                            pe.wait_ge(norm.hi_done, m.k + 1)
                            if m.after(2):
                                pe.wait_ge(z_t_done, m.k - 1)
                            for part in range(2):
                                for c in range(KC):
                                    last = nc.tensor.transpose(
                                        z_ps[m.i2][:, part, c, 0:m.rows],
                                        norm.hl[m.i][0:m.rows, part * D + c * P:part * D + (c + 1) * P],
                                        ident16[0:m.rows, 0:m.rows])
                            last.then_inc(turned, 1)
                        if m := item(1):
                            pe.wait_ge(z_t_done, m.k + 1)
                            if m.after(2):
                                pe.wait_ge(logits_done, m.k - 1)
                            split_product(l_ps[m.i2][0:m.rows, 0:NE], lambda c, part: z_t[m.i2][:, part, c, 0:m.rows],
                                          lambda c, part: rw[:, part, c, :], KC).then_inc(routed, 1)

                    pipeline(pe, NB, 1, step)
                    pe.wait_ge(hot_sent, 1)
                    flat = hot[:].rearrange("p b e -> p (b e)")
                    nc.tensor.matmul(in_ps[:, 0:NB * NE], before[:], flat, start=True, stop=True)
                    nc.tensor.matmul(all_ps[:, 0:NB * NE], ones[:], flat, start=True, stop=True).then_inc(ranked, 1)

                @block.scalar
                def _(act):
                    act.wait_ge(consts, 2)

                    def step(item):
                        if m := item(1):
                            act.wait_ge(x1_done, m.k + 1)
                            act.dma_start(x1_d[ds(m.k * P, m.rows), :], norm.x[m.i][0:m.rows, :])\
                               .then_inc(x1_stored[m.i], 16)
                        if m := item(3):
                            act.wait_ge(norm.lo_done, m.k + 1)
                            act.dma_start(z_d[ds(m.k * P, m.rows), :], norm.hl[m.i][0:m.rows, :])\
                               .then_inc(z_stored[m.i], 16)
                        if m := item(0):
                            norm.std(act, m)
                        if m := item(1):
                            if m.after(RING):
                                act.wait_ge(z_stored[m.i], m.loads - 16)
                            norm.hi(act, m)
                        if m := item(2):
                            act.wait_ge(turned, m.k + 1)
                            if m.after(2):
                                act.wait_ge(routed, m.k - 1)
                            nc.scalar.activation(z_t[m.i2][:, :, :, 0:m.rows], z_ps[m.i2][:, :, :, 0:m.rows],
                                                 ACT.Copy).then_inc(z_t_done, 1)
                        if m := item(3):
                            act.wait_ge(routed, m.k + 1)
                            nc.scalar.activation(logits[0:m.rows, m.k, :], l_ps[m.i2][0:m.rows, 0:NE], ACT.Copy)\
                              .then_inc(logits_done, 1)

                    pipeline(act, NB, 3, step)
                    for i in range(RING):
                        act.wait_ge(x1_stored[i], 16 * ring_uses(i, NB))
                        act.wait_ge(z_stored[i], 16 * ring_uses(i, NB))
                    act.wait_ge(shifted, 1)
                    nc.scalar.activation(t1[:], t1[:], ACT.Exp)
                    nc.scalar.activation(top2[:], top2[:], ACT.Exp).then_inc(exp_done, 1)

                @block.vector
                def _(dve):
                    V = nc.vector
                    dve.wait_ge(small_loaded, 32)
                    V.tensor_scalar(rw[:, 0], rw32[:], WS, None, ALU.mult)
                    dve.drain()
                    V.scalar_tensor_tensor(rw[:, 1], rw32[:], WS, rw[:, 0], ALU.mult, ALU.subtract)\
                     .then_inc(rw_split, 1)

                    def step(item):
                        if m := item(0):
                            r = slice(0, m.rows)
                            dve.wait_ge(bn_done, m.k + 1)
                            if m.after(RING):
                                dve.wait_ge(x1_stored[m.i], m.loads - 16)
                            V.scalar_tensor_tensor(norm.x[m.i][r, :], act_in[m.i2][r, :], 0.0, x_in[m.i][r, :],
                                                   ALU.max, ALU.add).then_inc(x1_done, 1)
                            dve.drain()
                            norm.var(dve, m)
                        if m := item(1):
                            norm.scale(dve, m)
                        if m := item(2):
                            norm.lo(dve, m)

                    pipeline(dve, NB, 2, step)

                    dve.wait_ge(logits_done, NB)
                    wide = lambda t: t[:].unsqueeze(2).to_broadcast([P, NB, NE])
                    per_expert = lambda t: t[:].unsqueeze(1).to_broadcast([P, NB, NE])
                    V.scalar_tensor_tensor(logits[:], logits[:], 1.0 / WS, per_expert(rb), ALU.mult, ALU.add)
                    dve.drain()
                    V.tensor_reduce(top1[:], logits[:], AX.X, ALU.max)
                    dve.drain()
                    V.tensor_tensor(t1[:], logits[:], wide(top1), ALU.subtract)
                    V.tensor_tensor(hot1[:], logits[:], wide(top1), ALU.is_equal)
                    dve.drain()
                    V.tensor_tensor(t2[:], hot1[:], per_expert(less), ALU.mult)
                    dve.drain()
                    V.tensor_reduce(mx[:], t2[:], AX.X, ALU.max)
                    dve.drain()
                    V.tensor_tensor(hot1[:], t2[:], wide(mx), ALU.is_equal)
                    dve.drain()
                    V.scalar_tensor_tensor(logits[:], hot1[:], -1e30, logits[:], ALU.mult, ALU.add)
                    dve.drain()
                    V.tensor_reduce(top2[:], logits[:], AX.X, ALU.max)
                    dve.drain()
                    V.tensor_tensor(hot2[:], logits[:], wide(top2), ALU.is_equal)
                    dve.drain()
                    V.tensor_tensor(t2[:], hot2[:], per_expert(less), ALU.mult)
                    V.tensor_tensor(top2[:], top2[:], top1[:], ALU.subtract).then_inc(shifted, 1)
                    dve.drain()
                    V.tensor_reduce(mx[:], t2[:], AX.X, ALU.max)
                    dve.drain()
                    V.tensor_tensor(hot2[:], t2[:], wide(mx), ALU.is_equal).then_inc(hots_done, 1)
                    dve.wait_ge(exp_done, 1)
                    V.tensor_reduce(den[:], t1[:], AX.X, ALU.add)
                    dve.drain()
                    V.reciprocal(top1[:], den[:])
                    dve.drain()
                    V.tensor_tensor(top2[:], top2[:], top1[:], ALU.mult)
                    dve.drain()
                    V.scalar_tensor_tensor(den[:], top1[:], 1e-9, top2[:], ALU.add, ALU.add)
                    dve.drain()
                    V.reciprocal(mx[:], den[:])
                    dve.drain()
                    V.tensor_tensor(share[:, :, 0], top1[:], mx[:], ALU.mult)
                    V.tensor_tensor(share[:, :, 1], top2[:], mx[:], ALU.mult)
                    dve.wait_ge(hot_masked, 2)
                    V.tensor_tensor(hot[:], hot1[:], hot2[:], ALU.add).then_inc(hot_sent, 1)
                    dve.wait_ge(ranked, 1)
                    blocks = lambda t: t[:, 0:NB * NE].rearrange("p (b e) -> p b e", e=NE)
                    V.tensor_copy(run1[:], blocks(all_ps))
                    dve.drain()
                    a, b, s = run1, run2, 1
                    while s < NB:
                        V.tensor_copy(b[:, 0:s, :], a[:, 0:s, :])
                        V.tensor_tensor(b[:, s:NB, :], a[:, s:NB, :], a[:, 0:NB - s, :], ALU.add)
                        dve.drain()
                        a, b, s = b, a, 2 * s
                    V.tensor_scalar(tiles_i[:], a[:, NB - 1, :], float(P - 1), None, ALU.add)
                    dve.drain()
                    V.tensor_scalar(tiles_i[:], tiles_i[:], P.bit_length() - 1, None, ALU.logical_shift_right)
                    dve.drain()
                    V.tensor_copy(tiles[:], tiles_i[:])
                    V.tensor_copy(end1[:], tiles_i[:])
                    dve.drain()
                    u, v, s = end1, end2, 1
                    while s < NE:
                        V.tensor_copy(v[:, 0:s], u[:, 0:s])
                        V.tensor_tensor(v[:, s:NE], u[:, s:NE], u[:, 0:NE - s], ALU.add)
                        dve.drain()
                        u, v, s = v, u, 2 * s
                    V.tensor_tensor(v[:], u[:], tiles[:], ALU.subtract)
                    dve.drain()
                    V.tensor_scalar(tiles[:], v[:], float(P), None, ALU.mult)
                    dve.drain()
                    V.tensor_tensor(base[:], a[:], blocks(all_ps), ALU.subtract)
                    dve.drain()
                    V.tensor_tensor(base[:], base[:], blocks(in_ps), ALU.add)
                    dve.drain()
                    V.tensor_tensor(base[:], base[:], per_expert(tiles), ALU.add)
                    dve.drain()
                    V.tensor_tensor(t1[:], base[:], hot1[:], ALU.mult)
                    V.tensor_tensor(t2[:], base[:], hot2[:], ALU.mult)
                    dve.drain()
                    V.tensor_reduce(top1[:], t1[:], AX.X, ALU.add)
                    V.tensor_reduce(top2[:], t2[:], AX.X, ALU.add)
                    dve.drain()
                    V.tensor_copy(place[:, :, 0], top1[:])
                    V.tensor_copy(place[:, :, 1], top2[:])
                    V.memset(slot_of[:], 0.0)
                    dve.drain()
                    for e in range(NE - 1):
                        V.scalar_tensor_tensor(slot_of[:], slot_iota[:], u[0:1, e:e + 1], slot_of[:],
                                               ALU.is_ge, ALU.add)
                        dve.drain()
                    V.tensor_copy(tile_expert[:], slot_of[:, 0:NS])

        def late():
            at = ExitStack()
            with at:
                w_gu = [sb(f"w_gu{n}", [P, 2, KC, FF], f16, at) for n in range(2)]
                w_dn = sb("w_dn", [P, 2, FT, D], f16, at)
                w_cv = sb("w_cv", [P, 2, KC, D], f16, at)
                expert_layer(w_gu, w_dn, w_cv)
                if upto >= 5:
                    graph_and_gated(w_gu, w_dn, w_cv)

        def expert_layer(w_gu, w_dn, w_cv):
            at = ExitStack()
            with at:
                w1_sb = sb("w1_sb", [P, 2, KC, NE, FE], f16, at)
                w2_sb = sb("w2_sb", [P, 2, FC, NE, D], f16, at)
                item_token = sb("item_token", [P, NS], i32, at)
                dispatch(w_gu, w_dn, w_cv, w1_sb, w2_sb, item_token)
                experts(w1_sb, w2_sb, item_token)
            combine()

        def dispatch(w_gu, w_dn, w_cv, w1_sb, w2_sb, item_token):
            at = ExitStack()
            with at:
                FP = -(-FT // 2)
                pieces = [(n, f0, min(FP, FT - f0)) for n in range(3) for f0 in (0, FP)]
                raw = [sb(f"raw{i}", [P, FP * KC, P], f32, at) for i in range(2)]
                w_in = [sb(f"w_in{i}", [P, KC * FE], f32, at) for i in range(2)]
                size = sb("size", [P, FP * KC], f32, at)
                inv_size = sb("inv_size", [P, FP * KC], f32, at)
                of = [sb(f"of{i}", [P, 3], i32, at) for i in range(RING)]
                no_token = sb("no_token", [NS, P], i32, at)
                slot_token = sb("slot_token", [NS, P], i32, at)
                slot_token32 = sb("slot_token32", [NS, P], f32, at)
                t_ps = [pb(f"t_ps{i}", [P, KC, P], f32, at) for i in range(2)]
                token_ps = pb("token_ps", [P, 512], f32, at)

                no_token_set = sem("no_token_set", at)
                tokens_cleared = sem("tokens_cleared", at)
                of_set = sem("of_set", at)
                of_seen = sem("of_seen", at)
                scattered = [sem(f"scattered{i}", at) for i in range(RING)]
                tokens_loaded = sem("tokens_loaded", at)
                tokens_f32 = sem("tokens_f32", at)
                tokens_turned = sem("tokens_turned", at)
                w_loaded = [sem(f"ew_loaded{i}", at) for i in range(2)]
                w_hi = sem("ew_hi", at)
                w_lo = sem("ew_lo", at)
                raw_loaded = [sem(f"raw_loaded{i}", at) for i in range(2)]
                rounded = sem("rounded", at)
                t_turned = sem("t_turned", at)
                t_hi = sem("t_hi", at)
                t_lo = sem("t_lo", at)
                block = at.enter_context(nc.Block())

                plain = [part for e in range(NE) for part in
                         ((w1[e], KC, w1_sb, lambda t, p, e=e: t[:, p, :, e, :]),
                          (w2[e], FC, w2_sb, lambda t, p, e=e: t[:, p, :, e, :]))]
                plain += [(W_g[h * D // 2:(h + 1) * D // 2, :], KC // 2, w_cv,
                           lambda t, p, h=h: t[:, p, h * KC // 2:(h + 1) * KC // 2, :]) for h in range(2)]

                def plain_in(n):
                    return w_in[n % 2][:].rearrange("p (c f) -> p c f", c=plain[n][1])

                def plain_out(n, part):
                    _, _, t, view = plain[n]
                    return view(t, part)

                units = [(q, f) for q, (_, _, nf) in enumerate(pieces) for f in range(nf)]

                def units_to(q):
                    return sum(nf for _, _, nf in pieces[:q + 1])

                def piece(q):
                    return raw[q % 2][:, 0:pieces[q][2] * KC, :]

                def group(q, f, c):
                    n, _, nf = pieces[q]
                    return raw[q % 2][:, f * KC + c if n < 2 else c * nf + f, :]

                def unit_out(q, f, part):
                    n, f0, _ = pieces[q]
                    if n < 2:
                        return w_gu[n][:, part, :, (f0 + f) * P:(f0 + f + 1) * P]
                    return w_dn[:, part, f0 + f, :].rearrange("p (c o) -> p c o", c=KC)

                PER = -(-len(plain) // len(pieces))

                @block.sync
                def _(sp):
                    sp.wait_ge(no_token_set, 1)
                    sp.dma_start(slot_token_d.rearrange("(s p) o -> s (p o)", p=P), no_token[:])\
                      .then_inc(tokens_cleared, 16)

                    def load_piece(q):
                        if q >= 2:
                            sp.wait_ge(t_turned, units_to(q - 2))
                        n, f0, nf = pieces[q]
                        if n < 2:
                            to = piece(q).rearrange("p (f c) k -> p f (c k)", f=nf)
                            part = (w_gate, w_up)[n][f0 * P:(f0 + nf) * P, :].rearrange("(f p) k -> p f k", p=P)
                        else:
                            to = piece(q).rearrange("p (c f) k -> p c (f k)", c=KC)
                            part = w_down[:, f0 * P:(f0 + nf) * P].rearrange("(c p) k -> p c k", p=P)
                        sp.dma_start(to, part).then_inc(raw_loaded[q % 2], 16)

                    load_piece(0)
                    load_piece(1)
                    for n in range(len(plain)):
                        if n >= 2:
                            sp.wait_ge(w_hi, n - 1)
                            sp.wait_ge(w_lo, n - 1)
                        sp.dma_start(plain_in(n), plain[n][0].rearrange("(c p) f -> p c f", p=P))                          .then_inc(w_loaded[n % 2], 16)
                        if n % PER == 1 and n > 1 and n // PER + 1 < len(pieces):
                            load_piece(n // PER + 1)
                    for i in range(RING):
                        sp.wait_ge(scattered[i], 32 * ring_uses(i, NB))
                    sp.dma_start(slot_token[:], slot_token_d.rearrange("(s p) o -> s (p o)", p=P))\
                      .then_inc(tokens_loaded, 16)

                @block.gpsimd
                def _(pool):
                    nc.gpsimd.memset(no_token[:], 0).then_inc(no_token_set, 1)
                    pool.wait_ge(tokens_cleared, 16)

                    def step(item):
                        if m := item(0):
                            if m.after(RING):
                                pool.wait_ge(scattered[m.i], m.loads * 2 - 32)
                            nc.gpsimd.tensor_copy(of[m.i][:], place[:, m.k, :]).then_inc(of_set, 1)
                        if m := item(1):
                            pool.wait_ge(of_set, m.k + 1)
                            pool.sem_inc(of_seen, 1)
                            for n in range(2):
                                pool.indirect_dma_start(
                                    out=slot_token_d, in_=of[m.i][0:m.rows, 2:3], in_offset=None,
                                    out_offset=bass.IndirectOffsetOnAxis(ap=of[m.i][0:m.rows, n:n + 1], axis=0),
                                ).then_inc(scattered[m.i], 16)

                    pipeline(pool, NB, 1, step)

                @block.tensor
                def _(pe):
                    for k, (q, f) in enumerate(units):
                        pe.wait_ge(rounded, q + 1)
                        if k >= 2:
                            pe.wait_ge(t_hi, k - 1)
                            pe.wait_ge(t_lo, k - 1)
                        for c in range(KC):
                            last = nc.tensor.transpose(t_ps[k % 2][:, c, :], group(q, f, c), ident32[:])
                        last.then_inc(t_turned, 1)
                    pe.wait_ge(tokens_f32, 1)
                    nc.tensor.transpose(token_ps[:, 0:NS], slot_token32[:], ident32[0:NS, 0:NS])\
                      .then_inc(tokens_turned, 1)

                @block.scalar
                def _(act):
                    for q in range(len(pieces)):
                        for n in range(q * PER, min((q + 1) * PER, len(plain))):
                            act.wait_ge(w_loaded[n % 2], 16 * (n // 2 + 1))
                            nc.scalar.activation(plain_out(n, 0), plain_in(n), ACT.Copy, scale=WS).then_inc(w_hi, 1)
                        for k, (of_piece, f) in enumerate(units):
                            if of_piece == q:
                                act.wait_ge(t_turned, k + 1)
                                nc.scalar.activation(unit_out(q, f, 0), t_ps[k % 2][:], ACT.Copy, scale=WS)\
                                  .then_inc(t_hi, 1)

                @block.vector
                def _(dve):
                    V = nc.vector
                    MAGIC = 1.5 * 2.0 ** 23

                    for q, (_, _, nf) in enumerate(pieces):
                        w, g = piece(q), slice(0, nf * KC)
                        wide = lambda t: t[:, g].unsqueeze(2).to_broadcast([P, nf * KC, P])
                        dve.wait_ge(raw_loaded[q % 2], 16 * (q // 2 + 1))
                        V.tensor_reduce(size[:, g], w, AX.X, ALU.add, apply_absolute_value=True)
                        dve.drain()
                        V.tensor_scalar(size[:, g], size[:, g], 1.0 / P, EPS, ALU.mult, ALU.add)
                        dve.drain()
                        V.reciprocal(inv_size[:, g], size[:, g])
                        dve.drain()
                        V.tensor_tensor(w, w, wide(inv_size), ALU.mult)
                        dve.drain()
                        V.tensor_scalar(w, w, -1.0, 1.0, ALU.max, ALU.min)
                        dve.drain()
                        V.tensor_scalar(w, w, MAGIC, MAGIC, ALU.add, ALU.subtract)
                        dve.drain()
                        V.tensor_tensor(w, w, wide(size), ALU.mult).then_inc(rounded, 1)
                        for n in range(q * PER, min((q + 1) * PER, len(plain))):
                            dve.wait_ge(w_hi, n + 1)
                            V.scalar_tensor_tensor(plain_out(n, 1), plain_in(n), WS, plain_out(n, 0), ALU.mult,
                                                   ALU.subtract).then_inc(w_lo, 1)
                        for k, (of_piece, f) in enumerate(units):
                            if of_piece == q:
                                dve.wait_ge(t_hi, k + 1)
                                V.scalar_tensor_tensor(unit_out(q, f, 1), t_ps[k % 2][:], WS, unit_out(q, f, 0),
                                                       ALU.mult, ALU.subtract).then_inc(t_lo, 1)
                        dve.drain()
                    dve.wait_ge(tokens_loaded, 16)
                    V.tensor_copy(slot_token32[:], slot_token[:]).then_inc(tokens_f32, 1)
                    dve.wait_ge(tokens_turned, 1)
                    V.tensor_copy(item_token[:], token_ps[:, 0:NS])

        def experts(w1_sb, w2_sb, item_token):
            at = ExitStack()
            with at:
                b1_sb, b2_sb = sb("b1_sb", [P, NE, FE], f32, at), sb("b2_sb", [P, NE, D], f32, at)
                item_of = [sb(f"item_of{i}", [P, 1], i32, at) for i in range(RING)]
                item_in = [sb(f"item_in{i}", [P, 2 * D], f16, at) for i in range(RING)]
                it_t = [sb(f"it_t{i}", [P, 2, KC, P], f16, at) for i in range(2)]
                u_sb = [sb(f"u_sb{i}", [P, FE], f32, at) for i in range(2)]
                g_sb = [sb(f"g_sb{i}", [P, FE], f32, at) for i in range(2)]
                g_hl = [sb(f"g_hl{i}", [P, 2, FE], f16, at) for i in range(2)]
                g_t = [sb(f"g_t{i}", [P, 2, FC, P], f16, at) for i in range(2)]
                y_sb = [sb(f"y_sb{i}", [P, D], f32, at) for i in range(RING)]
                it_ps = pb("it_ps", [P, 2, KC, P], f16, at)
                u_ps = [pb(f"u_ps{i}", [P, 512], f32, at) for i in range(2)]
                g_ps = [pb(f"g_ps{i}", [P, 2, FC, 2 * P], f16, at) for i in range(2)]
                y_ps = [pb(f"y_ps{i}", [P, D], f32, at) for i in range(2)]

                b_loaded = sem("eb_loaded", at)
                of_set = sem("item_of_set", at)
                of_seen = sem("item_of_seen", at)
                it_loaded = [sem(f"it_loaded{i}", at) for i in range(RING)]
                it_turned = sem("it_turned", at)
                it_t_done = sem("it_t_done", at)
                up_done = sem("up_done", at)
                u_done = sem("u_done", at)
                g_done = sem("g_done", at)
                g_hi = sem("g_hi", at)
                g_lo = sem("g_lo", at)
                g_turned = sem("g_turned", at)
                g_t_done = sem("g_t_done", at)
                down_done = sem("down_done", at)
                y_done = sem("y_done", at)
                y_stored = [sem(f"y_stored{i}", at) for i in range(RING)]
                block = at.enter_context(nc.Block())

                @block.gpsimd
                def _(pool):
                    def step(item):
                        if m := item(0):
                            if m.after(RING):
                                pool.wait_ge(it_turned, m.k - (RING - 1))
                            nc.gpsimd.tensor_copy(item_of[m.i][:], item_token[:, ds(m.k, 1)]).then_inc(of_set, 1)
                        if m := item(1):
                            pool.wait_ge(of_set, m.k + 1)
                            pool.sem_inc(of_seen, 1)
                            pool.indirect_dma_start(
                                out=item_in[m.i][:], out_offset=None, in_=z_d[0:N, :],
                                in_offset=bass.IndirectOffsetOnAxis(ap=item_of[m.i][:], axis=0),
                            ).then_inc(it_loaded[m.i], 16)

                    pipeline(pool, NS, 1, step)

                @block.sync
                def _(sp):
                    sp.dma_start(b1_sb[:], b1.partition_broadcast(P)).then_inc(b_loaded, 16)
                    sp.dma_start(b2_sb[:], b2.partition_broadcast(P)).then_inc(b_loaded, 16)

                    def step(item):
                        if m := item(0):
                            sp.wait_ge(y_done, m.k + 1)
                            sp.dma_start(items_out[ds(m.k * P, P), :], y_sb[m.i][:]).then_inc(y_stored[m.i], 16)

                    pipeline(sp, NS, 0, step)
                    for i in range(RING):
                        sp.wait_ge(y_stored[i], 16 * ring_uses(i, NS))

                @block.tensor
                def _(pe):
                    def expert(k):
                        return pe.value_load(tile_expert[0:1, ds(k, 1)], min_val=0, max_val=NE - 1)

                    def step(item):
                        if m := item(1):
                            e = expert(m.k)
                            pe.wait_ge(it_t_done, m.k + 1)
                            if m.after(2):
                                pe.wait_ge(u_done, m.k - 1)
                            split_product(u_ps[m.i2][:, 0:FE], lambda c, part: it_t[m.i2][:, part, c, :],
                                          lambda c, part: w1_sb[:, part, c, ds(e, 1), :], KC).then_inc(up_done, 1)
                        if m := item(0):
                            pe.wait_ge(it_loaded[m.i], m.loads)
                            if m.after(1):
                                pe.wait_ge(it_t_done, m.k)
                            for part in range(2):
                                for c in range(KC):
                                    last = nc.tensor.transpose(
                                        it_ps[:, part, c, :],
                                        item_in[m.i][:, part * D + c * P:part * D + (c + 1) * P], ident16[:])
                            last.then_inc(it_turned, 1)
                        if m := item(3):
                            e = expert(m.k)
                            pe.wait_ge(g_t_done, m.k + 1)
                            if m.after(2):
                                pe.wait_ge(y_done, m.k - 1)
                            split_product(y_ps[m.i2][:], lambda c, part: g_t[m.i2][:, part, c, :],
                                          lambda c, part: w2_sb[:, part, c, ds(e, 1), :], FC).then_inc(down_done, 1)
                        if m := item(2):
                            pe.wait_ge(g_hi, m.k + 1)
                            pe.wait_ge(g_lo, m.k + 1)
                            if m.after(2):
                                pe.wait_ge(g_t_done, m.k - 1)
                            for part in range(2):
                                for c in range(FC):
                                    last = nc.tensor.transpose(g_ps[m.i2][:, part, c, 0:P],
                                                               g_hl[m.i2][:, part, c * P:(c + 1) * P], ident16[:])
                            last.then_inc(g_turned, 1)

                    pipeline(pe, NS, 3, step)

                @block.scalar
                def _(act):
                    def step(item):
                        if m := item(1):
                            act.wait_ge(u_done, m.k + 1)
                            if m.after(2):
                                act.wait_ge(g_lo, m.k - 1)
                            nc.scalar.activation(g_sb[m.i2][:], u_sb[m.i2][:], ACT.Gelu).then_inc(g_done, 1)
                            if m.after(2):
                                act.wait_ge(g_turned, m.k - 1)
                            act.wait_ge(g_done, m.k + 1)
                            nc.scalar.activation(g_hl[m.i2][:, 0, :], g_sb[m.i2][:], ACT.Copy).then_inc(g_hi, 1)
                        if m := item(0):
                            act.wait_ge(it_turned, m.k + 1)
                            if m.after(2):
                                act.wait_ge(up_done, m.k - 1)
                            nc.scalar.activation(it_t[m.i2][:], it_ps[:], ACT.Copy).then_inc(it_t_done, 1)

                    pipeline(act, NS, 1, step)

                @block.vector
                def _(dve):
                    dve.wait_ge(b_loaded, 32)

                    def expert(k):
                        return dve.value_load(tile_expert[0:1, ds(k, 1)], min_val=0, max_val=NE - 1)

                    def step(item):
                        if m := item(3):
                            dve.wait_ge(g_turned, m.k + 1)
                            nc.vector.tensor_copy(g_t[m.i2][:], g_ps[m.i2][:, :, :, 0:P]).then_inc(g_t_done, 1)
                        if m := item(1):
                            e = expert(m.k)
                            dve.wait_ge(up_done, m.k + 1)
                            if m.after(2):
                                dve.wait_ge(g_done, m.k - 1)
                            nc.vector.scalar_tensor_tensor(u_sb[m.i2][:], u_ps[m.i2][:, 0:FE], 1.0 / WS,
                                                           b1_sb[:, ds(e, 1), :].rearrange("p a f -> p (a f)"),
                                                           ALU.mult, ALU.add).then_inc(u_done, 1)
                        if m := item(4):
                            e = expert(m.k)
                            dve.wait_ge(down_done, m.k + 1)
                            if m.after(RING):
                                dve.wait_ge(y_stored[m.i], m.loads - 16)
                            nc.vector.scalar_tensor_tensor(y_sb[m.i][:], y_ps[m.i2][:], 1.0 / WS,
                                                           b2_sb[:, ds(e, 1), :].rearrange("p a f -> p (a f)"),
                                                           ALU.mult, ALU.add).then_inc(y_done, 1)
                        if m := item(1):
                            dve.wait_ge(g_hi, m.k + 1)
                            nc.vector.tensor_tensor(g_hl[m.i2][:, 1, :], g_sb[m.i2][:], g_hl[m.i2][:, 0, :],
                                                    ALU.subtract).then_inc(g_lo, 1)

                    pipeline(dve, NS, 4, step)

        def combine():
            at = ExitStack()
            with at:
                norm = Norm(at, "n2")
                x1_in = [sb(f"x1_in{i}", [P, D], f32, at) for i in range(RING)]
                y_in = [[sb(f"y_in{i}_{n}", [P, D], f32, at) for n in range(2)] for i in range(RING)]
                places = [sb(f"places{i}", [P, 2], i32, at) for i in range(RING)]
                x1_loaded = [sem(f"x1_loaded{i}", at) for i in range(RING)]
                places_set = sem("places_set", at)
                places_seen = sem("places_seen", at)
                y_gathered = [sem(f"y_gathered{i}", at) for i in range(RING)]
                x2_done = sem("x2_done", at)
                x2_stored = [sem(f"x2_stored{i}", at) for i in range(RING)]
                z_stored = [sem(f"z2_stored{i}", at) for i in range(RING)]
                block = at.enter_context(nc.Block())

                @block.sync
                def _(sp):
                    def step(item):
                        if m := item(0):
                            if m.after(RING):
                                sp.wait_ge(x2_done, m.k - (RING - 1))
                            sp.dma_start(x1_in[m.i][0:m.rows, :], x1_d[ds(m.k * P, m.rows), :])\
                              .then_inc(x1_loaded[m.i], 16)

                    pipeline(sp, NB, 0, step)

                @block.gpsimd
                def _(pool):
                    def step(item):
                        if m := item(0):
                            if m.after(RING):
                                pool.wait_ge(x2_done, m.k - (RING - 1))
                            nc.gpsimd.tensor_copy(places[m.i][:], place[:, m.k, 0:2]).then_inc(places_set, 1)
                        if m := item(1):
                            pool.wait_ge(places_set, m.k + 1)
                            pool.sem_inc(places_seen, 1)
                            for n in range(2):
                                pool.indirect_dma_start(
                                    out=y_in[m.i][n][0:m.rows, :], out_offset=None, in_=items_out,
                                    in_offset=bass.IndirectOffsetOnAxis(ap=places[m.i][0:m.rows, n:n + 1], axis=0),
                                ).then_inc(y_gathered[m.i], 16)

                    pipeline(pool, NB, 1, step)

                @block.scalar
                def _(act):
                    def step(item):
                        if m := item(1):
                            act.wait_ge(x2_done, m.k + 1)
                            act.dma_start(x2_d[ds(m.k * P, m.rows), :], norm.x[m.i][0:m.rows, :])\
                               .then_inc(x2_stored[m.i], 16)
                        if m := item(3):
                            act.wait_ge(norm.lo_done, m.k + 1)
                            act.dma_start(xn3[ds(m.k * P, m.rows), :], norm.hl[m.i][0:m.rows, :])\
                               .then_inc(z_stored[m.i], 16)
                        if m := item(0):
                            norm.std(act, m)
                        if m := item(1):
                            if m.after(RING):
                                act.wait_ge(z_stored[m.i], m.loads - 16)
                            norm.hi(act, m)

                    pipeline(act, NB, 3, step)
                    for i in range(RING):
                        act.wait_ge(x2_stored[i], 16 * ring_uses(i, NB))
                        act.wait_ge(z_stored[i], 16 * ring_uses(i, NB))

                @block.vector
                def _(dve):
                    def step(item):
                        if m := item(0):
                            r = slice(0, m.rows)
                            dve.wait_ge(y_gathered[m.i], m.loads * 2)
                            dve.wait_ge(x1_loaded[m.i], m.loads)
                            if m.after(RING):
                                dve.wait_ge(x2_stored[m.i], m.loads - 16)
                            nc.vector.scalar_tensor_tensor(x1_in[m.i][r, :], y_in[m.i][0][r, :],
                                                           share[r, m.k, 0:1], x1_in[m.i][r, :],
                                                           ALU.mult, ALU.add)
                            dve.drain()
                            nc.vector.scalar_tensor_tensor(norm.x[m.i][r, :], y_in[m.i][1][r, :],
                                                           share[r, m.k, 1:2], x1_in[m.i][r, :],
                                                           ALU.mult, ALU.add).then_inc(x2_done, 1)
                            dve.drain()
                            norm.var(dve, m)
                        if m := item(1):
                            norm.scale(dve, m)
                        if m := item(2):
                            norm.lo(dve, m)

                    pipeline(dve, NB, 2, step)

        def graph_and_gated(w_gu, w_dn, w_cv):
            at = ExitStack()
            with at:
                R = 4
                W = R * P
                NGR = (NB - 1) // R
                edges = Edges(at, True)
                acc_hl = sb("acc_hl", [P, 2, D], f16, at)
                acc_t = sb("acc_t", [P, 2, KC, P], f16, at)
                x2_in = sb("x2_in", [P, D], f32, at)
                conv = sb("conv", [P, D], f32, at)
                x3 = [[sb(f"x3_{p}_{r}", [P, D], f32, at) for r in range(R)] for p in range(2)]
                norm = Norm(at, "n3", 1, [None])
                z_t = [sb(f"z_t3_{p}", [P, 2, KC, W], f16, at) for p in range(2)]
                silu = [sb(f"silu{i}", [P, W], f32, at) for i in range(2)]
                prod = [sb(f"prod{i}", [P, W], f32, at) for i in range(2)]
                h_t = sb("h_t", [P, FT, 2, W], f16, at)
                acc = pb("acc3", [P, D], f32, at)
                turn_ps = pb("turn_ps", [P, 2, KC, P], f16, at)
                conv_ps = pb("conv_ps", [P, D], f32, at)
                gate_ps = [pb(f"gate_ps{i}", [P, W], f32, at) for i in range(2)]
                up_ps = [pb(f"up_ps{i}", [P, W], f32, at) for i in range(2)]
                down_ps = pb("down_ps", [P, D], f32, at)

                acc_ready = sem("acc_ready3", at)
                acc_hi_done = sem("acc_hi_done", at)
                acc_lo_done = sem("acc_lo_done", at)
                acc_turned = sem("acc_turned", at)
                acc_t_done = sem("acc_t_done", at)
                projected = sem("projected", at)
                conv_done = sem("conv_done", at)
                x2_loaded = sem("x2_loaded", at)
                x3_done = sem("x3_done", at)
                z_turned = sem("z_turned", at)
                z_t_done = sem("z_t_done3", at)
                up_ready = sem("up_ready", at)
                silu_done = sem("silu_done", at)
                prod_done = sem("prod_done", at)
                h_hi_done = sem("h_hi_done", at)
                h_lo_done = sem("h_lo_done", at)
                down_ready = sem("down_ready", at)
                out_done = sem("out_done", at)
                out_stored = [[sem(f"out_stored{p}_{r}", at) for r in range(R)] for p in range(2)]
                block = at.enter_context(nc.Block())

                class Step:

                    def __init__(self, g, p, r):
                        self.g, self.p, self.r = g, p, r
                        self.b = g * R + r
                        self.first = isinstance(g, int) and g == 0 and r == 0
                        self.last = isinstance(g, int) and g == NGR
                        self.rows = LAST if self.last else P

                class Gated:

                    def __init__(self, g, p):
                        self.g, self.p = g, p
                        self.last = isinstance(g, int) and g == NGR
                        self.n = 1 if self.last else R
                        self.width = self.n * P
                        self.first = isinstance(g, int) and g == 0
                        self.units = [("up", f) for f in range(FT)] + [("down", r) for r in range(self.n)]

                def program(step, rest):
                    cuts = [(0, 2, 3, 4), (4, 6, 7, 8), (8, 10, 11, 12), (12, 13, 14, 15)]

                    def group(g, p, before):
                        for r in range(R):
                            gated = Gated(g - 1, 1 - p) if before else None
                            c = cuts[r]
                            step(Step(g, p, r), gated,
                                 [gated.units[c[n]:c[n + 1]] if gated else [] for n in range(3)])

                    group(0, 0, False)
                    group(1, 1, True)
                    group(2, 0, True)
                    with nc_engine[0].Fori(3, NGR - 1, 2) as n:
                        g = n.with_bounds(min_val=3, max_val=NGR - 3)
                        group(g, 1, True)
                        group(g + 1, 0, True)
                    group(NGR - 1, 1, True)
                    gated = Gated(NGR - 1, 1)
                    step(Step(NGR, 0, 0), gated, [gated.units[0:6], gated.units[6:11], gated.units[11:]])
                    rest(Gated(NGR, 0))

                nc_engine = [None]
                assert NGR % 2 == 0 and NB - 1 == NGR * R

                def waits_unit(t, f):
                    return f - 2 if f >= 2 else -1 - f

                @block.gpsimd
                def _(pool):
                    edges.gather(pool, 0, xn3[0:N, :])
                    with pool.Fori(1, NB) as b:
                        edges.gather(pool, b, xn3[0:N, :])

                @block.sync
                def _(sp):
                    edges.load(sp, 0)
                    with sp.Fori(1, NB) as b:
                        edges.load(sp, b)

                @block.tensor
                def _(pe):
                    pe.sem_inc(edges.summed, 2)
                    nc_engine[0] = pe

                    def unit(t, kind, n):
                        if kind == "up":
                            if n == 0:
                                pe.wait_ge(z_t_done, t.g * R + t.n)
                            if not t.first or n >= 2:
                                pe.wait_ge(prod_done, t.g * FT + (waits_unit(t, n) + 1))
                            for ps, w in ((gate_ps, w_gu[0]), (up_ps, w_gu[1])):
                                last = split_product(ps[n % 2][:, 0:t.width],
                                                     lambda c, part: w[:, part, c, n * P:(n + 1) * P],
                                                     lambda c, part: z_t[t.p][:, part, c, 0:t.width], KC)
                            last.then_inc(up_ready, 1)
                        else:
                            pe.wait_ge(h_lo_done, t.g * FT + FT)
                            if not t.first or n >= 1:
                                pe.wait_ge(out_done, t.g * R + n)
                            split_product(down_ps[:], lambda c, part: h_t[:, c, part, n * P:(n + 1) * P],
                                          lambda c, part: w_dn[:, part, c, :], FT).then_inc(down_ready, 1)

                    def step(s, gated, parts):
                        edges.sum(pe, s.b, acc, None)
                        nc.tensor.matmul(acc[:, 0:1], zeros16[:, 0:P], zeros16[:, 0:1], start=False, stop=True,
                                         skip_group_check=True).then_inc(acc_ready, 1)
                        for u in parts[0]:
                            unit(gated, *u)
                        pe.wait_ge(acc_hi_done, s.b + 1)
                        pe.wait_ge(acc_lo_done, s.b + 1)
                        if not s.first:
                            pe.wait_ge(z_t_done, s.b)
                        for part in range(2):
                            for c in range(KC):
                                last = nc.tensor.transpose(turn_ps[:, part, c, :],
                                                           acc_hl[:, part, c * P:(c + 1) * P], ident16[:])
                        last.then_inc(acc_turned, 1)
                        for u in parts[1]:
                            unit(gated, *u)
                        pe.wait_ge(acc_t_done, s.b + 1)
                        if not s.first:
                            pe.wait_ge(conv_done, s.b)
                        split_product(conv_ps[:], lambda c, part: acc_t[:, part, c, :],
                                      lambda c, part: w_cv[:, part, c, :], KC).then_inc(projected, 1)
                        for u in parts[2]:
                            unit(gated, *u)
                        pe.wait_ge(norm.hi_done, s.b + 1)
                        pe.wait_ge(norm.lo_done, s.b + 1)
                        for part in range(2):
                            for c in range(KC):
                                last = nc.tensor.transpose(turn_ps[:, part, c, :],
                                                           norm.hl[0][:, part * D + c * P:part * D + (c + 1) * P],
                                                           ident16[:])
                        last.then_inc(z_turned, 1)

                    def rest(gated):
                        for u in gated.units:
                            unit(gated, *u)

                    program(step, rest)

                class Whole:

                    def __init__(self, b):
                        self.k, self.i, self.rows = b, 0, P

                @block.scalar
                def _(act):
                    nc_engine[0] = act

                    def unit(t, kind, n):
                        if kind == "up":
                            act.wait_ge(up_ready, t.g * FT + (n + 1))
                            nc.scalar.activation(silu[n % 2][:, 0:t.width], gate_ps[n % 2][:, 0:t.width], ACT.Silu,
                                                 scale=1.0 / WS).then_inc(silu_done, 1)
                            act.wait_ge(prod_done, t.g * FT + (n + 1))
                            nc.scalar.activation(h_t[:, n, 0, 0:t.width], prod[n % 2][:, 0:t.width], ACT.Copy)\
                              .then_inc(h_hi_done, 1)
                        else:
                            act.wait_ge(out_done, t.g * R + (n + 1))
                            rows = LAST if t.last else P
                            act.dma_start(out[ds(t.g * W + n * P, rows), :], x3[t.p][n][0:rows, :])\
                               .then_inc(out_stored[t.p][n], 16)

                    def step(s, gated, parts):
                        if not s.first:
                            act.wait_ge(x3_done, s.b)
                        act.dma_start(x2_in[0:s.rows, :], x2_d[ds(s.b * P, s.rows), :]).then_inc(x2_loaded, 16)
                        act.wait_ge(acc_ready, s.b + 1)
                        nc.scalar.activation(acc_hl[:, 0, :], acc[:], ACT.Copy).then_inc(acc_hi_done, 1)
                        for u in parts[0]:
                            unit(gated, *u)
                        act.wait_ge(acc_turned, s.b + 1)
                        nc.scalar.activation(acc_t[:], turn_ps[:], ACT.Copy).then_inc(acc_t_done, 1)
                        for u in parts[1]:
                            unit(gated, *u)
                        act.wait_ge(projected, s.b + 1)
                        nc.scalar.activation(conv[:], conv_ps[:], ACT.Relu, scale=1.0 / WS).then_inc(conv_done, 1)
                        m = Whole(s.b)
                        norm.std(act, m)
                        norm.hi(act, m)
                        for u in parts[2]:
                            unit(gated, *u)
                        act.wait_ge(z_turned, s.b + 1)
                        nc.scalar.activation(z_t[s.p][:, :, :, s.r * P:(s.r + 1) * P], turn_ps[:], ACT.Copy)\
                          .then_inc(z_t_done, 1)

                    def rest(gated):
                        for u in gated.units:
                            unit(gated, *u)
                        for p in range(2):
                            for r in range(R):
                                stores = NGR // 2 + (p == 0 and r == 0)
                                act.wait_ge(out_stored[p][r], 16 * stores)

                    program(step, rest)

                @block.vector
                def _(dve):
                    nc_engine[0] = dve

                    def unit(t, kind, n):
                        if kind == "up":
                            dve.wait_ge(silu_done, t.g * FT + (n + 1))
                            if not t.first or n >= 2:
                                dve.wait_ge(h_hi_done, t.g * FT + (waits_unit(t, n) + 1))
                            nc.vector.scalar_tensor_tensor(prod[n % 2][:, 0:t.width], up_ps[n % 2][:, 0:t.width],
                                                           1.0 / WS, silu[n % 2][:, 0:t.width], ALU.mult, ALU.mult)\
                              .then_inc(prod_done, 1)
                            dve.wait_ge(h_hi_done, t.g * FT + (n + 1))
                            nc.vector.tensor_tensor(h_t[:, n, 1, 0:t.width], prod[n % 2][:, 0:t.width],
                                                    h_t[:, n, 0, 0:t.width], ALU.subtract).then_inc(h_lo_done, 1)
                        else:
                            dve.wait_ge(down_ready, t.g * R + (n + 1))
                            nc.vector.scalar_tensor_tensor(x3[t.p][n][:], down_ps[:], 1.0 / WS, x3[t.p][n][:],
                                                           ALU.mult, ALU.add).then_inc(out_done, 1)

                    nc.vector.memset(edges.first_node[:], 0.0)
                    dve.drain()
                    edges.masks_first(dve, 0)

                    def step(s, gated, parts):
                        edges.masks_rest(dve, s.b)
                        dve.wait_ge(acc_hi_done, s.b + 1)
                        nc.vector.tensor_tensor(acc_hl[:, 1, :], acc[:], acc_hl[:, 0, :], ALU.subtract)\
                          .then_inc(acc_lo_done, 1)
                        if not s.last:
                            edges.masks_first(dve, s.b + 1)
                        for u in parts[0] + parts[1]:
                            unit(gated, *u)
                        dve.wait_ge(conv_done, s.b + 1)
                        dve.wait_ge(x2_loaded, s.b * 16 + 16)
                        if not isinstance(s.g, int) or s.g >= 2:
                            dve.wait_ge(out_stored[s.p][s.r], (s.g - s.p) * 8)
                        norm.x[0] = x3[s.p][s.r]
                        nc.vector.tensor_tensor(x3[s.p][s.r][:], conv[:], x2_in[:], ALU.add).then_inc(x3_done, 1)
                        dve.drain()
                        m = Whole(s.b)
                        norm.var(dve, m)
                        norm.scale(dve, m)
                        norm.lo(dve, m)
                        for u in parts[2]:
                            unit(gated, *u)

                    def rest(gated):
                        for u in gated.units:
                            unit(gated, *u)

                    program(step, rest)

        layer0()
        if upto >= 3:
            late()


_INS = ['x', 'src', 'dst', 'edge_weight', 'L0_gnn_W_l', 'L0_gnn_b_l', 'L0_gnn_W_r', 'L0_gnn_gamma', 'L0_gnn_beta',
        'L0_ffn_router_w', 'L0_ffn_router_b', 'L0_ffn_w1', 'L0_ffn_b1', 'L0_ffn_w2', 'L0_ffn_b2',
        'L1_gnn_weight', 'L1_ffn_w_gate', 'L1_ffn_w_up', 'L1_ffn_w_down']


def kernel(**inputs):
    import numpy as _np
    import concourse.bacc as _bacc
    from concourse import mybir as _mybir
    from concourse.bass_utils import run_bass_kernel_spmd as _run

    nc = _bacc.Bacc("TRN2", target_bir_lowering=False, num_devices=1)
    arrays, args = {}, []
    for name in _INS:
        a = _np.ascontiguousarray(inputs[name])
        arrays[f"in_{name}"] = a
        args.append(nc.dram_tensor(f"in_{name}", a.shape, _mybir.dt.from_np(a.dtype), kind="ExternalInput").ap())
    shape = inputs['x'].shape
    args.append(nc.dram_tensor("out_0", shape, _mybir.dt.float32, kind="ExternalOutput").ap())
    gnn_kernel(nc, *args)
    r = _run(nc, [arrays], core_ids=[0])
    return r.results[0]["out_0"]
```

```python
import concourse.bass as bass
from concourse import mybir
from contextlib import ExitStack


def gnn_kernel(nc, x, src, dst, edge_weight, W_l, b_l, W_r, gamma, beta, router_w, router_b,
               w1, b1, w2, b2, W_g, w_gate, w_up, w_down, out):
    f32, f16, i32 = mybir.dt.float32, mybir.dt.float16, mybir.dt.int32
    ALU = mybir.AluOpType
    ACT = mybir.ActivationFunctionType
    AX = mybir.AxisListType
    ds = bass.ds

    N, D = x.shape
    E = src.shape[0]
    P = 128
    KC = D // P
    NB = -(-N // P)
    LAST = N - (NB - 1) * P
    NP = NB * P
    NE, _, FE = w1.shape
    FC = FE // P
    FF = w_gate.shape[0]
    FT = FF // P
    EPS = 1e-5
    WS = 256.0

    G = 16
    NG = -(-E // (P * G)) * P
    HT = 9
    HE = HT * P
    CE = 2 * HE
    GPC = CE // G
    EP = NG * G + CE
    MAXCH = -(-NG // GPC)
    BIG = 8192.0
    assert NG < BIG and NB <= 64
    MAGIC = 1.5 * 2.0 ** 23
    SPLIT = 50

    def dram(name, shape, dt):
        return nc.dram_tensor(name, shape, dt, kind="Internal").ap()

    src_p, dst_p = dram("src_p", [EP], i32), dram("dst_p", [EP], i32)
    ew_p = dram("ew_p", [EP], f32)
    group_min, group_max = dram("group_min", [NG], f32), dram("group_max", [NG], f32)
    xn1 = dram("xn1", [NP, 2 * D], f16)
    NS = 2 * N // P + NE
    x1_d, x2_d = dram("x1_d", [NP, D], f32), dram("x2_d", [NP, D], f32)
    z_d, support_d = dram("z_d", [NP, 2 * D], f16), dram("support_d", [NP, D], f32)
    slot_token_d = dram("slot_token_d", [NS * P, 1], i32)
    items_out = dram("items_out", [NS * P, D], f32)

    RING = 4

    class Item:

        def __init__(self, k, i, count):
            self.k, self.i, self.i2 = k, i, i % 2
            self.fixed = isinstance(k, int)
            self.valid = not self.fixed or 0 <= k < count
            self.rows = LAST if self.fixed and k == NB - 1 and count == NB else P
            self.loads = (k - i) * (16 // RING) + 16

        def after(self, n):
            return not self.fixed or self.k >= n

    def ring_uses(i, count):
        return (count + RING - 1 - i) // RING

    def pipeline(eng, count, lag, body):
        lead = RING * (-(-(lag + RING) // RING))
        stop = lead + RING * ((count - 1 - lead) // RING)

        def step(t, i):
            def item(s):
                found = Item(t - s, (i - s) % RING, count)
                return found if found.valid else None
            body(item)

        for t in range(lead):
            step(t, t % RING)
        with eng.Fori(lead, stop, RING) as n:
            t = n.with_bounds(min_val=lead, max_val=stop - RING)
            for i in range(RING):
                step(t + i, i)
        for t in range(stop, count + lag):
            step(t, t % RING)

    ctx = ExitStack()
    with ctx:
        def sb(name, shape, dt, at=ctx):
            return at.enter_context(nc.sbuf_tensor(name, shape, dt))

        def pb(name, shape, dt, at=ctx):
            return at.enter_context(nc.psum_tensor(name, shape, dt))

        def sem(name, at):
            if at not in sems_of:
                sems_of[at] = []

                def release():
                    nc.clear_and_free_semaphores(sems_of[at])
                    nc.all_engine_barrier()

                at.callback(release)
            sems_of[at].append(nc.alloc_semaphore(f"{name}_p{len(sems_of)}"))
            return sems_of[at][-1]

        sems_of = {}

        table = sb("table", [1, 3 * 64], i32)
        ident16 = sb("ident16", [P, P], f16)
        ident32 = sb("ident32", [P, P], f32)
        iota_row = sb("iota_row", [P, P], f32)
        zeros16 = sb("zeros16", [P, D], f16)
        ones_col = sb("ones_col", [P, 1], f16)
        eps_col = sb("eps_col", [P, 1], f32)
        place = sb("place", [P, NB, 3], i32)
        share = sb("share", [P, NB, 2], f32)
        tile_expert = sb("tile_expert", [1, NS], i32)

        class Norm:

            def __init__(self, at, name, buffers=RING, x=None):
                self.x = x or [sb(f"{name}_x{i}", [P, D], f32, at) for i in range(buffers)]
                self.z = [sb(f"{name}_z{i}", [P, D], f32, at) for i in range(buffers)]
                self.hl = [sb(f"{name}_hl{i}", [P, 2 * D], f16, at) for i in range(buffers)]
                self.st6 = [sb(f"{name}_st6_{i}", [P, 6], f32, at) for i in range(buffers)]
                self.mean = [sb(f"{name}_mean{i}", [P, 1], f32, at) for i in range(buffers)]
                self.centred = sem(f"{name}_centred", at)
                self.mv = [sb(f"{name}_mv{i}", [P, 4], f32, at) for i in range(buffers)]
                self.var_done, self.std_done, self.z_done, self.hi_done, self.lo_done = (
                    sem(f"{name}_{n}", at) for n in ("var_done", "std_done", "z_done", "hi_done", "lo_done"))

            def var(self, dve, m):
                r = slice(0, m.rows)
                nc.vector.bn_stats(self.st6[m.i][r, :], self.x[m.i][r, :])
                dve.drain()
                nc.vector.bn_aggr(self.mv[m.i][r, 0:2], self.st6[m.i][r, :]).then_inc(self.var_done, 1)

            def std(self, act, m):
                r = slice(0, m.rows)
                act.wait_ge(self.var_done, m.k + 1)
                nc.scalar.activation(self.mv[m.i][r, 2:3], self.mv[m.i][r, 1:2], ACT.Sqrt, bias=eps_col[r, :])\
                  .then_inc(self.std_done, 1)

            def scale(self, dve, m):
                r = slice(0, m.rows)
                dve.wait_ge(self.std_done, m.k + 1)
                nc.vector.reciprocal(self.mv[m.i][r, 3:4], self.mv[m.i][r, 2:3])
                dve.drain()
                nc.vector.tensor_scalar(self.z[m.i][r, :], self.x[m.i][r, :], self.mv[m.i][r, 0:1],
                                        self.mv[m.i][r, 3:4], ALU.subtract, ALU.mult).then_inc(self.z_done, 1)

            def factors(self, dve, m):
                r = slice(0, m.rows)
                dve.wait_ge(self.std_done, m.k + 1)
                nc.vector.reciprocal(self.mv[m.i][r, 3:4], self.mv[m.i][r, 2:3])
                nc.vector.tensor_scalar(self.mean[m.i][r, :], self.mv[m.i][r, 0:1], -1.0, None, ALU.mult)\
                  .then_inc(self.z_done, 1)

            def centre(self, act, m):
                r = slice(0, m.rows)
                act.wait_ge(self.z_done, m.k + 1)
                nc.scalar.activation(self.z[m.i][r, :], self.x[m.i][r, :], ACT.Identity,
                                     bias=self.mean[m.i][r, :]).then_inc(self.centred, 1)

            def centred_hi(self, act, m):
                r = slice(0, m.rows)
                act.wait_ge(self.centred, m.k + 1)
                nc.scalar.activation(self.hl[m.i][r, 0:D], self.z[m.i][r, :], ACT.Copy,
                                     scale=self.mv[m.i][r, 3:4]).then_inc(self.hi_done, 1)

            def centred_lo(self, dve, m):
                r = slice(0, m.rows)
                dve.wait_ge(self.hi_done, m.k + 1)
                nc.vector.scalar_tensor_tensor(self.hl[m.i][r, D:2 * D], self.z[m.i][r, :], self.mv[m.i][r, 3:4],
                                               self.hl[m.i][r, 0:D], ALU.mult, ALU.subtract)\
                  .then_inc(self.lo_done, 1)

            def hi(self, act, m):
                r = slice(0, m.rows)
                act.wait_ge(self.z_done, m.k + 1)
                nc.scalar.activation(self.hl[m.i][r, 0:D], self.z[m.i][r, :], ACT.Copy).then_inc(self.hi_done, 1)

            def lo(self, dve, m):
                r = slice(0, m.rows)
                dve.wait_ge(self.hi_done, m.k + 1)
                nc.vector.tensor_tensor(self.hl[m.i][r, D:2 * D], self.z[m.i][r, :], self.hl[m.i][r, 0:D],
                                        ALU.subtract).then_inc(self.lo_done, 1)

        def layer0():
            ph = ExitStack()
            with ph:
                bn_scale, bn_shift = sb("bn_scale", [P, D], f32, ph), sb("bn_shift", [P, D], f32, ph)
                wlr = sb("wlr", [P, 2 * KC, 2, D], f16, ph)
                prepare(wlr)
                h_all = sb("h_all", [P, NB, D], f32, ph)
                sage(wlr, h_all, bn_scale, bn_shift)
                route(h_all, bn_scale, bn_shift)

        def prepare(wlr):
            p1 = ExitStack()
            with p1:
                pad_0 = sb("pad_0", [SPLIT, (EP - E) // SPLIT], i32, p1)
                pad_d = sb("pad_d", [SPLIT, (EP - E) // SPLIT], i32, p1)
                dst_all = sb("dst_all", [P, NG * G // P], i32, p1)
                gmin = sb("gmin", [P, NG // P], f32, p1)
                gmax = sb("gmax", [P, NG // P], f32, p1)
                gmin_all = sb("gmin_all", [P, NG // 2], f32, p1)
                gmax_all = sb("gmax_all", [P, NG // 2], f32, p1)
                g_iota = sb("g_iota", [P, NG // 2], f32, p1)
                g_back = sb("g_back", [P, NG // 2], f32, p1)
                win = sb("win", [P, 4], f32, p1)
                ends = sb("ends", [1, 4, 64], f32, p1)
                chunks_of = [sb(f"chunks_of{i}", [1, 64], f32, p1) for i in range(3)]
                wnat = sb("wnat", [P, 2, KC, D], f32, p1)
                zpad = sb("zpad", [32, 2 * D], f16, p1)
                tab_ps = pb("tab_ps", [1, 512], f32, p1)
                WB = 6
                w_ps = [pb(f"w_ps{i}", [P, D], f32, p1) for i in range(WB)]

                pads_set = sem("pads_set", p1)
                edges_copied = sem("edges_copied", p1)
                dst_loaded = sem("dst_loaded", p1)
                groups_reduced = sem("groups_reduced", p1)
                groups_stored = sem("groups_stored", p1)
                groups_loaded = sem("groups_loaded", p1)
                pool_zeroed = sem("pool_zeroed", p1)
                consts_set = sem("consts_set", p1)
                hit_ends = sem("hit_ends", p1)
                hits_weighed = sem("hits_weighed", p1)
                hits_found = sem("hits_found", p1)
                ends_turned = sem("ends_turned", p1)
                w_loaded = sem("w_loaded", p1)
                w_turned = sem("w_turned", p1)
                w_hi_done = sem("w_hi_done", p1)
                w_lo_done = sem("w_lo_done", p1)
                pad_stored = sem("pad_stored", p1)
                norm = Norm(p1, "n0")
                x_loaded = [sem(f"x_loaded{i}", p1) for i in range(RING)]
                z_stored = [sem(f"z0_stored{i}", p1) for i in range(RING)]

                block = p1.enter_context(nc.Block())

                APART = RING + 3

                def apart(item):
                    m = item(0)
                    return m and m.fixed and m.k == APART

                @block.gpsimd
                def _(pool):
                    nc.gpsimd.memset(pad_0[:], 0).then_inc(pads_set, 1)
                    nc.gpsimd.memset(pad_d[:], NP).then_inc(pads_set, 1)
                    nc.gpsimd.memset(eps_col[:], EPS).then_inc(pool_zeroed, 1)
                    for a, padded in ((dst, dst_p), (src, src_p), (edge_weight, ew_p)):
                        pool.dma_start(padded[0:E].rearrange("(a b) -> a b", a=SPLIT),
                                       a.rearrange("(a b) -> a b", a=SPLIT)).then_inc(edges_copied, 16)
                    pool.wait_ge(pads_set, 2)
                    for padded, pad in ((src_p, pad_0), (dst_p, pad_d), (ew_p, pad_0)):
                        view = pad[:].bitcast(f32) if padded is ew_p else pad[:]
                        pool.dma_start(padded[E:EP].rearrange("(a b) -> a b", a=SPLIT), view)\
                            .then_inc(edges_copied, 16)
                    for n, w in enumerate((W_l, W_r)):
                        pool.dma_start(wnat[:, n], w.rearrange("(c p) k -> p c k", p=P)).then_inc(w_loaded, 16)
                    nc.gpsimd.memset(zpad[:], 0.0).then_inc(pool_zeroed, 1)
                    nc.gpsimd.memset(ident16[:], 0.0).then_inc(pool_zeroed, 1)
                    nc.gpsimd.memset(ident32[:], 0.0).then_inc(pool_zeroed, 1)
                    nc.gpsimd.memset(zeros16[:], 0.0)
                    nc.gpsimd.memset(ones_col[:], 1.0)
                    pool.wait_ge(pool_zeroed, 4)
                    nc.gpsimd.affine_select(out=ident32[:], in_=ident32[:], compare_op=ALU.not_equal, fill=1.0,
                                            base=0, pattern=[[-1, P]], channel_multiplier=1).then_inc(consts_set, 1)
                    pool.wait_ge(edges_copied, 96)
                    pool.dma_start(dst_all[:], dst_p[0:NG * G].rearrange("(p c) -> p c", p=P))\
                        .then_inc(dst_loaded, 16)
                    pool.dma_start(xn1[N:NP, :], zpad[0:NP - N, :]).then_inc(pad_stored, 16)
                    nc.gpsimd.affine_select(out=ident16[:], in_=ident16[:], compare_op=ALU.not_equal, fill=1.0,
                                            base=0, pattern=[[-1, P]], channel_multiplier=1)
                    nc.gpsimd.iota(iota_row[:], [[1, P]], base=0, channel_multiplier=0,
                                   allow_small_or_imprecise_dtypes=True)
                    nc.gpsimd.iota(win[:, 0:1], [[0, 1]], base=0, channel_multiplier=P,
                                   allow_small_or_imprecise_dtypes=True)
                    nc.gpsimd.iota(g_iota[:], [[1, NG // 2]], base=1, channel_multiplier=0,
                                   allow_small_or_imprecise_dtypes=True)
                    nc.gpsimd.iota(g_back[:], [[-1, NG // 2]], base=int(BIG), channel_multiplier=0,
                                   allow_small_or_imprecise_dtypes=True).then_inc(consts_set, 1)
                    pool.wait_ge(groups_reduced, 2)
                    pool.dma_start(group_min.rearrange("(p c) -> p c", p=P), gmin[:]).then_inc(groups_stored, 16)
                    pool.dma_start(group_max.rearrange("(p c) -> p c", p=P), gmax[:]).then_inc(groups_stored, 16)
                    pool.wait_ge(groups_stored, 32)
                    for a, t in ((group_min, gmin_all), (group_max, gmax_all)):
                        for h in range(2):
                            half = a[h * (NG // 2):(h + 1) * (NG // 2)]
                            pool.dma_start(t[h * 64:(h + 1) * 64, :], half.partition_broadcast(64))\
                                .then_inc(groups_loaded, 16)
                    pool.wait_ge(pad_stored, 16)
                    pool.wait_ge(consts_set, 2)
                    nc.gpsimd.tensor_scalar(win[:, 1:2], win[:, 0:1], 64.0 * P, 64.0 * P, ALU.is_ge, ALU.mult)\
                      .then_inc(hit_ends, 1)
                    pool.wait_ge(hit_ends, 1)
                    nc.gpsimd.tensor_tensor(win[:, 0:1], win[:, 0:1], win[:, 1:2], ALU.subtract).then_inc(hit_ends, 1)
                    pool.wait_ge(hit_ends, 2)
                    nc.gpsimd.tensor_scalar(win[:, 1:2], win[:, 0:1], float(P - 1), None, ALU.add)\
                      .then_inc(hit_ends, 1)
                    pool.wait_ge(groups_loaded, 64)
                    pool.wait_ge(hit_ends, 3)
                    nc.gpsimd.tensor_scalar(gmin_all[:], gmin_all[:], win[:, 1:2], None, ALU.is_le)
                    nc.gpsimd.tensor_scalar(gmax_all[:], gmax_all[:], win[:, 0:1], None, ALU.is_ge)\
                      .then_inc(hit_ends, 1)
                    pool.wait_ge(hit_ends, 4)
                    nc.gpsimd.tensor_tensor(gmax_all[:], gmax_all[:], gmin_all[:], ALU.mult).then_inc(hits_weighed, 1)
                    pool.wait_ge(hits_weighed, 1)
                    nc.gpsimd.tensor_tensor(g_iota[:], g_iota[:], gmax_all[:], ALU.mult).then_inc(hits_weighed, 1)
                    nc.gpsimd.tensor_tensor(g_back[:], g_back[:], gmax_all[:], ALU.mult).then_inc(hits_weighed, 1)

                @block.sync
                def _(sp):
                    def step(item):
                        if m := item(0):
                            if m.after(RING):
                                sp.wait_ge(norm.centred, m.k - (RING - 1))
                            sp.dma_start(norm.x[m.i][0:m.rows, :], x[ds(m.k * P, m.rows), :])\
                              .then_inc(x_loaded[m.i], 16)

                    pipeline(sp, NB, 0, step)

                @block.tensor
                def _(pe):
                    pe.wait_ge(w_loaded, 32)
                    pe.wait_ge(consts_set, 1)
                    for k in range(2 * KC):
                        if k >= WB:
                            pe.wait_ge(w_hi_done, k - WB + 1)
                            pe.wait_ge(w_lo_done, k - WB + 1)
                        for o in range(KC):
                            last = nc.tensor.transpose(w_ps[k % WB][:, o * P:(o + 1) * P],
                                                       wnat[:, k // KC, o, (k % KC) * P:(k % KC + 1) * P],
                                                       ident32[:])
                        last.then_inc(w_turned, 1)
                    pe.wait_ge(hits_found, 1)
                    for n in range(2):
                        last = nc.tensor.matmul(tab_ps[0:1, n * P:(n + 1) * P], win[:, 2 + n:3 + n], ident32[:],
                                                start=True, stop=True)
                    last.then_inc(ends_turned, 1)

                @block.scalar
                def _(act):
                    act.wait_ge(pool_zeroed, 1)

                    def step(item):
                        if m := item(3):
                            act.wait_ge(norm.lo_done, m.k + 1)
                            act.dma_start(xn1[ds(m.k * P, m.rows), :], norm.hl[m.i][0:m.rows, :])\
                               .then_inc(z_stored[m.i], 16)
                        if m := item(1):
                            norm.centre(act, m)
                        if m := item(0):
                            norm.std(act, m)
                        if m := item(1):
                            if m.after(RING):
                                act.wait_ge(z_stored[m.i], m.loads - 16)
                            norm.centred_hi(act, m)
                        if apart(item):
                            for k in range(2 * KC):
                                act.wait_ge(w_turned, k + 1)
                                nc.scalar.activation(wlr[:, k, 0, :], w_ps[k % WB][:], ACT.Copy, scale=WS)\
                                  .then_inc(w_hi_done, 1)

                    pipeline(act, NB, 3, step)
                    for i in range(RING):
                        act.wait_ge(z_stored[i], 16 * ring_uses(i, NB))

                @block.vector
                def _(dve):
                    V = nc.vector

                    def step(item):
                        if m := item(0):
                            dve.wait_ge(x_loaded[m.i], m.loads)
                            norm.var(dve, m)
                        if m := item(1):
                            norm.factors(dve, m)
                        if m := item(2):
                            norm.centred_lo(dve, m)
                        if apart(item):
                            dve.wait_ge(dst_loaded, 16)
                            groups = dst_all[:].rearrange("p (c g) -> p c g", g=G)
                            V.tensor_reduce(gmin[:], groups, AX.X, ALU.min).then_inc(groups_reduced, 1)
                            V.tensor_reduce(gmax[:], groups, AX.X, ALU.max).then_inc(groups_reduced, 1)
                            for k in range(2 * KC):
                                dve.wait_ge(w_hi_done, k + 1)
                                V.scalar_tensor_tensor(wlr[:, k, 1, :], w_ps[k % WB][:], WS, wlr[:, k, 0, :],
                                                       ALU.mult, ALU.subtract).then_inc(w_lo_done, 1)

                    pipeline(dve, NB, 2, step)
                    dve.wait_ge(hits_weighed, 3)
                    V.tensor_reduce(win[:, 2:3], g_iota[:], AX.X, ALU.max)
                    V.tensor_reduce(win[:, 3:4], g_back[:], AX.X, ALU.max).then_inc(hits_found, 1)
                    dve.wait_ge(ends_turned, 1)
                    V.tensor_copy(ends[:].rearrange("p a b -> p (a b)"), tab_ps[:, 0:256])
                    dve.drain()
                    last0, last1, back0, back1 = (ends[:, n, :] for n in range(4))
                    hit, number, length = (chunks_of[n][:] for n in range(3))
                    V.tensor_scalar(hit, last1, 0.0, float(NG // 2), ALU.is_gt, ALU.mult)
                    dve.drain()
                    V.tensor_tensor(last1, last1, hit, ALU.add)
                    V.tensor_tensor(back1, back1, hit, ALU.subtract)
                    dve.drain()
                    V.tensor_tensor(last0, last0, last1, ALU.max)
                    V.tensor_tensor(back0, back0, back1, ALU.max)
                    dve.drain()
                    V.tensor_scalar(back0, back0, -1.0, BIG, ALU.mult, ALU.add)
                    dve.drain()
                    V.tensor_tensor(length, last0, back0, ALU.subtract)
                    V.tensor_scalar(back0, back0, float(NG - 1), float(G), ALU.min, ALU.mult)
                    dve.drain()
                    V.tensor_scalar(length, length, 1.0 / GPC, 0.5 - 0.5 / GPC, ALU.mult, ALU.add)
                    dve.drain()
                    V.tensor_scalar(length, length, 1.0, None, ALU.max)
                    dve.drain()
                    V.tensor_scalar(number, length, MAGIC, MAGIC, ALU.add, ALU.subtract)
                    dve.drain()
                    V.tensor_copy(table[:, 0:64], number)
                    V.tensor_copy(table[:, 128:192], back0)
                    V.tensor_copy(last0, number)
                    dve.drain()
                    a, b, n = last0, last1, 1
                    while n < NB:
                        V.tensor_copy(b[:, 0:n], a[:, 0:n])
                        V.tensor_tensor(b[:, n:64], a[:, n:64], a[:, 0:64 - n], ALU.add)
                        dve.drain()
                        a, b, n = b, a, 2 * n
                    V.tensor_tensor(b, a, number, ALU.subtract)
                    dve.drain()
                    V.tensor_copy(table[:, 64:128], b)

        class Edges:

            def __init__(self, at, tag, weighted):
                self.weighted = weighted
                self.idx = [sb(f"{tag}idx{h}", [P, HT], i32, at) for h in range(2)]
                self.tgt = [sb(f"{tag}tgt{h}", [P, HT], i32, at) for h in range(2)]
                self.local = [sb(f"{tag}local{h}", [P, HT], f32, at) for h in range(2)]
                self.first_node = sb(f"{tag}first_node", [P, 1], f32, at)
                if weighted:
                    self.ew = [sb(f"{tag}ew{h}", [P, HT], f32, at) for h in range(2)]
                self.idx_loaded = [sem(f"{tag}idx_loaded{h}", at) for h in range(2)]
                self.tgt_loaded = [sem(f"{tag}tgt_loaded{h}", at) for h in range(2)]
                self.idx_seen = sem(f"{tag}idx_seen", at)

            def first_chunk(self, eng, b):
                q0 = eng.value_load(table[0:1, ds(b + 64, 1)], min_val=0, max_val=NB * MAXCH)
                return q0

            def chunks(self, eng, b, body):
                n = eng.value_load(table[0:1, ds(b, 1)], min_val=1, max_val=MAXCH)
                q0 = self.first_chunk(eng, b)
                with eng.Fori(0, n) as i:
                    body(eng.snap(q0 + i).with_bounds(min_val=0, max_val=NB * MAXCH), i)

            def further_chunks(self, eng, b, body):
                n = eng.value_load(table[0:1, ds(b, 1)], min_val=1, max_val=MAXCH)
                q0 = self.first_chunk(eng, b)
                with eng.If(n > 1):
                    with eng.Fori(1, n) as i:
                        body(eng.snap(q0 + i).with_bounds(min_val=0, max_val=NB * MAXCH))

            def load(self, eng, b, wait_free):
                e0 = eng.value_load(table[0:1, ds(b + 128, 1)], min_val=0, max_val=(NG - 1) * G)

                def chunk(q, i):
                    for h in range(2):
                        wait_free(q, h)
                        at = eng.snap(e0 + i * CE + h * HE).with_bounds(min_val=0, max_val=EP - HE)
                        part = lambda t: t[ds(at, HE)].rearrange("(p j) -> p j", j=HT)
                        eng.dma_start(self.idx[h][:], part(src_p)).then_inc(self.idx_loaded[h], 16)
                        eng.dma_start(self.tgt[h][:], part(dst_p)).then_inc(self.tgt_loaded[h], 16)
                        if self.weighted:
                            eng.dma_start(self.ew[h][:], part(ew_p)).then_inc(self.tgt_loaded[h], 16)

                self.chunks(eng, b, chunk)

            def find_local(self, dve, h):
                nc.vector.tensor_scalar(self.local[h][:], self.tgt[h][:], self.first_node[:], None, ALU.subtract)
                dve.drain()

            def next_block(self, dve):
                dve.drain()
                nc.vector.tensor_scalar(self.first_node[:], self.first_node[:], float(P), None, ALU.add)
                dve.drain()

            def gather_tile(self, eng, rows, rows_of, h, j):
                return eng.indirect_dma_start(
                    out=rows, out_offset=None, in_=rows_of,
                    in_offset=bass.IndirectOffsetOnAxis(ap=self.idx[h][:, j:j + 1], axis=0))

        class PlainSums(Edges):

            def __init__(self, at):
                super().__init__(at, "u_", False)
                self.rows = sb("u_rows", [P, 2 * HT, 2 * D], f16, at)
                self.mask = [sb(f"u_mask{h}", [P, HT, P], f16, at) for h in range(2)]
                self.gathered = [sem(f"u_gathered{j}", at) for j in range(2 * HT)]
                self.masked = sem("u_masked", at)
                self.summed = sem("u_summed", at)

            def load_block(self, eng, b):
                self.load(eng, b, lambda q, h: eng.wait_ge(self.summed, q * 2 + (h + 1)))

            def gather(self, eng, b, rows_of):
                def chunk(q, i):
                    for h in range(2):
                        eng.wait_ge(self.idx_loaded[h], q * 16 + 16)
                        eng.sem_inc(self.idx_seen, 1)
                        for j in range(HT):
                            self.gather_tile(eng, self.rows[:, h * HT + j, :], rows_of, h, j)\
                                .then_inc(self.gathered[h * HT + j], 16)

                self.chunks(eng, b, chunk)

            def masks(self, dve, q):
                for h in range(2):
                    dve.wait_ge(self.tgt_loaded[h], q * 16 + 16)
                    self.find_local(dve, h)
                    for j in range(HT):
                        last = nc.vector.tensor_scalar(self.mask[h][:, j, :], iota_row[:],
                                                       self.local[h][:, j:j + 1], None, ALU.is_equal)
                    last.then_inc(self.masked, 1)

            def first_masks(self, dve, b):
                self.masks(dve, self.first_chunk(dve, b))

            def other_masks(self, dve, b):
                self.further_chunks(dve, b, lambda q: self.masks(dve, q))
                self.next_block(dve)

            def sum(self, pe, b, acc, count):
                nc.tensor.matmul(acc[:], zeros16[:, 0:P], zeros16[:], start=True, stop=False, skip_group_check=True)
                nc.tensor.matmul(count, zeros16[:, 0:P], zeros16[:, 0:1], start=True, stop=False,
                                 skip_group_check=True)

                def add(to, mask, rows):
                    return nc.tensor.matmul(to, mask, rows, start=False, stop=False, skip_group_check=True)

                def chunk(q, i):
                    for h in range(2):
                        pe.wait_ge(self.masked, q * 2 + (h + 1))
                        for j in range(HT):
                            t = h * HT + j
                            pe.wait_ge(self.gathered[t], q * 16 + 16)
                            mask = self.mask[h][:, j, :]
                            add(acc[:], mask, self.rows[:, t, 0:D])
                            add(acc[:], mask, self.rows[:, t, D:2 * D])
                            last = add(count, mask, ones_col[:])
                        last.then_inc(self.summed, 1)

                self.chunks(pe, b, chunk)

        PT = 3
        PARTS = 2 * HT // PT
        SLOTS = 3

        class WeightedSums(Edges):

            def __init__(self, at):
                super().__init__(at, "w_", True)
                self.rows = [sb(f"w_rows{n}", [P, PT, D], f32, at) for n in range(SLOTS)]
                self.scaled = [sb(f"w_scaled{k}", [P, PT, 2, D], f16, at) for k in range(PARTS)]
                self.mask = [sb(f"w_mask{k}", [P, PT, P], f16, at) for k in range(PARTS)]
                self.gathered = [sem(f"w_gathered{j}", at) for j in range(SLOTS * PT)]
                self.scaled_hi = sem("w_scaled_hi", at)
                self.prepared = sem("w_prepared", at)
                self.summed = sem("w_summed", at)
                assert HT % PT == 0 and PARTS % SLOTS == 0

            def place_of(self, k, j):
                return (k * PT + j) // HT, (k * PT + j) % HT

            def load_block(self, eng, b):
                self.load(eng, b, lambda q, h: eng.wait_ge(self.prepared, q * PARTS + (h + 1) * PARTS // 2))

            def gather(self, eng, b, rows_of):
                def chunk(q, i):
                    for k in range(PARTS):
                        h, _ = self.place_of(k, 0)
                        if k * PT % HT == 0:
                            eng.wait_ge(self.idx_loaded[h], q * 16 + 16)
                        eng.wait_ge(self.prepared, q * PARTS + (PARTS + k - SLOTS + 1))
                        eng.sem_inc(self.idx_seen, 1)
                        for j in range(PT):
                            tile = k % SLOTS * PT + j
                            self.gather_tile(eng, self.rows[k % SLOTS][:, j, :], rows_of, *self.place_of(k, j))\
                                .then_inc(self.gathered[tile], 16)

                self.chunks(eng, b, chunk)

            def scale_hi(self, act, q, k):
                h, _ = self.place_of(k, 0)
                n = k % SLOTS
                act.wait_ge(self.tgt_loaded[h], q * 32 + 32)
                act.wait_ge(self.summed, q * PARTS + (k + 1))
                for j in range(PT):
                    h, col = self.place_of(k, j)
                    act.wait_ge(self.gathered[n * PT + j],
                                q * (16 * PARTS // SLOTS) + 16 * (k // SLOTS + 1))
                    last = nc.scalar.activation(self.scaled[k][:, j, 0, :], self.rows[n][:, j, :], ACT.Copy,
                                                scale=self.ew[h][:, col:col + 1])
                last.then_inc(self.scaled_hi, 1)

            def prepare(self, dve, q, k):
                h, _ = self.place_of(k, 0)
                n = k % SLOTS
                if k * PT % HT == 0:
                    dve.wait_ge(self.tgt_loaded[h], q * 32 + 32)
                    self.find_local(dve, h)
                dve.wait_ge(self.summed, q * PARTS + (k + 1))
                for j in range(PT):
                    h, col = self.place_of(k, j)
                    nc.vector.tensor_scalar(self.mask[k][:, j, :], iota_row[:], self.local[h][:, col:col + 1],
                                            None, ALU.is_equal)
                dve.wait_ge(self.scaled_hi, q * PARTS + (k + 1))
                for j in range(PT):
                    h, col = self.place_of(k, j)
                    last = nc.vector.scalar_tensor_tensor(
                        self.scaled[k][:, j, 1, :], self.rows[n][:, j, :], self.ew[h][:, col:col + 1],
                        self.scaled[k][:, j, 0, :], ALU.mult, ALU.subtract)
                last.then_inc(self.prepared, 1)

            def sum_part(self, pe, q, k, acc):
                pe.wait_ge(self.prepared, q * PARTS + (PARTS + k + 1))
                for j in range(PT):
                    for part in range(2):
                        last = nc.tensor.matmul(acc[:], self.mask[k][:, j, :], self.scaled[k][:, j, part, :],
                                                start=False, stop=False, skip_group_check=True)
                last.then_inc(self.summed, 1)

        def split_product(out, left, right, chunks, last_sem=None):
            for c in range(chunks):
                for n, (l, r) in enumerate(((0, 0), (0, 1), (1, 0))):
                    last = nc.tensor.matmul(out, left(c, l), right(c, r), start=(c == 0 and n == 0),
                                            stop=(c == chunks - 1 and n == 2))
            return last

        def sage(wlr, h_all, bn_scale, bn_shift):
            p2 = ExitStack()
            with p2:
                edges = PlainSums(p2)
                own = sb("own", [P, 2 * D], f16, p2)
                mean_hl = sb("mean_hl", [P, 2, D], f16, p2)
                mean_t = sb("mean_t", [P, 2, KC, P], f16, p2)
                own_t = sb("own_t", [P, 2, KC, P], f16, p2)
                inv = sb("inv", [P, 2], f32, p2)
                h_sq = sb("h_sq", [P, D], f32, p2)
                bias = sb("bias", [P, D], f32, p2)
                gam = sb("gam", [P, D], f32, p2)
                bet = sb("bet", [P, D], f32, p2)
                ones32 = sb("ones32", [P, 2, P], f32, p2)
                stat = sb("stat", [P, 3, D], f32, p2)
                acc = pb("acc", [P, D], f32, p2)
                cnt = pb("cnt", [P, D], f32, p2)
                mean_ps = pb("mean_ps", [P, 2, KC, P], f16, p2)
                own_ps = pb("own_ps", [P, 2, KC, P], f16, p2)
                h_ps = pb("h_ps", [P, D], f32, p2)
                sum_ps = pb("sum_ps", [P, D], f32, p2)
                sq_ps = pb("sq_ps", [P, D], f32, p2)

                ones_set = sem("ones_set", p2)
                rows_loaded = sem("rows_loaded", p2)
                own_loaded = sem("own_loaded", p2)
                acc_ready = sem("acc_ready", p2)
                inv_done = sem("inv_done", p2)
                mean_hi_done = sem("mean_hi_done", p2)
                mean_lo_done = sem("mean_lo_done", p2)
                turned = sem("turned", p2)
                mean_t_done = sem("mean_t_done", p2)
                own_t_done = sem("own_t_done", p2)
                h_summed = sem("h_summed", p2)
                h_done = sem("h_done", p2)
                h_sq_done = sem("h_sq_done", p2)
                stats_added = sem("stats_added", p2)
                bn_var = sem("bn_var", p2)
                bn_std = sem("bn_std", p2)

                block = p2.enter_context(nc.Block())

                def each_block(eng, body):
                    body(0)
                    body(1)
                    with eng.Fori(2, NB - 1) as b:
                        body(b)
                    body(NB - 1)

                def h_block(b):
                    return h_all[:, ds(b, 1), :].rearrange("p a d -> p (a d)")

                first = lambda b: isinstance(b, int) and b == 0
                final = lambda b: isinstance(b, int) and b == NB - 1

                @block.gpsimd
                def _(pool):
                    nc.gpsimd.memset(ones32[:], 1.0).then_inc(ones_set, 1)
                    pool.wait_ge(ones_set, 1)
                    nc.gpsimd.affine_select(out=ones32[:, 1, :], in_=ones32[:, 1, :], compare_op=ALU.is_gt,
                                            fill=0.0, base=LAST, pattern=[[0, P]], channel_multiplier=-1)\
                        .then_inc(ones_set, 1)
                    each_block(pool, lambda b: edges.gather(pool, b, xn1))

                @block.sync
                def _(sp):
                    for t, a in ((bias, b_l), (gam, gamma), (bet, beta)):
                        sp.dma_start(t[:], a.partition_broadcast(P)).then_inc(rows_loaded, 16)

                    def step(b):
                        edges.load_block(sp, b)
                        if not first(b):
                            sp.wait_ge(turned, b)
                        sp.dma_start(own[:], xn1[ds(b * P, P), :]).then_inc(own_loaded, 16)

                    each_block(sp, step)

                @block.tensor
                def _(pe):
                    pe.sem_inc(edges.summed, 2)
                    pe.wait_ge(ones_set, 2)
                    for t in (sum_ps, sq_ps):
                        nc.tensor.matmul(t[:], zeros16[:, 0:P], zeros16[:], start=True, stop=False,
                                         skip_group_check=True)

                    def project(b):
                        pe.wait_ge(mean_t_done, b + 1)
                        pe.wait_ge(own_t_done, b + 1)
                        split_product(h_ps[:], lambda c, part: (mean_t if c < KC else own_t)[:, part, c % KC, :],
                                      lambda c, part: wlr[:, c, part, :], 2 * KC).then_inc(h_summed, 1)

                    def turn(b):
                        pe.wait_ge(mean_hi_done, b + 1)
                        pe.wait_ge(mean_lo_done, b + 1)
                        pe.wait_ge(own_loaded, b * 16 + 16)
                        for part in range(2):
                            for c in range(KC):
                                nc.tensor.transpose(mean_ps[:, part, c, :], mean_hl[:, part, c * P:(c + 1) * P],
                                                    ident16[:])
                                last = nc.tensor.transpose(own_ps[:, part, c, :],
                                                           own[:, part * D + c * P:part * D + (c + 1) * P],
                                                           ident16[:])
                        last.then_inc(turned, 1)

                    def add_stats(b, valid):
                        pe.wait_ge(h_done, b + 1)
                        pe.wait_ge(h_sq_done, b + 1)
                        nc.tensor.matmul(sum_ps[:], ones32[:, valid, :], h_block(b), start=False, stop=False,
                                         skip_group_check=True)
                        nc.tensor.matmul(sq_ps[:], ones32[:, valid, :], h_sq[:], start=False, stop=False,
                                         skip_group_check=True).then_inc(stats_added, 1)

                    def step(b):
                        edges.sum(pe, b, acc, cnt[:, 0:1])
                        nc.tensor.matmul(cnt[:, 0:1], zeros16[:, 0:P], zeros16[:, 0:1], start=False, stop=True,
                                         skip_group_check=True).then_inc(acc_ready, 1)
                        if not isinstance(b, int) or b >= 2:
                            add_stats(b - 2, 0)
                        if not first(b):
                            project(b - 1)
                        turn(b)

                    each_block(pe, step)
                    add_stats(NB - 2, 0)
                    project(NB - 1)
                    add_stats(NB - 1, 1)

                @block.scalar
                def _(act):
                    def square(b):
                        act.wait_ge(h_done, b + 1)
                        if not first(b):
                            act.wait_ge(stats_added, b)
                        nc.scalar.activation(h_sq[:], h_block(b), ACT.Square).then_inc(h_sq_done, 1)

                    def step(b):
                        act.wait_ge(inv_done, b + 1)
                        nc.scalar.activation(mean_hl[:, 0, :], acc[:], ACT.Copy, scale=inv[:, 1:2])\
                          .then_inc(mean_hi_done, 1)
                        if not first(b):
                            square(b - 1)
                        act.wait_ge(turned, b + 1)
                        nc.scalar.activation(mean_t[:], mean_ps[:], ACT.Copy).then_inc(mean_t_done, 1)

                    each_block(act, step)
                    square(NB - 1)
                    act.wait_ge(bn_var, 1)
                    nc.scalar.activation(bn_scale[:], stat[:, 1, :], ACT.Sqrt, bias=eps_col[:]).then_inc(bn_std, 1)

                @block.vector
                def _(dve):
                    nc.vector.memset(edges.first_node[:], 0.0)
                    dve.drain()
                    edges.first_masks(dve, 0)
                    dve.wait_ge(rows_loaded, 48)

                    def add_bias(b):
                        dve.wait_ge(h_summed, b + 1)
                        nc.vector.scalar_tensor_tensor(h_block(b), h_ps[:], 1.0 / WS, bias[:], ALU.mult, ALU.add)\
                          .then_inc(h_done, 1)

                    def step(b):
                        edges.other_masks(dve, b)
                        dve.wait_ge(acc_ready, b + 1)
                        nc.vector.tensor_scalar(inv[:, 0:1], cnt[:, 0:1], 1.0, None, ALU.max)
                        dve.drain()
                        nc.vector.reciprocal(inv[:, 1:2], inv[:, 0:1]).then_inc(inv_done, 1)
                        dve.drain()
                        dve.wait_ge(mean_hi_done, b + 1)
                        nc.vector.scalar_tensor_tensor(mean_hl[:, 1, :], acc[:], inv[:, 1:2], mean_hl[:, 0, :],
                                                       ALU.mult, ALU.subtract).then_inc(mean_lo_done, 1)
                        if not final(b):
                            edges.first_masks(dve, b + 1)
                        if not first(b):
                            add_bias(b - 1)
                        dve.wait_ge(turned, b + 1)
                        nc.vector.tensor_copy(own_t[:], own_ps[:]).then_inc(own_t_done, 1)

                    each_block(dve, step)
                    add_bias(NB - 1)
                    dve.wait_ge(stats_added, NB)
                    nc.vector.tensor_scalar(stat[:, 0, :], sum_ps[:], 1.0 / N, None, ALU.mult)
                    dve.drain()
                    nc.vector.tensor_tensor(stat[:, 2, :], stat[:, 0, :], stat[:, 0, :], ALU.mult)
                    dve.drain()
                    nc.vector.scalar_tensor_tensor(stat[:, 1, :], sq_ps[:], 1.0 / N, stat[:, 2, :], ALU.mult,
                                                   ALU.subtract).then_inc(bn_var, 1)
                    dve.wait_ge(bn_std, 1)
                    nc.vector.reciprocal(stat[:, 1, :], bn_scale[:])
                    dve.drain()
                    nc.vector.tensor_tensor(bn_scale[:], stat[:, 1, :], gam[:], ALU.mult)
                    dve.drain()
                    nc.vector.tensor_tensor(stat[:, 2, :], stat[:, 0, :], bn_scale[:], ALU.mult)
                    dve.drain()
                    nc.vector.tensor_tensor(bn_shift[:], bet[:], stat[:, 2, :], ALU.subtract)

        def route(h_all, bn_scale, bn_shift):
            at = ExitStack()
            with at:
                norm = Norm(at, "n1")
                x_in = [sb(f"x_in{i}", [P, D], f32, at) for i in range(RING)]
                act_in = [sb(f"act_in{i}", [P, D], f32, at) for i in range(2)]
                z_t = [sb(f"z_t{i}", [P, 2, KC, P], f16, at) for i in range(2)]
                rw32 = sb("rw32", [P, KC, NE], f32, at)
                rw = sb("rw", [P, 2, KC, NE], f16, at)
                rb = sb("rb", [P, NE], f32, at)
                logits = sb("logits", [P, NB, NE], f32, at)
                less = sb("less", [P, NE], f32, at)
                t1, t2, hot1, hot2, base = (sb(n, [P, NB, NE], f32, at) for n in ("t1", "t2", "hot1", "hot2", "base"))
                hot = sb("hot", [P, NB, NE], f16, at)
                top1, top2, mx, den = (sb(n, [P, NB], f32, at) for n in ("top1", "top2", "mx", "den"))
                before = sb("before", [P, P], f16, at)
                ones = sb("ones", [P, P], f16, at)
                run1, run2 = sb("run1", [P, NB, NE], f32, at), sb("run2", [P, NB, NE], f32, at)
                tiles_i = sb("tiles_i", [P, NE], i32, at)
                tiles, end1, end2 = (sb(n, [P, NE], f32, at) for n in ("tiles", "end1", "end2"))
                slot_iota, slot_of = sb("slot_iota", [1, P], f32, at), sb("slot_of", [1, P], f32, at)
                z_ps = [pb(f"z_ps{i}", [P, 2, KC, P], f16, at) for i in range(2)]
                l_ps = [pb(f"l_ps{i}", [P, 512], f32, at) for i in range(2)]
                in_ps = pb("in_ps", [P, 512], f32, at)
                all_ps = pb("all_ps", [P, 512], f32, at)

                loaded = [sem(f"loaded{i}", at) for i in range(RING)]
                x1_stored = [sem(f"x1_stored{i}", at) for i in range(RING)]
                z_stored = [sem(f"z_stored{i}", at) for i in range(RING)]
                small_loaded = sem("small_loaded", at)
                consts = sem("consts", at)
                rw_split = sem("rw_split", at)
                bn_done = sem("bn_done", at)
                x1_done = sem("x1_done", at)
                turned = sem("turned", at)
                z_t_done = sem("z_t_done", at)
                routed = sem("routed", at)
                logits_done = sem("logits_done", at)
                shifted = sem("shifted", at)
                exp_done = sem("exp_done", at)
                hots_done = sem("hots_done", at)
                hot_masked = sem("hot_masked", at)
                hot_sent = sem("hot_sent", at)
                ranked = sem("ranked", at)
                zeroed = sem("zeroed", at)
                pool_mult = sem("pool_mult", at)

                block = at.enter_context(nc.Block())

                @block.sync
                def _(sp):
                    sp.dma_start(rw32[:], router_w.rearrange("(c p) e -> p c e", p=P)).then_inc(small_loaded, 16)
                    sp.dma_start(rb[:], router_b.partition_broadcast(P)).then_inc(small_loaded, 16)

                    def step(item):
                        if m := item(0):
                            if m.after(RING):
                                sp.wait_ge(x1_done, m.k - (RING - 1))
                            r, rows = slice(0, m.rows), ds(m.k * P, m.rows)
                            sp.dma_start(x_in[m.i][r, :], x[rows, :]).then_inc(loaded[m.i], 16)

                    pipeline(sp, NB, 0, step)

                @block.gpsimd
                def _(pool):
                    nc.gpsimd.memset(logits[:], 0.0).then_inc(consts, 1)
                    nc.gpsimd.memset(before[:], 1.0).then_inc(zeroed, 1)
                    nc.gpsimd.memset(ones[:], 1.0)
                    pool.wait_ge(zeroed, 1)
                    nc.gpsimd.affine_select(out=before[:], in_=before[:], compare_op=ALU.is_gt, fill=0.0,
                                            base=0, pattern=[[1, P]], channel_multiplier=-1)
                    nc.gpsimd.iota(place[:, :, 2], [[P, NB]], base=0, channel_multiplier=1)
                    nc.gpsimd.iota(less[:], [[-1, NE]], base=NE, channel_multiplier=0,
                                   allow_small_or_imprecise_dtypes=True)
                    nc.gpsimd.iota(slot_iota[:], [[1, P]], base=0, channel_multiplier=0,
                                   allow_small_or_imprecise_dtypes=True).then_inc(consts, 1)

                    def step(item):
                        if m := item(0):
                            r = slice(0, m.rows)
                            if m.after(2):
                                pool.wait_ge(x1_done, m.k - 1)
                            nc.gpsimd.tensor_tensor(act_in[m.i2][r, :], h_all[r, ds(m.k, 1), :].rearrange("p a d -> p (a d)"), bn_scale[r, :], ALU.mult)\
                              .then_inc(pool_mult, 1)
                            pool.wait_ge(pool_mult, m.k + 1)
                            nc.gpsimd.tensor_tensor(act_in[m.i2][r, :], act_in[m.i2][r, :], bn_shift[r, :], ALU.add)\
                              .then_inc(bn_done, 1)

                    pipeline(pool, NB, 0, step)
                    pool.wait_ge(hots_done, 1)
                    for hot_ in (hot1, hot2):
                        nc.gpsimd.affine_select(out=hot_[:, NB - 1, :], in_=hot_[:, NB - 1, :], compare_op=ALU.is_gt,
                                                fill=0.0, base=LAST, pattern=[[0, NE]], channel_multiplier=-1)\
                          .then_inc(hot_masked, 1)

                @block.tensor
                def _(pe):
                    pe.wait_ge(consts, 2)
                    pe.wait_ge(rw_split, 1)

                    def step(item):
                        if m := item(0):
                            pe.wait_ge(norm.lo_done, m.k + 1)
                            pe.wait_ge(norm.hi_done, m.k + 1)
                            if m.after(2):
                                pe.wait_ge(z_t_done, m.k - 1)
                            for part in range(2):
                                for c in range(KC):
                                    last = nc.tensor.transpose(
                                        z_ps[m.i2][:, part, c, 0:m.rows],
                                        norm.hl[m.i][0:m.rows, part * D + c * P:part * D + (c + 1) * P],
                                        ident16[0:m.rows, 0:m.rows])
                            last.then_inc(turned, 1)
                        if m := item(1):
                            pe.wait_ge(z_t_done, m.k + 1)
                            if m.after(2):
                                pe.wait_ge(logits_done, m.k - 1)
                            split_product(l_ps[m.i2][0:m.rows, 0:NE], lambda c, part: z_t[m.i2][:, part, c, 0:m.rows],
                                          lambda c, part: rw[:, part, c, :], KC).then_inc(routed, 1)

                    pipeline(pe, NB, 1, step)
                    pe.wait_ge(hot_sent, 1)
                    flat = hot[:].rearrange("p b e -> p (b e)")
                    nc.tensor.matmul(in_ps[:, 0:NB * NE], before[:], flat, start=True, stop=True)
                    nc.tensor.matmul(all_ps[:, 0:NB * NE], ones[:], flat, start=True, stop=True).then_inc(ranked, 1)

                @block.scalar
                def _(act):
                    act.wait_ge(consts, 2)

                    def step(item):
                        if m := item(1):
                            act.wait_ge(x1_done, m.k + 1)
                            act.dma_start(x1_d[ds(m.k * P, m.rows), :], norm.x[m.i][0:m.rows, :])\
                               .then_inc(x1_stored[m.i], 16)
                        if m := item(3):
                            act.wait_ge(norm.lo_done, m.k + 1)
                            act.dma_start(z_d[ds(m.k * P, m.rows), :], norm.hl[m.i][0:m.rows, :])\
                               .then_inc(z_stored[m.i], 16)
                        if m := item(1):
                            norm.centre(act, m)
                        if m := item(0):
                            norm.std(act, m)
                        if m := item(1):
                            if m.after(RING):
                                act.wait_ge(z_stored[m.i], m.loads - 16)
                            norm.centred_hi(act, m)
                        if m := item(2):
                            act.wait_ge(turned, m.k + 1)
                            if m.after(2):
                                act.wait_ge(routed, m.k - 1)
                            nc.scalar.activation(z_t[m.i2][:, :, :, 0:m.rows], z_ps[m.i2][:, :, :, 0:m.rows],
                                                 ACT.Copy).then_inc(z_t_done, 1)
                        if m := item(3):
                            act.wait_ge(routed, m.k + 1)
                            nc.scalar.activation(logits[0:m.rows, m.k, :], l_ps[m.i2][0:m.rows, 0:NE], ACT.Copy)\
                              .then_inc(logits_done, 1)

                    pipeline(act, NB, 3, step)
                    for i in range(RING):
                        act.wait_ge(x1_stored[i], 16 * ring_uses(i, NB))
                        act.wait_ge(z_stored[i], 16 * ring_uses(i, NB))
                    act.wait_ge(shifted, 1)
                    nc.scalar.activation(t1[:], t1[:], ACT.Exp)
                    nc.scalar.activation(top2[:], top2[:], ACT.Exp).then_inc(exp_done, 1)

                @block.vector
                def _(dve):
                    V = nc.vector
                    dve.wait_ge(small_loaded, 32)
                    V.tensor_scalar(rw[:, 0], rw32[:], WS, None, ALU.mult)
                    dve.drain()
                    V.scalar_tensor_tensor(rw[:, 1], rw32[:], WS, rw[:, 0], ALU.mult, ALU.subtract)\
                     .then_inc(rw_split, 1)

                    def step(item):
                        if m := item(0):
                            r = slice(0, m.rows)
                            dve.wait_ge(loaded[m.i], m.loads)
                            dve.wait_ge(bn_done, m.k + 1)
                            if m.after(RING):
                                dve.wait_ge(x1_stored[m.i], m.loads - 16)
                            V.scalar_tensor_tensor(norm.x[m.i][r, :], act_in[m.i2][r, :], 0.0, x_in[m.i][r, :],
                                                   ALU.max, ALU.add).then_inc(x1_done, 1)
                            dve.drain()
                            norm.var(dve, m)
                        if m := item(2):
                            norm.centred_lo(dve, m)
                        if m := item(1):
                            norm.factors(dve, m)

                    pipeline(dve, NB, 2, step)

                    dve.wait_ge(logits_done, NB)
                    wide = lambda t: t[:].unsqueeze(2).to_broadcast([P, NB, NE])
                    per_expert = lambda t: t[:].unsqueeze(1).to_broadcast([P, NB, NE])
                    V.scalar_tensor_tensor(logits[:], logits[:], 1.0 / WS, per_expert(rb), ALU.mult, ALU.add)
                    dve.drain()
                    V.tensor_reduce(top1[:], logits[:], AX.X, ALU.max)
                    dve.drain()
                    V.tensor_tensor(t1[:], logits[:], wide(top1), ALU.subtract)
                    V.tensor_tensor(hot1[:], logits[:], wide(top1), ALU.is_equal)
                    dve.drain()
                    V.tensor_tensor(t2[:], hot1[:], per_expert(less), ALU.mult)
                    dve.drain()
                    V.tensor_reduce(mx[:], t2[:], AX.X, ALU.max)
                    dve.drain()
                    V.tensor_tensor(hot1[:], t2[:], wide(mx), ALU.is_equal)
                    dve.drain()
                    V.scalar_tensor_tensor(logits[:], hot1[:], -1e30, logits[:], ALU.mult, ALU.add)
                    dve.drain()
                    V.tensor_reduce(top2[:], logits[:], AX.X, ALU.max)
                    dve.drain()
                    V.tensor_tensor(hot2[:], logits[:], wide(top2), ALU.is_equal)
                    dve.drain()
                    V.tensor_tensor(t2[:], hot2[:], per_expert(less), ALU.mult)
                    V.tensor_tensor(top2[:], top2[:], top1[:], ALU.subtract).then_inc(shifted, 1)
                    dve.drain()
                    V.tensor_reduce(mx[:], t2[:], AX.X, ALU.max)
                    dve.drain()
                    V.tensor_tensor(hot2[:], t2[:], wide(mx), ALU.is_equal).then_inc(hots_done, 1)
                    dve.wait_ge(exp_done, 1)
                    V.tensor_reduce(den[:], t1[:], AX.X, ALU.add)
                    dve.drain()
                    V.reciprocal(top1[:], den[:])
                    dve.drain()
                    V.tensor_tensor(top2[:], top2[:], top1[:], ALU.mult)
                    dve.drain()
                    V.scalar_tensor_tensor(den[:], top1[:], 1e-9, top2[:], ALU.add, ALU.add)
                    dve.drain()
                    V.reciprocal(mx[:], den[:])
                    dve.drain()
                    V.tensor_tensor(share[:, :, 0], top1[:], mx[:], ALU.mult)
                    V.tensor_tensor(share[:, :, 1], top2[:], mx[:], ALU.mult)
                    dve.wait_ge(hot_masked, 2)
                    V.tensor_tensor(hot[:], hot1[:], hot2[:], ALU.add).then_inc(hot_sent, 1)
                    dve.wait_ge(ranked, 1)
                    blocks = lambda t: t[:, 0:NB * NE].rearrange("p (b e) -> p b e", e=NE)
                    V.tensor_copy(run1[:], blocks(all_ps))
                    dve.drain()
                    a, b, s = run1, run2, 1
                    while s < NB:
                        V.tensor_copy(b[:, 0:s, :], a[:, 0:s, :])
                        V.tensor_tensor(b[:, s:NB, :], a[:, s:NB, :], a[:, 0:NB - s, :], ALU.add)
                        dve.drain()
                        a, b, s = b, a, 2 * s
                    V.tensor_scalar(tiles_i[:], a[:, NB - 1, :], float(P - 1), None, ALU.add)
                    dve.drain()
                    V.tensor_scalar(tiles_i[:], tiles_i[:], P.bit_length() - 1, None, ALU.logical_shift_right)
                    dve.drain()
                    V.tensor_copy(tiles[:], tiles_i[:])
                    V.tensor_copy(end1[:], tiles_i[:])
                    dve.drain()
                    u, v, s = end1, end2, 1
                    while s < NE:
                        V.tensor_copy(v[:, 0:s], u[:, 0:s])
                        V.tensor_tensor(v[:, s:NE], u[:, s:NE], u[:, 0:NE - s], ALU.add)
                        dve.drain()
                        u, v, s = v, u, 2 * s
                    V.tensor_tensor(v[:], u[:], tiles[:], ALU.subtract)
                    dve.drain()
                    V.tensor_scalar(tiles[:], v[:], float(P), None, ALU.mult)
                    dve.drain()
                    V.tensor_tensor(base[:], a[:], blocks(all_ps), ALU.subtract)
                    dve.drain()
                    V.tensor_tensor(base[:], base[:], blocks(in_ps), ALU.add)
                    dve.drain()
                    V.tensor_tensor(base[:], base[:], per_expert(tiles), ALU.add)
                    dve.drain()
                    V.tensor_tensor(t1[:], base[:], hot1[:], ALU.mult)
                    V.tensor_tensor(t2[:], base[:], hot2[:], ALU.mult)
                    dve.drain()
                    V.tensor_reduce(top1[:], t1[:], AX.X, ALU.add)
                    V.tensor_reduce(top2[:], t2[:], AX.X, ALU.add)
                    dve.drain()
                    V.tensor_copy(place[:, :, 0], top1[:])
                    V.tensor_copy(place[:, :, 1], top2[:])
                    V.memset(slot_of[:], 0.0)
                    dve.drain()
                    for e in range(NE - 1):
                        V.scalar_tensor_tensor(slot_of[:], slot_iota[:], u[0:1, e:e + 1], slot_of[:],
                                               ALU.is_ge, ALU.add)
                        dve.drain()
                    V.tensor_copy(tile_expert[:], slot_of[:, 0:NS])

        def late():
            at = ExitStack()
            with at:
                w_gu = [sb(f"w_gu{n}", [P, 2, KC, FF], f16, at) for n in range(2)]
                w_dn = sb("w_dn", [P, 2, FT, D], f16, at)
                w_cv = sb("w_cv", [P, 2, KC, D], f16, at)
                expert_layer(w_gu, w_dn, w_cv)
                graph_and_gated(w_gu, w_dn)

        def expert_layer(w_gu, w_dn, w_cv):
            at = ExitStack()
            with at:
                w1_sb = sb("w1_sb", [P, 2, KC, NE, FE], f16, at)
                w2_sb = sb("w2_sb", [P, 2, FC, NE, D], f16, at)
                item_token = sb("item_token", [P, NS], i32, at)
                dispatch(w_gu, w_dn, w_cv, w1_sb, w2_sb, item_token)
                experts(w1_sb, w2_sb, item_token)
            combine(w_cv)

        def dispatch(w_gu, w_dn, w_cv, w1_sb, w2_sb, item_token):
            at = ExitStack()
            with at:
                FP = -(-FT // 2)
                pieces = [(n, f0, min(FP, FT - f0)) for n in range(3) for f0 in (0, FP)]
                RB = 3
                PB = 3
                raw = [sb(f"raw{i}", [P, FP * KC, P], f32, at) for i in range(RB)]
                w_in = [sb(f"w_in{i}", [P, KC * FE], f32, at) for i in range(PB)]
                size = sb("size", [P, FP * KC], f32, at)
                inv_size = sb("inv_size", [P, FP * KC], f32, at)
                of = [sb(f"of{i}", [P, 3], i32, at) for i in range(RING)]
                no_token = sb("no_token", [NS, P], i32, at)
                slot_token = sb("slot_token", [NS, P], i32, at)
                slot_token32 = sb("slot_token32", [NS, P], f32, at)
                TB = 4
                t_ps = [pb(f"t_ps{i}", [P, KC, P], f32, at) for i in range(TB)]
                token_ps = pb("token_ps", [P, 512], f32, at)

                no_token_set = sem("no_token_set", at)
                tokens_cleared = sem("tokens_cleared", at)
                of_set = sem("of_set", at)
                of_seen = sem("of_seen", at)
                scattered = [sem(f"scattered{i}", at) for i in range(RING)]
                tokens_loaded = sem("tokens_loaded", at)
                tokens_f32 = sem("tokens_f32", at)
                tokens_turned = sem("tokens_turned", at)
                w_loaded = [sem(f"ew_loaded{i}", at) for i in range(PB)]
                w_hi = sem("ew_hi", at)
                w_lo = sem("ew_lo", at)
                raw_loaded = [sem(f"raw_loaded{i}", at) for i in range(RB)]
                rounded = sem("rounded", at)
                t_turned = sem("t_turned", at)
                t_hi = sem("t_hi", at)
                t_lo = sem("t_lo", at)
                block = at.enter_context(nc.Block())

                plain = [part for e in range(NE) for part in
                         ((w1[e], KC, w1_sb, lambda t, p, e=e: t[:, p, :, e, :]),
                          (w2[e], FC, w2_sb, lambda t, p, e=e: t[:, p, :, e, :]))]
                plain += [(W_g[h * D // 2:(h + 1) * D // 2, :], KC // 2, w_cv,
                           lambda t, p, h=h: t[:, p, h * KC // 2:(h + 1) * KC // 2, :]) for h in range(2)]

                def plain_in(n):
                    return w_in[n % PB][:].rearrange("p (c f) -> p c f", c=plain[n][1])

                def plain_out(n, part):
                    _, _, t, view = plain[n]
                    return view(t, part)

                units = [(q, f) for q, (_, _, nf) in enumerate(pieces) for f in range(nf)]

                def units_to(q):
                    return sum(nf for _, _, nf in pieces[:q + 1])

                def piece(q):
                    return raw[q % RB][:, 0:pieces[q][2] * KC, :]

                def group(q, f, c):
                    n, _, nf = pieces[q]
                    return raw[q % RB][:, f * KC + c if n < 2 else c * nf + f, :]

                def unit_out(q, f, part):
                    n, f0, _ = pieces[q]
                    if n < 2:
                        return w_gu[n][:, part, :, (f0 + f) * P:(f0 + f + 1) * P]
                    return w_dn[:, part, f0 + f, :].rearrange("p (c o) -> p c o", c=KC)

                PER = -(-len(plain) // (len(pieces) + 1))

                def beside(q):
                    return range((q + 1) * PER, min((q + 2) * PER, len(plain)))

                @block.sync
                def _(sp):
                    sp.wait_ge(no_token_set, 1)
                    sp.dma_start(slot_token_d.rearrange("(s p) o -> s (p o)", p=P), no_token[:])\
                      .then_inc(tokens_cleared, 16)

                    def load_piece(q):
                        if q >= RB:
                            sp.wait_ge(t_turned, units_to(q - RB))
                        n, f0, nf = pieces[q]
                        if n < 2:
                            to = piece(q).rearrange("p (f c) k -> p f (c k)", f=nf)
                            part = (w_gate, w_up)[n][f0 * P:(f0 + nf) * P, :].rearrange("(f p) k -> p f k", p=P)
                        else:
                            to = piece(q).rearrange("p (c f) k -> p c (f k)", c=KC)
                            part = w_down[:, f0 * P:(f0 + nf) * P].rearrange("(c p) k -> p c k", p=P)
                        sp.dma_start(to, part).then_inc(raw_loaded[q % RB], 16)

                    def load_plain(n):
                        if n >= PB:
                            sp.wait_ge(w_hi, n - PB + 1)
                            sp.wait_ge(w_lo, n - PB + 1)
                        sp.dma_start(plain_in(n), plain[n][0].rearrange("(c p) f -> p c f", p=P))\
                          .then_inc(w_loaded[n % PB], 16)

                    for n in range(PB):
                        load_plain(n)
                    for q in range(RB):
                        load_piece(q)
                    for n in range(PB, len(plain)):
                        load_plain(n)
                        for q in range(RB, len(pieces)):
                            if n == max(beside(q - RB)):
                                load_piece(q)
                    for i in range(RING):
                        sp.wait_ge(scattered[i], 32 * ring_uses(i, NB))
                    sp.dma_start(slot_token[:], slot_token_d.rearrange("(s p) o -> s (p o)", p=P))\
                      .then_inc(tokens_loaded, 16)

                @block.gpsimd
                def _(pool):
                    nc.gpsimd.memset(no_token[:], 0).then_inc(no_token_set, 1)
                    pool.wait_ge(tokens_cleared, 16)

                    def step(item):
                        if m := item(0):
                            if m.after(RING):
                                pool.wait_ge(scattered[m.i], m.loads * 2 - 32)
                            nc.gpsimd.tensor_copy(of[m.i][:], place[:, m.k, :]).then_inc(of_set, 1)
                        if m := item(1):
                            pool.wait_ge(of_set, m.k + 1)
                            pool.sem_inc(of_seen, 1)
                            for n in range(2):
                                pool.indirect_dma_start(
                                    out=slot_token_d, in_=of[m.i][0:m.rows, 2:3], in_offset=None,
                                    out_offset=bass.IndirectOffsetOnAxis(ap=of[m.i][0:m.rows, n:n + 1], axis=0),
                                ).then_inc(scattered[m.i], 16)

                    pipeline(pool, NB, 1, step)

                @block.tensor
                def _(pe):
                    for k, (q, f) in enumerate(units):
                        pe.wait_ge(rounded, q + 1)
                        if k >= TB:
                            pe.wait_ge(t_hi, k - TB + 1)
                            pe.wait_ge(t_lo, k - TB + 1)
                        for c in range(KC):
                            last = nc.tensor.transpose(t_ps[k % TB][:, c, :], group(q, f, c), ident32[:])
                        last.then_inc(t_turned, 1)
                    pe.wait_ge(tokens_f32, 1)
                    nc.tensor.transpose(token_ps[:, 0:NS], slot_token32[:], ident32[0:NS, 0:NS])\
                      .then_inc(tokens_turned, 1)

                @block.scalar
                def _(act):
                    def split_plain(some):
                        for n in some:
                            act.wait_ge(w_loaded[n % PB], 16 * (n // PB + 1))
                            nc.scalar.activation(plain_out(n, 0), plain_in(n), ACT.Copy, scale=WS).then_inc(w_hi, 1)

                    split_plain(beside(-1))
                    for q in range(len(pieces)):
                        for k, (of_piece, f) in enumerate(units):
                            if of_piece == q:
                                act.wait_ge(t_turned, k + 1)
                                nc.scalar.activation(unit_out(q, f, 0), t_ps[k % TB][:], ACT.Copy, scale=WS)\
                                  .then_inc(t_hi, 1)
                        split_plain(beside(q))

                @block.vector
                def _(dve):
                    V = nc.vector

                    def round_piece(q):
                        nf = pieces[q][2]
                        w, g = piece(q), slice(0, nf * KC)
                        wide = lambda t: t[:, g].unsqueeze(2).to_broadcast([P, nf * KC, P])
                        dve.wait_ge(raw_loaded[q % RB], 16 * (q // RB + 1))
                        V.tensor_reduce(size[:, g], w, AX.X, ALU.add, apply_absolute_value=True)
                        dve.drain()
                        V.tensor_scalar(size[:, g], size[:, g], 1.0 / P, EPS, ALU.mult, ALU.add)
                        dve.drain()
                        V.reciprocal(inv_size[:, g], size[:, g])
                        dve.drain()
                        V.tensor_tensor(w, w, wide(inv_size), ALU.mult)
                        dve.drain()
                        V.tensor_scalar(w, w, -1.0, 1.0, ALU.max, ALU.min)
                        dve.drain()
                        V.tensor_scalar(w, w, MAGIC, MAGIC, ALU.add, ALU.subtract)
                        dve.drain()
                        V.tensor_tensor(w, w, wide(size), ALU.mult).then_inc(rounded, 1)

                    def split_piece(q):
                        for k, (of_piece, f) in enumerate(units):
                            if of_piece == q:
                                dve.wait_ge(t_hi, k + 1)
                                V.scalar_tensor_tensor(unit_out(q, f, 1), t_ps[k % TB][:], WS, unit_out(q, f, 0),
                                                       ALU.mult, ALU.subtract).then_inc(t_lo, 1)

                    def split_plain(some):
                        for n in some:
                            dve.wait_ge(w_hi, n + 1)
                            V.scalar_tensor_tensor(plain_out(n, 1), plain_in(n), WS, plain_out(n, 0), ALU.mult,
                                                   ALU.subtract).then_inc(w_lo, 1)

                    split_plain(beside(-1))
                    round_piece(0)
                    for q in range(len(pieces)):
                        if q + 1 < len(pieces):
                            dve.drain()
                            round_piece(q + 1)
                        split_piece(q)
                        split_plain(beside(q))
                    dve.wait_ge(tokens_loaded, 16)
                    V.tensor_copy(slot_token32[:], slot_token[:]).then_inc(tokens_f32, 1)
                    dve.wait_ge(tokens_turned, 1)
                    V.tensor_copy(item_token[:], token_ps[:, 0:NS])

        def experts(w1_sb, w2_sb, item_token):
            at = ExitStack()
            with at:
                b1_sb, b2_sb = sb("b1_sb", [P, NE, FE], f32, at), sb("b2_sb", [P, NE, D], f32, at)
                item_of = [sb(f"item_of{i}", [P, 1], i32, at) for i in range(RING)]
                item_in = [sb(f"item_in{i}", [P, 2 * D], f16, at) for i in range(RING)]
                it_t = [sb(f"it_t{i}", [P, 2, KC, P], f16, at) for i in range(2)]
                u_sb = [sb(f"u_sb{i}", [P, FE], f32, at) for i in range(2)]
                g_sb = [sb(f"g_sb{i}", [P, FE], f32, at) for i in range(2)]
                g_hl = [sb(f"g_hl{i}", [P, 2, FE], f16, at) for i in range(2)]
                g_t = [sb(f"g_t{i}", [P, 2, FC, P], f16, at) for i in range(2)]
                y_sb = [sb(f"y_sb{i}", [P, D], f32, at) for i in range(RING)]
                it_ps = pb("it_ps", [P, 2, KC, P], f16, at)
                u_ps = [pb(f"u_ps{i}", [P, 512], f32, at) for i in range(2)]
                g_ps = [pb(f"g_ps{i}", [P, 2, FC, 2 * P], f16, at) for i in range(2)]
                y_ps = [pb(f"y_ps{i}", [P, D], f32, at) for i in range(2)]

                b_loaded = [sem(f"eb_loaded{i}", at) for i in range(2)]
                of_set = sem("item_of_set", at)
                of_seen = sem("item_of_seen", at)
                it_loaded = [sem(f"it_loaded{i}", at) for i in range(RING)]
                it_turned = sem("it_turned", at)
                it_t_done = sem("it_t_done", at)
                up_done = sem("up_done", at)
                u_done = sem("u_done", at)
                g_done = sem("g_done", at)
                g_hi = sem("g_hi", at)
                g_lo = sem("g_lo", at)
                g_turned = sem("g_turned", at)
                g_t_done = sem("g_t_done", at)
                down_done = sem("down_done", at)
                y_done = sem("y_done", at)
                y_stored = [sem(f"y_stored{i}", at) for i in range(RING)]
                block = at.enter_context(nc.Block())

                @block.gpsimd
                def _(pool):
                    def step(item):
                        if m := item(0):
                            if m.after(RING):
                                pool.wait_ge(it_turned, m.k - (RING - 1))
                            nc.gpsimd.tensor_copy(item_of[m.i][:], item_token[:, ds(m.k, 1)]).then_inc(of_set, 1)
                        if m := item(1):
                            pool.wait_ge(of_set, m.k + 1)
                            pool.sem_inc(of_seen, 1)
                            pool.indirect_dma_start(
                                out=item_in[m.i][:], out_offset=None, in_=z_d[0:N, :],
                                in_offset=bass.IndirectOffsetOnAxis(ap=item_of[m.i][:], axis=0),
                            ).then_inc(it_loaded[m.i], 16)

                    pipeline(pool, NS, 1, step)

                @block.sync
                def _(sp):
                    sp.dma_start(b1_sb[:], b1.partition_broadcast(P)).then_inc(b_loaded[0], 16)
                    sp.wait_ge(it_loaded[1], 16)
                    sp.dma_start(b2_sb[:], b2.partition_broadcast(P)).then_inc(b_loaded[1], 16)

                    def step(item):
                        if m := item(0):
                            sp.wait_ge(y_done, m.k + 1)
                            sp.dma_start(items_out[ds(m.k * P, P), :], y_sb[m.i][:]).then_inc(y_stored[m.i], 16)

                    pipeline(sp, NS, 0, step)
                    for i in range(RING):
                        sp.wait_ge(y_stored[i], 16 * ring_uses(i, NS))

                @block.tensor
                def _(pe):
                    def expert(k):
                        return pe.value_load(tile_expert[0:1, ds(k, 1)], min_val=0, max_val=NE - 1)

                    def step(item):
                        if m := item(1):
                            e = expert(m.k)
                            pe.wait_ge(it_t_done, m.k + 1)
                            if m.after(2):
                                pe.wait_ge(u_done, m.k - 1)
                            split_product(u_ps[m.i2][:, 0:FE], lambda c, part: it_t[m.i2][:, part, c, :],
                                          lambda c, part: w1_sb[:, part, c, ds(e, 1), :], KC).then_inc(up_done, 1)
                        if m := item(0):
                            pe.wait_ge(it_loaded[m.i], m.loads)
                            if m.after(1):
                                pe.wait_ge(it_t_done, m.k)
                            for part in range(2):
                                for c in range(KC):
                                    last = nc.tensor.transpose(
                                        it_ps[:, part, c, :],
                                        item_in[m.i][:, part * D + c * P:part * D + (c + 1) * P], ident16[:])
                            last.then_inc(it_turned, 1)
                        if m := item(3):
                            e = expert(m.k)
                            pe.wait_ge(g_t_done, m.k + 1)
                            if m.after(2):
                                pe.wait_ge(y_done, m.k - 1)
                            split_product(y_ps[m.i2][:], lambda c, part: g_t[m.i2][:, part, c, :],
                                          lambda c, part: w2_sb[:, part, c, ds(e, 1), :], FC).then_inc(down_done, 1)
                        if m := item(2):
                            pe.wait_ge(g_hi, m.k + 1)
                            pe.wait_ge(g_lo, m.k + 1)
                            if m.after(2):
                                pe.wait_ge(g_t_done, m.k - 1)
                            for part in range(2):
                                for c in range(FC):
                                    last = nc.tensor.transpose(g_ps[m.i2][:, part, c, 0:P],
                                                               g_hl[m.i2][:, part, c * P:(c + 1) * P], ident16[:])
                            last.then_inc(g_turned, 1)

                    pipeline(pe, NS, 3, step)

                @block.scalar
                def _(act):
                    def step(item):
                        if m := item(0):
                            act.wait_ge(it_turned, m.k + 1)
                            if m.after(2):
                                act.wait_ge(up_done, m.k - 1)
                            nc.scalar.activation(it_t[m.i2][:], it_ps[:], ACT.Copy).then_inc(it_t_done, 1)
                        if m := item(1):
                            act.wait_ge(u_done, m.k + 1)
                            if m.after(2):
                                act.wait_ge(g_lo, m.k - 1)
                            nc.scalar.activation(g_sb[m.i2][:], u_sb[m.i2][:], ACT.Gelu).then_inc(g_done, 1)
                            if m.after(2):
                                act.wait_ge(g_turned, m.k - 1)
                            act.wait_ge(g_done, m.k + 1)
                            nc.scalar.activation(g_hl[m.i2][:, 0, :], g_sb[m.i2][:], ACT.Copy).then_inc(g_hi, 1)

                    pipeline(act, NS, 1, step)

                @block.vector
                def _(dve):
                    dve.wait_ge(b_loaded[0], 16)

                    def expert(k):
                        return dve.value_load(tile_expert[0:1, ds(k, 1)], min_val=0, max_val=NE - 1)

                    def step(item):
                        if m := item(3):
                            dve.wait_ge(g_turned, m.k + 1)
                            nc.vector.tensor_copy(g_t[m.i2][:], g_ps[m.i2][:, :, :, 0:P]).then_inc(g_t_done, 1)
                        if m := item(1):
                            e = expert(m.k)
                            dve.wait_ge(up_done, m.k + 1)
                            if m.after(2):
                                dve.wait_ge(g_done, m.k - 1)
                            nc.vector.scalar_tensor_tensor(u_sb[m.i2][:], u_ps[m.i2][:, 0:FE], 1.0 / WS,
                                                           b1_sb[:, ds(e, 1), :].rearrange("p a f -> p (a f)"),
                                                           ALU.mult, ALU.add).then_inc(u_done, 1)
                        if m := item(4):
                            e = expert(m.k)
                            if m.fixed and m.k == 0:
                                dve.wait_ge(b_loaded[1], 16)
                            dve.wait_ge(down_done, m.k + 1)
                            if m.after(RING):
                                dve.wait_ge(y_stored[m.i], m.loads - 16)
                            nc.vector.scalar_tensor_tensor(y_sb[m.i][:], y_ps[m.i2][:], 1.0 / WS,
                                                           b2_sb[:, ds(e, 1), :].rearrange("p a f -> p (a f)"),
                                                           ALU.mult, ALU.add).then_inc(y_done, 1)
                        if m := item(1):
                            dve.wait_ge(g_hi, m.k + 1)
                            nc.vector.tensor_tensor(g_hl[m.i2][:, 1, :], g_sb[m.i2][:], g_hl[m.i2][:, 0, :],
                                                    ALU.subtract).then_inc(g_lo, 1)

                    pipeline(dve, NS, 4, step)

        def combine(w_cv):
            at = ExitStack()
            with at:
                norm = Norm(at, "n2")
                x1_in = [sb(f"x1_in{i}", [P, D], f32, at) for i in range(RING)]
                y_in = [[sb(f"y_in{i}_{n}", [P, D], f32, at) for n in range(2)] for i in range(RING)]
                places = [sb(f"places{i}", [P, 2], i32, at) for i in range(RING)]
                z_t = [sb(f"z_t2_{i}", [P, 2, KC, P], f16, at) for i in range(2)]
                support = [sb(f"support{i}", [P, D], f32, at) for i in range(RING)]
                z_ps = [pb(f"z_ps2_{i}", [P, 2, KC, P], f16, at) for i in range(2)]
                support_ps = [pb(f"support_ps{i}", [P, D], f32, at) for i in range(2)]
                x1_loaded = [sem(f"x1_loaded{i}", at) for i in range(RING)]
                places_set = sem("places_set", at)
                places_seen = sem("places_seen", at)
                y_gathered = [sem(f"y_gathered{i}", at) for i in range(RING)]
                x2_done = sem("x2_done", at)
                x2_stored = [sem(f"x2_stored{i}", at) for i in range(RING)]
                turned = sem("z2_turned", at)
                z_t_done = sem("z2_t_done", at)
                projected = sem("projected", at)
                support_done = sem("support_done", at)
                support_stored = [sem(f"support_stored{i}", at) for i in range(RING)]
                block = at.enter_context(nc.Block())

                @block.sync
                def _(sp):
                    def step(item):
                        if m := item(0):
                            if m.after(RING):
                                sp.wait_ge(x2_done, m.k - (RING - 1))
                            sp.dma_start(x1_in[m.i][0:m.rows, :], x1_d[ds(m.k * P, m.rows), :])\
                              .then_inc(x1_loaded[m.i], 16)

                    pipeline(sp, NB, 0, step)

                @block.gpsimd
                def _(pool):
                    def step(item):
                        if m := item(0):
                            if m.after(RING):
                                pool.wait_ge(x2_done, m.k - (RING - 1))
                            nc.gpsimd.tensor_copy(places[m.i][:], place[:, m.k, 0:2]).then_inc(places_set, 1)
                        if m := item(1):
                            pool.wait_ge(places_set, m.k + 1)
                            pool.sem_inc(places_seen, 1)
                            for n in range(2):
                                pool.indirect_dma_start(
                                    out=y_in[m.i][n][0:m.rows, :], out_offset=None, in_=items_out,
                                    in_offset=bass.IndirectOffsetOnAxis(ap=places[m.i][0:m.rows, n:n + 1], axis=0),
                                ).then_inc(y_gathered[m.i], 16)

                    pipeline(pool, NB, 1, step)

                @block.tensor
                def _(pe):
                    def step(item):
                        if m := item(0):
                            pe.wait_ge(norm.lo_done, m.k + 1)
                            if m.after(2):
                                pe.wait_ge(z_t_done, m.k - 1)
                            for part in range(2):
                                for c in range(KC):
                                    last = nc.tensor.transpose(
                                        z_ps[m.i2][:, part, c, 0:m.rows],
                                        norm.hl[m.i][0:m.rows, part * D + c * P:part * D + (c + 1) * P],
                                        ident16[0:m.rows, 0:m.rows])
                            last.then_inc(turned, 1)
                        if m := item(1):
                            pe.wait_ge(z_t_done, m.k + 1)
                            if m.after(2):
                                pe.wait_ge(support_done, m.k - 1)
                            split_product(support_ps[m.i2][0:m.rows, :],
                                          lambda c, part: z_t[m.i2][:, part, c, 0:m.rows],
                                          lambda c, part: w_cv[:, part, c, :], KC).then_inc(projected, 1)

                    pipeline(pe, NB, 1, step)

                @block.scalar
                def _(act):
                    def step(item):
                        if m := item(1):
                            act.wait_ge(x2_done, m.k + 1)
                            act.dma_start(x2_d[ds(m.k * P, m.rows), :], norm.x[m.i][0:m.rows, :])\
                               .then_inc(x2_stored[m.i], 16)
                        if m := item(4):
                            act.wait_ge(support_done, m.k + 1)
                            act.dma_start(support_d[ds(m.k * P, m.rows), :], support[m.i][0:m.rows, :])\
                               .then_inc(support_stored[m.i], 16)
                        if m := item(1):
                            norm.centre(act, m)
                        if m := item(0):
                            norm.std(act, m)
                        if m := item(1):
                            norm.centred_hi(act, m)
                        if m := item(2):
                            act.wait_ge(turned, m.k + 1)
                            if m.after(2):
                                act.wait_ge(projected, m.k - 1)
                            nc.scalar.activation(z_t[m.i2][:, :, :, 0:m.rows], z_ps[m.i2][:, :, :, 0:m.rows],
                                                 ACT.Copy).then_inc(z_t_done, 1)
                        if m := item(3):
                            act.wait_ge(projected, m.k + 1)
                            if m.after(RING):
                                act.wait_ge(support_stored[m.i], m.loads - 16)
                            nc.scalar.activation(support[m.i][0:m.rows, :], support_ps[m.i2][0:m.rows, :], ACT.Copy,
                                                 scale=1.0 / WS).then_inc(support_done, 1)

                    pipeline(act, NB, 4, step)
                    for i in range(RING):
                        act.wait_ge(x2_stored[i], 16 * ring_uses(i, NB))
                        act.wait_ge(support_stored[i], 16 * ring_uses(i, NB))

                @block.vector
                def _(dve):
                    def step(item):
                        if m := item(0):
                            r = slice(0, m.rows)
                            dve.wait_ge(y_gathered[m.i], m.loads * 2)
                            dve.wait_ge(x1_loaded[m.i], m.loads)
                            if m.after(RING):
                                dve.wait_ge(x2_stored[m.i], m.loads - 16)
                            nc.vector.scalar_tensor_tensor(x1_in[m.i][r, :], y_in[m.i][0][r, :],
                                                           share[r, m.k, 0:1], x1_in[m.i][r, :],
                                                           ALU.mult, ALU.add)
                            dve.drain()
                            nc.vector.scalar_tensor_tensor(norm.x[m.i][r, :], y_in[m.i][1][r, :],
                                                           share[r, m.k, 1:2], x1_in[m.i][r, :],
                                                           ALU.mult, ALU.add).then_inc(x2_done, 1)
                            dve.drain()
                            norm.var(dve, m)
                        if m := item(1):
                            norm.factors(dve, m)
                        if m := item(2):
                            norm.centred_lo(dve, m)

                    pipeline(dve, NB, 2, step)

        def graph_and_gated(w_gu, w_dn):
            at = ExitStack()
            with at:
                R = 4
                W = R * P
                NGR = (NB - 1) // R
                edges = WeightedSums(at)
                x2_in = sb("x2_in", [P, D], f32, at)
                conv = sb("conv", [P, D], f32, at)
                x3 = [[sb(f"x3_{p}_{r}", [P, D], f32, at) for r in range(R)] for p in range(2)]
                norm = Norm(at, "n3", 1, [None])
                z_t = [sb(f"z_t3_{p}", [P, 2, KC, W], f16, at) for p in range(2)]
                silu = [sb(f"silu{i}", [P, W], f32, at) for i in range(2)]
                h_t = sb("h_t", [P, FT, 2, W], f16, at)
                acc = pb("acc3", [P, D], f32, at)
                turn_ps = pb("turn_ps", [P, 2, KC, P], f16, at)
                gate_ps = [pb(f"gate_ps{i}", [P, W], f32, at) for i in range(2)]
                up_ps = [pb(f"up_ps{i}", [P, W], f32, at) for i in range(2)]
                down_ps = [pb(f"down_ps{i}", [P, D], f32, at) for i in range(2)]

                acc_ready = sem("acc_ready3", at)
                conv_done = sem("conv_done", at)
                x2_loaded = sem("x2_loaded", at)
                x3_done = sem("x3_done", at)
                z_turned = sem("z_turned", at)
                z_t_done = sem("z_t_done3", at)
                up_ready = sem("up_ready", at)
                silu_done = sem("silu_done", at)
                prod_done = sem("prod_done", at)
                h_hi_done = sem("h_hi_done", at)
                h_lo_done = sem("h_lo_done", at)
                down_ready = sem("down_ready", at)
                out_done = sem("out_done", at)
                out_stored = [[sem(f"out_stored{p}_{r}", at) for r in range(R)] for p in range(2)]
                block = at.enter_context(nc.Block())

                class Step:

                    def __init__(self, g, p, r):
                        self.g, self.p, self.r = g, p, r
                        self.b = g * R + r
                        self.first = isinstance(g, int) and g == 0 and r == 0
                        self.last = isinstance(g, int) and g == NGR
                        self.rows = LAST if self.last else P

                class Gated:

                    def __init__(self, g, p):
                        self.g, self.p = g, p
                        self.last = isinstance(g, int) and g == NGR
                        self.n = 1 if self.last else R
                        self.width = self.n * P
                        self.first = isinstance(g, int) and g == 0
                        self.units = [("up", f) for f in range(FT)] + [("down", r) for r in range(self.n)]

                def program(eng, step, tail):
                    cuts = [(0, 1, 2, 4), (4, 5, 6, 8), (8, 9, 10, 11), (11, 12, 13, 15)]
                    assert FT + R == 15

                    def group(g, p, before):
                        for r in range(R):
                            gated = Gated(g - 1, 1 - p) if before else None
                            c = cuts[r]
                            step(Step(g, p, r), gated,
                                 [gated.units[c[n]:c[n + 1]] if gated else [] for n in range(3)])

                    group(0, 0, False)
                    group(1, 1, True)
                    group(2, 0, True)
                    with eng.Fori(3, NGR - 1, 2) as n:
                        g = n.with_bounds(min_val=3, max_val=NGR - 3)
                        group(g, 1, True)
                        group(g + 1, 0, True)
                    group(NGR - 1, 1, True)
                    gated = Gated(NGR - 1, 1)
                    step(Step(NGR, 0, 0), gated, [gated.units[0:1], gated.units[1:2], gated.units[2:4]])
                    tail(Step(NGR, 0, 0), gated, gated.units[4:], Gated(NGR, 0))

                assert NGR % 2 == 0 and NB - 1 == NGR * R

                def waits_unit(t, f):
                    return f - 2 if f >= 2 else -1 - f

                @block.gpsimd
                def _(pool):
                    edges.gather(pool, 0, support_d[0:N, :])
                    with pool.Fori(1, NB) as b:
                        edges.gather(pool, b, support_d[0:N, :])

                @block.sync
                def _(sp):
                    edges.load_block(sp, 0)
                    with sp.Fori(1, NB) as b:
                        edges.load_block(sp, b)

                @block.tensor
                def _(pe):
                    pe.sem_inc(edges.prepared, PARTS)
                    pe.sem_inc(edges.summed, PARTS)

                    def unit(t, kind, n):
                        if kind == "up":
                            if n == 0:
                                pe.wait_ge(z_t_done, t.g * R + t.n)
                            if not t.first or n >= 2:
                                pe.wait_ge(prod_done, t.g * FT + (waits_unit(t, n) + 1))
                            for ps, w in ((gate_ps, w_gu[0]), (up_ps, w_gu[1])):
                                last = split_product(ps[n % 2][:, 0:t.width],
                                                     lambda c, part: w[:, part, c, n * P:(n + 1) * P],
                                                     lambda c, part: z_t[t.p][:, part, c, 0:t.width], KC)
                            last.then_inc(up_ready, 1)
                        else:
                            pe.wait_ge(h_lo_done, t.g * FT + FT)
                            if not t.first or n >= 2:
                                pe.wait_ge(out_done, t.g * R + (n - 1))
                            split_product(down_ps[n % 2][:], lambda c, part: h_t[:, c, part, n * P:(n + 1) * P],
                                          lambda c, part: w_dn[:, part, c, :], FT).then_inc(down_ready, 1)

                    def turn_z(s):
                        if not s.first:
                            pe.wait_ge(z_t_done, s.b)
                        pe.wait_ge(norm.hi_done, s.b + 1)
                        pe.wait_ge(norm.lo_done, s.b + 1)
                        for part in range(2):
                            for c in range(KC):
                                last = nc.tensor.transpose(turn_ps[:, part, c, :],
                                                           norm.hl[0][:, part * D + c * P:part * D + (c + 1) * P],
                                                           ident16[:])
                        last.then_inc(z_turned, 1)

                    def step(s, gated, units):
                        q = edges.first_chunk(pe, s.b)
                        if not s.first:
                            pe.wait_ge(conv_done, s.b)
                        nc.tensor.matmul(acc[:], zeros16[:, 0:P], zeros16[:], start=True, stop=False,
                                         skip_group_check=True)

                        def sum_chunk(q):
                            for k in range(PARTS):
                                edges.sum_part(pe, q, k, acc)

                        sum_chunk(q)
                        edges.further_chunks(pe, s.b, sum_chunk)
                        nc.tensor.matmul(acc[:, 0:1], zeros16[:, 0:P], zeros16[:, 0:1], start=False, stop=True,
                                         skip_group_check=True).then_inc(acc_ready, 1)
                        for u in units[0] + units[1]:
                            unit(gated, *u)
                        turn_z(s)
                        for u in units[2]:
                            unit(gated, *u)

                    def tail(s, gated, units, final):
                        for u in units:
                            unit(gated, *u)
                        for u in final.units:
                            unit(final, *u)

                    program(pe, step, tail)

                class Whole:

                    def __init__(self, b):
                        self.k, self.i, self.rows = b, 0, P

                @block.scalar
                def _(act):
                    def gate(t, kind, n):
                        if kind == "up":
                            act.wait_ge(up_ready, t.g * FT + (n + 1))
                            if not t.first or n >= 2:
                                act.wait_ge(h_lo_done, t.g * FT + (waits_unit(t, n) + 1))
                            nc.scalar.activation(silu[n % 2][:, 0:t.width], gate_ps[n % 2][:, 0:t.width], ACT.Silu,
                                                 scale=1.0 / WS).then_inc(silu_done, 1)

                    def split(t, kind, n):
                        if kind == "up":
                            act.wait_ge(prod_done, t.g * FT + (n + 1))
                            nc.scalar.activation(h_t[:, n, 0, 0:t.width], silu[n % 2][:, 0:t.width], ACT.Copy)\
                              .then_inc(h_hi_done, 1)
                        else:
                            act.wait_ge(out_done, t.g * R + (n + 1))
                            rows = LAST if t.last else P
                            act.dma_start(out[ds(t.g * W + n * P, rows), :], x3[t.p][n][0:rows, :])\
                               .then_inc(out_stored[t.p][n], 16)

                    def unit(t, between, kind, n):
                        gate(t, kind, n)
                        between()
                        split(t, kind, n)

                    for k in range(PARTS):
                        edges.scale_hi(act, 0, k)

                    def copy_z(s):
                        act.wait_ge(z_turned, s.b + 1)
                        nc.scalar.activation(z_t[s.p][:, :, :, s.r * P:(s.r + 1) * P], turn_ps[:], ACT.Copy)\
                          .then_inc(z_t_done, 1)

                    def step(s, gated, units):
                        if not s.first:
                            act.wait_ge(x3_done, s.b)
                        act.dma_start(x2_in[0:s.rows, :], x2_d[ds(s.b * P, s.rows), :]).then_inc(x2_loaded, 16)
                        def further(q):
                            for k in range(PARTS):
                                edges.scale_hi(act, q, k)

                        edges.further_chunks(act, s.b, further)
                        if not s.last:
                            q = edges.first_chunk(act, s.b + 1)

                        def scale_next(k):
                            if not s.last:
                                edges.scale_hi(act, q, k)

                        early = 0 if gated else 2
                        for k in range(early):
                            scale_next(k)
                        act.wait_ge(acc_ready, s.b + 1)
                        nc.scalar.activation(conv[:], acc[:], ACT.Relu).then_inc(conv_done, 1)
                        def units_with(some, work):
                            for n, u in enumerate(some):
                                unit(gated, work if n == 0 else lambda: None, *u)
                            if not some:
                                work()

                        if not early:
                            scale_next(0)
                        m = Whole(s.b)
                        norm.std(act, m)
                        norm.hi(act, m)
                        units_with(units[0], lambda: early or scale_next(1))
                        units_with(units[1], lambda: scale_next(2))
                        copy_z(s)
                        units_with(units[2][0:1], lambda: scale_next(3))
                        scale_next(4)
                        units_with(units[2][1:], lambda: scale_next(5))

                    def tail(s, gated, units, final):
                        for u in units:
                            unit(gated, lambda: None, *u)
                        for u in final.units:
                            unit(final, lambda: None, *u)
                        for p in range(2):
                            for r in range(R):
                                stores = NGR // 2 + (p == 0 and r == 0)
                                act.wait_ge(out_stored[p][r], 16 * stores)

                    program(act, step, tail)

                @block.vector
                def _(dve):
                    def product(t, kind, n):
                        if kind == "up":
                            dve.wait_ge(silu_done, t.g * FT + (n + 1))
                            nc.vector.scalar_tensor_tensor(silu[n % 2][:, 0:t.width], up_ps[n % 2][:, 0:t.width],
                                                           1.0 / WS, silu[n % 2][:, 0:t.width], ALU.mult, ALU.mult)\
                              .then_inc(prod_done, 1)
                        else:
                            dve.wait_ge(down_ready, t.g * R + (n + 1))
                            nc.vector.scalar_tensor_tensor(x3[t.p][n][:], down_ps[n % 2][:], 1.0 / WS, x3[t.p][n][:],
                                                           ALU.mult, ALU.add).then_inc(out_done, 1)

                    def split(t, kind, n):
                        if kind == "up":
                            dve.wait_ge(h_hi_done, t.g * FT + (n + 1))
                            nc.vector.tensor_tensor(h_t[:, n, 1, 0:t.width], silu[n % 2][:, 0:t.width],
                                                    h_t[:, n, 0, 0:t.width], ALU.subtract).then_inc(h_lo_done, 1)

                    def unit(t, between, kind, n):
                        product(t, kind, n)
                        between()
                        split(t, kind, n)

                    nc.vector.memset(edges.first_node[:], 0.0)
                    dve.drain()
                    for k in range(PARTS):
                        edges.prepare(dve, 0, k)

                    def step(s, gated, units):

                        def further(q):
                            for k in range(PARTS):
                                edges.prepare(dve, q, k)

                        edges.further_chunks(dve, s.b, further)
                        edges.next_block(dve)
                        if not s.last:
                            q = edges.first_chunk(dve, s.b + 1)

                        def prepare_next(k):
                            if not s.last:
                                edges.prepare(dve, q, k)

                        def units_with(some, work):
                            for n, u in enumerate(some):
                                unit(gated, work if n == 0 else lambda: None, *u)
                            if not some:
                                work()

                        early = 0 if gated else 2
                        for k in range(early):
                            prepare_next(k)
                        dve.wait_ge(conv_done, s.b + 1)
                        dve.wait_ge(x2_loaded, s.b * 16 + 16)
                        if not isinstance(s.g, int) or s.g >= 2:
                            dve.wait_ge(out_stored[s.p][s.r], (s.g - s.p) * 8)
                        norm.x[0] = x3[s.p][s.r]
                        nc.vector.tensor_tensor(x3[s.p][s.r][:], conv[:], x2_in[:], ALU.add).then_inc(x3_done, 1)
                        dve.drain()
                        m = Whole(s.b)
                        norm.var(dve, m)
                        if not early:
                            prepare_next(0)
                        norm.scale(dve, m)
                        norm.lo(dve, m)
                        units_with(units[0], lambda: early or prepare_next(1))
                        units_with(units[1], lambda: prepare_next(2))
                        units_with(units[2][0:1], lambda: prepare_next(3))
                        prepare_next(4)
                        units_with(units[2][1:], lambda: prepare_next(5))

                    def tail(s, gated, units, final):
                        for u in units:
                            unit(gated, lambda: None, *u)
                        for u in final.units:
                            unit(final, lambda: None, *u)

                    program(dve, step, tail)

        layer0()
        late()


_INS = ['x', 'src', 'dst', 'edge_weight', 'L0_gnn_W_l', 'L0_gnn_b_l', 'L0_gnn_W_r', 'L0_gnn_gamma', 'L0_gnn_beta',
        'L0_ffn_router_w', 'L0_ffn_router_b', 'L0_ffn_w1', 'L0_ffn_b1', 'L0_ffn_w2', 'L0_ffn_b2',
        'L1_gnn_weight', 'L1_ffn_w_gate', 'L1_ffn_w_up', 'L1_ffn_w_down']


def kernel(**inputs):
    import numpy as _np
    import concourse.bacc as _bacc
    from concourse import mybir as _mybir
    from concourse.bass_utils import run_bass_kernel_spmd as _run

    nc = _bacc.Bacc("TRN2", target_bir_lowering=False, num_devices=1)
    arrays, args = {}, []
    for name in _INS:
        a = _np.ascontiguousarray(inputs[name])
        arrays[f"in_{name}"] = a
        args.append(nc.dram_tensor(f"in_{name}", a.shape, _mybir.dt.from_np(a.dtype), kind="ExternalInput").ap())
    shape = inputs['x'].shape
    args.append(nc.dram_tensor("out_0", shape, _mybir.dt.float32, kind="ExternalOutput").ap())
    gnn_kernel(nc, *args)
    r = _run(nc, [arrays], core_ids=[0])
    return r.results[0]["out_0"]
```
